# Optimizing a Trainium2 kernel written in Bass

```python
import numpy as np
import jax
import jax.numpy as jnp

def _softmax(x, axis=-1):
    return jax.nn.softmax(x, axis=axis)

def _gelu(x):
    return jax.nn.gelu(x, approximate=True)

def _silu(x):
    return jax.nn.silu(x)

def _sigmoid(x):
    return jax.nn.sigmoid(x)

def _layernorm(x, axis=-1, eps=1e-05):
    m = jnp.mean(x, axis=axis, keepdims=True)
    v = jnp.var(x, axis=axis, keepdims=True)
    return (x - m) / jnp.sqrt(v + eps)

def _scatter_add(tgt, idx, src, axis=0):
    return tgt.at[idx].add(src)

def _segment_sum(src, seg, n):
    return jax.ops.segment_sum(src, seg, n)
kernel_name = 'mk_flamingo_gated_d2_seqx_r4_70efb1'

def setup_inputs(seed: int=0):
    np.random.seed(seed)
    _w = jnp.asarray

    def _rec_inputs():
        import jax
        import jax.numpy as jnp
        _rk = jax.random.key(seed)
        x = 7.22e-05 + 1 * jax.random.normal(jax.random.fold_in(_rk, 1), (16, 256, 512), jnp.float32)
        _lenS = 256 - jax.random.randint(jax.random.fold_in(_rk, 7), (16,), 0, max(1, 256 // 4) + 1, jnp.int32)
        _lenS2 = 256 - jax.random.randint(jax.random.fold_in(_rk, 8), (16,), 0, max(1, 256 // 4) + 1, jnp.int32)
        _ctx_2048P = jax.random.normal(jax.random.fold_in(_rk, 11), (16, 16, 512), jnp.float32)
        _ctx_2048c = jax.random.dirichlet(jax.random.fold_in(_rk, 511), 0.3 * jnp.ones((16,), jnp.float32), (16, 256))
        _ctx_2048t = jnp.einsum('bsk,bkd->bsd', _ctx_2048c, _ctx_2048P)
        _ctx_2048t = _ctx_2048t * jax.lax.rsqrt(jnp.mean(jnp.square(_ctx_2048t)) + 1e-12) * 0.953939
        ctx_2048 = 4.13588e-05 + 0.999923 * (_ctx_2048t + 0.3 * jax.random.normal(jax.random.fold_in(_rk, 611), (16, 256, 512), jnp.float32))
        _g = jax.random.normal(jax.random.fold_in(_rk, 9001), (2, 2), jnp.float32)
        _g = jnp.sign(_g) * jnp.maximum(jnp.abs(_g), 1.0) + (_g == 0) * 1.0
        g_xattn = _g[0]
        g_ffn = _g[1]
        return (x, ctx_2048, g_xattn, g_ffn)
    x, ctx_2048, g_xattn, g_ffn = _rec_inputs()

    def _L0_xattn_setup():
        import jax, jax.numpy as jnp
        import numpy as np
        BS, S, DK = (8, 128, 512)
        key = jax.random.key(seed)
        kq, kk, kv = jax.random.split(key, 3)
        q = jax.random.normal(kq, (BS, S, DK), dtype=jnp.float32)
        k = jax.random.normal(kk, (BS, S, DK), dtype=jnp.float32)
        v = jax.random.normal(kv, (BS, S, DK), dtype=jnp.float32)
        return {'q': q, 'k': k, 'v': v}
    _L0_xattn_all = _L0_xattn_setup()
    _L0_xattn_in = {k: v for k, v in _L0_xattn_all.items() if k in ()}
    del _L0_xattn_all

    def _L0_ffn_setup():
        import jax, jax.numpy as jnp
        import numpy as np
        _FP8_MAX = 448.0
        _BLOCK = 32
        _EPS = 1e-30

        def _mx_dequant(t):
            rows, feat = t.shape
            blocks = t.reshape(rows, feat // _BLOCK, _BLOCK)
            max_abs = jnp.max(jnp.abs(blocks), axis=-1)
            scales = jnp.maximum(max_abs / _FP8_MAX, _EPS)
            q = (blocks / scales[..., None]).astype(jnp.float8_e4m3fn).astype(jnp.float32)
            return (q * scales[..., None]).reshape(rows, feat)

        def _mx_linear(x2d, w):
            return _mx_dequant(x2d) @ _mx_dequant(w).T
        key = jax.random.key(seed)
        k1, k2, k3, k4 = jax.random.split(key, 4)
        B, S, H, I = (2, 256, 512, 2048)
        return {'x': jax.random.normal(k1, (B, S, H), dtype=jnp.float32), 'gate_w': jax.random.normal(k2, (I, H), dtype=jnp.float32) * 0.02, 'up_w': jax.random.normal(k3, (I, H), dtype=jnp.float32) * 0.02, 'down_w': jax.random.normal(k4, (H, I), dtype=jnp.float32) * 0.02}
    _L0_ffn_all = _L0_ffn_setup()
    _L0_ffn_in = {k: v for k, v in _L0_ffn_all.items() if k in ('gate_w', 'up_w', 'down_w')}
    del _L0_ffn_all

    def _L1_xattn_setup():
        import jax, jax.numpy as jnp
        import numpy as np
        from jax import lax
        LN_EPS = 1e-05
        key = jax.random.key(seed)
        ks = jax.random.split(key, 8)
        B, S, T, D = (4, 128, 512, 512)
        scale = 0.02
        return {'Z': jax.random.normal(ks[0], (B, S, D), dtype=jnp.float32), 'kv': jax.random.normal(ks[1], (B, T, D), dtype=jnp.float32), 'decay': jnp.float32(0.9), 'W_in': jax.random.normal(ks[2], (D, D), dtype=jnp.float32) * scale, 'b_in': jnp.zeros((D,), dtype=jnp.float32), 'W_out': jax.random.normal(ks[3], (D, D), dtype=jnp.float32) * scale, 'b_out': jnp.zeros((D,), dtype=jnp.float32), 'gamma': jnp.ones((D,), dtype=jnp.float32), 'beta': jnp.zeros((D,), dtype=jnp.float32)}
    _L1_xattn_all = _L1_xattn_setup()
    _L1_xattn_in = {k: v for k, v in _L1_xattn_all.items() if k in ('decay', 'W_in', 'b_in', 'W_out', 'b_out', 'gamma', 'beta')}
    del _L1_xattn_all

    def _L1_ffn_setup():
        import jax, jax.numpy as jnp
        import numpy as np
        _FP4_LUT = jnp.array([0.0, 0.5, 1.0, 1.5, 2.0, 3.0, 4.0, 6.0, -0.0, -0.5, -1.0, -1.5, -2.0, -3.0, -4.0, -6.0], dtype=jnp.float32)
        GROUP_SIZE = 128
        EPS = 1e-06

        def _dequant_fp4(packed_i32, scales_f16, group_size):
            out_f, in_p = packed_i32.shape
            w = packed_i32.astype(jnp.uint32)
            shifts = jnp.arange(8, dtype=jnp.uint32) * 4
            nib = w[:, :, None] >> shifts & jnp.uint32(15)
            vals = _FP4_LUT[nib.astype(jnp.int32)].reshape(out_f, in_p * 8)
            s = scales_f16.astype(jnp.float32).T
            s_full = jnp.repeat(s, group_size, axis=1)
            return vals * s_full
        key = jax.random.key(seed)
        k1, k2, k3, k4, k5 = jax.random.split(key, 5)
        B, S, H, I = (4, 512, 512, 1408)
        x = jax.random.normal(k1, (B, S, H), dtype=jnp.float32)
        gate_up_packed = jax.random.randint(k2, (2 * I, H // 8), 0, 2147483647, dtype=jnp.int32)
        gate_up_scales = jax.random.uniform(k3, (H // GROUP_SIZE, 2 * I), dtype=jnp.float32).astype(jnp.float16)
        down_packed = jax.random.randint(k4, (H, I // 8), 0, 2147483647, dtype=jnp.int32)
        down_scales = jax.random.uniform(k5, (I // GROUP_SIZE, H), dtype=jnp.float32).astype(jnp.float16)
        return {'x': x, 'gate_up_packed': gate_up_packed, 'gate_up_scales': gate_up_scales, 'down_packed': down_packed, 'down_scales': down_scales}
    _L1_ffn_all = _L1_ffn_setup()
    _L1_ffn_in = {k: v for k, v in _L1_ffn_all.items() if k in ('gate_up_packed', 'gate_up_scales', 'down_packed', 'down_scales')}
    del _L1_ffn_all
    return {'x': x, 'ctx_2048': ctx_2048, 'g_xattn': g_xattn, 'g_ffn': g_ffn, 'L0_ffn_gate_w': _L0_ffn_in['gate_w'], 'L0_ffn_up_w': _L0_ffn_in['up_w'], 'L0_ffn_down_w': _L0_ffn_in['down_w'], 'L1_xattn_decay': _L1_xattn_in['decay'], 'L1_xattn_W_in': _L1_xattn_in['W_in'], 'L1_xattn_b_in': _L1_xattn_in['b_in'], 'L1_xattn_W_out': _L1_xattn_in['W_out'], 'L1_xattn_b_out': _L1_xattn_in['b_out'], 'L1_xattn_gamma': _L1_xattn_in['gamma'], 'L1_xattn_beta': _L1_xattn_in['beta'], 'L1_ffn_gate_up_packed': _L1_ffn_in['gate_up_packed'], 'L1_ffn_gate_up_scales': _L1_ffn_in['gate_up_scales'], 'L1_ffn_down_packed': _L1_ffn_in['down_packed'], 'L1_ffn_down_scales': _L1_ffn_in['down_scales']}

def reference(x, ctx_2048, g_xattn, g_ffn, L0_ffn_gate_w, L0_ffn_up_w, L0_ffn_down_w, L1_xattn_decay, L1_xattn_W_in, L1_xattn_b_in, L1_xattn_W_out, L1_xattn_b_out, L1_xattn_gamma, L1_xattn_beta, L1_ffn_gate_up_packed, L1_ffn_gate_up_scales, L1_ffn_down_packed, L1_ffn_down_scales):
    import jax
    import jax.numpy as jnp

    def _L0_xattn_ref(q, k, v):
        import jax, jax.numpy as jnp
        import numpy as np
        BS, S, DK = (8, 128, 512)
        dk = q.shape[-1]
        scale = 1.0 / jnp.sqrt(jnp.asarray(dk, dtype=q.dtype))
        scaled = jnp.einsum('bsd,bse->bde', q, k) * scale
        attn = jax.nn.softmax(scaled, axis=1)
        out = jnp.einsum('bde,bse->bsd', attn, v)
        return out

    def _L0_ffn_ref(x, gate_w, up_w, down_w):
        import jax, jax.numpy as jnp
        import numpy as np
        _FP8_MAX = 448.0
        _BLOCK = 32
        _EPS = 1e-30

        def _mx_dequant(t):
            rows, feat = t.shape
            blocks = t.reshape(rows, feat // _BLOCK, _BLOCK)
            max_abs = jnp.max(jnp.abs(blocks), axis=-1)
            scales = jnp.maximum(max_abs / _FP8_MAX, _EPS)
            q = (blocks / scales[..., None]).astype(jnp.float8_e4m3fn).astype(jnp.float32)
            return (q * scales[..., None]).reshape(rows, feat)

        def _mx_linear(x2d, w):
            return _mx_dequant(x2d) @ _mx_dequant(w).T
        B, S, H = x.shape
        x2d = x.reshape(B * S, H)
        gate = _mx_linear(x2d, gate_w)
        up = _mx_linear(x2d, up_w)
        h = jax.nn.silu(gate) * up
        out = _mx_linear(h, down_w)
        return out.reshape(B, S, H)

    def _L1_xattn_ref(Z, kv, decay, W_in, b_in, W_out, b_out, gamma, beta):
        import jax, jax.numpy as jnp
        import numpy as np
        from jax import lax
        LN_EPS = 1e-05
        B, T, D = kv.shape
        K = jax.nn.sigmoid(decay)
        x = jnp.einsum('btd,ed->bte', kv, W_in) + b_in

        def scan_fn(s, xt):
            s = K * s + xt
            return (s, s)
        s0 = jnp.zeros((B, D), dtype=kv.dtype)
        _, states = lax.scan(scan_fn, s0, jnp.swapaxes(x, 0, 1))
        states = jnp.swapaxes(states, 0, 1)
        proj = jnp.einsum('btd,ed->bte', states, W_out) + b_out
        summary = jnp.mean(proj, axis=1, keepdims=True)
        y = Z + summary
        mu = jnp.mean(y, axis=-1, keepdims=True)
        var = jnp.mean((y - mu) ** 2, axis=-1, keepdims=True)
        return (y - mu) / jnp.sqrt(var + LN_EPS) * gamma + beta

    def _L1_ffn_ref(x, gate_up_packed, gate_up_scales, down_packed, down_scales):
        import jax, jax.numpy as jnp
        import numpy as np
        _FP4_LUT = jnp.array([0.0, 0.5, 1.0, 1.5, 2.0, 3.0, 4.0, 6.0, -0.0, -0.5, -1.0, -1.5, -2.0, -3.0, -4.0, -6.0], dtype=jnp.float32)
        GROUP_SIZE = 128
        EPS = 1e-06

        def _dequant_fp4(packed_i32, scales_f16, group_size):
            out_f, in_p = packed_i32.shape
            w = packed_i32.astype(jnp.uint32)
            shifts = jnp.arange(8, dtype=jnp.uint32) * 4
            nib = w[:, :, None] >> shifts & jnp.uint32(15)
            vals = _FP4_LUT[nib.astype(jnp.int32)].reshape(out_f, in_p * 8)
            s = scales_f16.astype(jnp.float32).T
            s_full = jnp.repeat(s, group_size, axis=1)
            return vals * s_full
        I = gate_up_packed.shape[0] // 2
        w_gu = _dequant_fp4(gate_up_packed, gate_up_scales, GROUP_SIZE)
        w_down = _dequant_fp4(down_packed, down_scales, GROUP_SIZE)
        gate_up = jnp.einsum('bsh,oh->bso', x, w_gu)
        gate, up = (gate_up[..., :I], gate_up[..., I:])
        h = jax.nn.silu(gate) * up
        y = jnp.einsum('bsi,hi->bsh', h, w_down)
        rms = jnp.sqrt(jnp.mean(y * y, axis=-1, keepdims=True) + EPS)
        return y / rms
    x = x + jnp.tanh(g_xattn[0]) * _L0_xattn_ref(_layernorm(x, axis=-1), ctx_2048, ctx_2048)
    x = x + jnp.tanh(g_ffn[0]) * _L0_ffn_ref(_layernorm(x, axis=-1), L0_ffn_gate_w, L0_ffn_up_w, L0_ffn_down_w)
    x = x + jnp.tanh(g_xattn[1]) * _L1_xattn_ref(_layernorm(x, axis=-1), ctx_2048, L1_xattn_decay, L1_xattn_W_in, L1_xattn_b_in, L1_xattn_W_out, L1_xattn_b_out, L1_xattn_gamma, L1_xattn_beta)
    x = x + jnp.tanh(g_ffn[1]) * _L1_ffn_ref(_layernorm(x, axis=-1), L1_ffn_gate_up_packed, L1_ffn_gate_up_scales, L1_ffn_down_packed, L1_ffn_down_scales)
    return x

_drawn_inputs = setup_inputs


def setup_inputs(seed=0):
    import zlib

    import numpy as np

    out = dict(_drawn_inputs(seed))
    spreads = {'g_ffn': (-1.0, 0.2),
     'L1_xattn_b_in': (0.0, 0.1),
     'L1_xattn_b_out': (0.0, 0.1),
     'L1_xattn_gamma': (1.0, 0.2),
     'L1_xattn_beta': (0.0, 0.1)}
    factors = {}
    for name, (base, spread) in spreads.items():
        noise = np.random.default_rng([zlib.crc32(name.encode()), seed]).standard_normal(out[name].shape)
        drawn = base * np.exp(spread * noise) if base else spread * noise
        out[name] = jnp.asarray(drawn.astype(out[name].dtype))
    for name, factor in factors.items():
        out[name] = (out[name] * factor).astype(out[name].dtype)
    return out
```

```python
from contextlib import ExitStack

import concourse.bass as bass
from concourse import mybir
from concourse.alu_op_type import AluOpType as ALU

F32 = mybir.dt.float32
F32R = mybir.dt.float32r
F16 = mybir.dt.float16
I32 = mybir.dt.int32
ACT = mybir.ActivationFunctionType
AX = mybir.AxisListType

P = 128
LN_EPS = 1e-5
RMS_EPS = 1e-6
BLOCK = 32
FP8_MAX = 448.0
SCALE_MIN = 1e-30
EXPONENT = 0x7F800000
HALF_BIT = 0x00400000
HIHI_HILO_LOHI = ((0, 0), (0, 1), (1, 0))


def run_pipeline(loop, n_items, unroll, peel, stages):
    most = max(lag for lag, _ in stages)
    start = most + peel
    rounds = max(0, n_items - start) // unroll

    def tick(t, base):
        for lag, body in stages:
            if base is not None:
                body(base + (t - lag), (t - lag) % unroll)
            elif 0 <= t - lag < n_items:
                body(t - lag, (t - lag) % unroll)

    for t in range(start):
        tick(t, None)
    if rounds:
        with loop(0, (rounds - 1) * unroll + 1, unroll) as base:
            for t in range(start, start + unroll):
                tick(t, base)
    for t in range(start + rounds * unroll, n_items + most):
        tick(t, None)


def wait_item(eng, sem, n, back=0, per=1, of=None):
    if isinstance(n, int) and n < back:
        return
    eng.wait_ge(sem, (n - back) * per + (per if of is None else of + 1))


def wait_slot(eng, sem, n, slot, slots, dmas=1):
    eng.wait_ge(sem, (n - slot % slots) * (16 * dmas // slots) + 16 * dmas)


def own_wait(eng, passed):
    eng.sem_inc(passed, 1)


class Memory:

    def __init__(self, nc, ctx):
        self.nc, self.ctx = nc, ctx

    def sbuf(self, name, shape, dtype=F32):
        return self.ctx.enter_context(self.nc.sbuf_tensor(name, shape, dtype))

    def psum(self, name, shape=(P, 512)):
        return self.ctx.enter_context(self.nc.psum_tensor(name, list(shape), F32))

    def sem(self, name):
        return self.ctx.enter_context(self.nc.semaphore(name))

    def sems(self, name, n):
        return [self.sem(f"{name}{i}") for i in range(n)]


def split_matmul(pe, out, stationary, moving, first, last):
    for n, (a, b) in enumerate(HIHI_HILO_LOHI):
        mm = pe.matmul(out, stationary[a], moving[b], start=first and n == 0, stop=last and n == 2)
    return mm


def attend(nc, io, shared):
    B, S, D = io["x"].shape
    ST, DB = S // P, D // P
    U = 4
    SCALE = float(D) ** -0.5
    with ExitStack() as ctx:
        m = Memory(nc, ctx)
        X = m.sbuf("x_tiles", [P, U, ST, D])
        C = m.sbuf("ctx_tiles", [P, 2, ST, D])
        CT = m.sbuf("ctx_transposed", [P, 2, DB, S])
        Q = m.sbuf("q", [P, 2, ST, D])
        Qp = [m.sbuf(f"q_{s}", [P, 2, ST, D], F32R) for s in ("hi", "lo")]
        Kp = [m.sbuf(f"k_{s}", [P, 2, ST, D], F32R) for s in ("hi", "lo")]
        Vp = [m.sbuf(f"vT_{s}", [P, 2, DB, S], F32R) for s in ("hi", "lo")]
        E = m.sbuf("exps", [P, 2, D])
        Ep = [m.sbuf(f"exp_{s}", [P, 2, DB, D], F32R) for s in ("hi", "lo")]
        stats = m.sbuf("ln_stats", [P, 2, ST, 6])
        mv = m.sbuf("mean_var", [P, 2, ST, 2])
        veps = m.sbuf("var_eps", [P, 2, ST])
        rstd = m.sbuf("rstd", [P, 2, ST])
        nmax = m.sbuf("neg_max", [P, 2, DB])
        bias = m.sbuf("exp_bias", [P, 2, DB])
        zsum = m.sbuf("exp_sum", [P, 2, DB])
        rz = m.sbuf("exp_sum_inverse", [P, 2, DB])
        ones = m.sbuf("ones", [P, P])
        keep = m.sbuf("keep", [1, 2])
        row = m.sbuf("decay_row", [1, S])
        wcol = m.sbuf("state_weights", [P, ST])
        WinT = m.sbuf("W_inT_sb", [P, DB, D])
        WoutT = m.sbuf("W_outT_sb", [P, DB, D])
        bin_ = m.sbuf("b_in_columns", [P, DB])
        bout = m.sbuf("b_out_row", [1, D])
        bw = m.sbuf("b_in_weighted", [P, DB])
        sumw = m.sbuf("state_weight_sum", [P, 1])
        cw = m.sbuf("ctx_weighted", [P, DB, B])
        states = m.sbuf("mean_states", [P, DB, B])
        summ = m.sbuf("summary_rows", [B, D])
        pS = [m.psum(f"pScores{i}") for i in range(DB)]
        pO = [m.psum(f"pOut{i}") for i in range(ST)]
        pC = m.psum("pCtxWeighted")
        pW = m.psum("pSmall")

        consts_loaded = m.sem("consts_loaded")
        x_loaded, x_stored = m.sems("x_loaded", U), m.sems("x_stored", U)
        c_loaded = m.sems("c_loaded", 2)
        summary_stored = m.sem("summary_stored")
        gates_ready, keep_ready, row_ready = m.sem("gates_ready"), m.sem("keep_ready"), m.sem("row_ready")
        weights_psum, weights_ready = m.sem("weights_psum"), m.sem("weights_ready")
        stats_ready, mv_ready, veps_ready = m.sem("stats_ready"), m.sem("mv_ready"), m.sem("veps_ready")
        rstd_ready, q_ready = m.sem("rstd_ready"), m.sem("q_ready")
        qhi_ready, qlo_ready = m.sem("qhi_ready"), m.sem("qlo_ready")
        khi_ready, klo_ready = m.sem("khi_ready"), m.sem("klo_ready")
        scores_ready, nmax_ready, bias_ready = m.sem("scores_ready"), m.sem("nmax_ready"), m.sem("bias_ready")
        exps_ready, ehi_ready, elo_ready = m.sem("exps_ready"), m.sem("ehi_ready"), m.sem("elo_ready")
        rz_ready, vhi_ready, v_ready = m.sem("rz_ready"), m.sem("vhi_ready"), m.sem("v_ready")
        out_ready, out_added = m.sem("out_ready"), m.sem("out_added")
        const_order = m.sem("const_order")
        cw_ready, states_psum, states_ready = m.sem("cw_ready"), m.sem("states_psum"), m.sem("states_ready")
        summary_psum, summary_ready = m.sem("summary_psum"), m.sem("summary_ready")
        block = ctx.enter_context(nc.Block())

        x_in = io["x"].rearrange("b (t p) d -> b p t d", p=P)
        c_in = io["ctx"].rearrange("b (t p) d -> b p t d", p=P)
        ct_in = io["ctxT"].rearrange("b (e p) s -> b p e s", p=P)
        x_out = shared["x1"].rearrange("(b t p) d -> b p t d", p=P, t=ST)
        gates, ident = shared["gates"], shared["ident"]
        CONSTS = 7

        @block.sync
        def _(sp):
            def load_x(n, slot):
                sp.dma_start(X[:, slot], x_in[n]).then_inc(x_loaded[slot], 16)

            def load_ctx(n, slot):
                sp.dma_start(C[:, slot % 2], c_in[n]).then_inc(c_loaded[slot % 2], 16)
                sp.dma_start(CT[:, slot % 2], ct_in[n]).then_inc(c_loaded[slot % 2], 16)

            def const(dst, src):
                sp.dma_start(dst, src).then_inc(consts_loaded, 16)

            def next_ctx(n, slot):
                wait_item(sp, scores_ready, n, per=DB)
                own_wait(sp, shared["passed_sp"])
                wait_item(sp, v_ready, n)
                own_wait(sp, shared["passed_sp"])
                load_ctx(n + 2, slot)

            def store_x(n, slot):
                wait_item(sp, out_added, n, per=ST)
                sp.dma_start(x_out[n], X[:, slot]).then_inc(x_stored[slot], 16)

            def next_x(n, slot):
                wait_slot(sp, x_stored[slot], n, slot, U)
                load_x(n + U, slot)

            load_x(0, 0)
            load_ctx(0, 0)
            const(gates[:, 0:2], io["g_xattn"].rearrange("(a n) -> a n", a=1).to_broadcast([P, 2]))
            const(gates[:, 2:4], io["g_ffn"].rearrange("(a n) -> a n", a=1).to_broadcast([P, 2]))
            const(keep[0:1, 0:1], io["decay"])
            const(bin_[:], io["b_in"])
            const(bout[:], io["b_out"].rearrange("(a n) -> a n", a=1))
            load_x(1, 1)
            load_ctx(1, 1)
            load_x(2, 2)
            load_x(3, 3)
            const(WinT[:], io["W_inT"].rearrange("(e p) n -> p e n", p=P))
            const(WoutT[:], io["W_outT"].rearrange("(e p) n -> p e n", p=P))
            next_ctx(0, 0)
            with sp.Fori(0, B - 2 * U + 1, U) as base:
                for j in range(U):
                    next_ctx(base + (j + 1), (j + 1) % U)
                    store_x(base + j, j)
                    next_x(base + j, j)
            for n in range(B - U, B):
                if n + 3 < B:
                    next_ctx(n + 1, (n + 1) % U)
                store_x(n, n % U)
            for j in range(U):
                wait_slot(sp, x_stored[j], B - U + j, j, U)
            sp.wait_ge(summary_ready, 1)
            sp.dma_start(shared["summary"], summ[:]).then_inc(summary_stored, 16)
            sp.wait_ge(summary_stored, 16)

        @block.gpsimd
        def _(pool):
            pool.memset(ident[:], 0.0).then_inc(const_order, 1)
            pool.memset(shared["minus_half"][:], -0.5).then_inc(const_order, 1)
            pool.memset(ones[:], 1.0).then_inc(const_order, 1)
            pool.wait_ge(const_order, 3)
            pool.affine_select(out=ident[:], in_=ident[:], compare_op=ALU.not_equal, fill=1.0,
                               base=0, pattern=[[-1, P]], channel_multiplier=1).then_inc(const_order, 1)

            def rstd_of(n, slot):
                h = slot % 2
                wait_item(pool, mv_ready, n, per=ST)
                wait_item(pool, q_ready, n, back=2, per=ST)
                own_wait(pool, shared["passed_pool"])
                pool.tensor_scalar(veps[:, h], mv[:, h, :, 1], LN_EPS, None, ALU.add).then_inc(veps_ready, 1)
                wait_item(pool, veps_ready, n)
                pool.tensor_tensor(rstd[:, h], veps[:, h], shared["minus_half"][:, 0:ST],
                                   ALU.pow).then_inc(rstd_ready, 1)

            def k_lo(n, slot):
                h = slot % 2
                wait_item(pool, khi_ready, n)
                pool.tensor_tensor(Kp[1][:, h], C[:, h], Kp[0][:, h].bitcast(F32), ALU.subtract)\
                    .then_inc(klo_ready, 1)

            def e_lo(n, slot):
                h = slot % 2
                for e in range(DB):
                    wait_item(pool, ehi_ready, n, per=DB, of=e)
                    pool.tensor_tensor(Ep[1][:, h, e], E[:, e % 2], Ep[0][:, h, e].bitcast(F32),
                                       ALU.subtract).then_inc(elo_ready, 1)

            run_pipeline(pool.Fori, B, U, 2, [(0, rstd_of), (0, k_lo), (1, e_lo)])

        @block.scalar
        def _(act):
            act.wait_ge(consts_loaded, 16 * CONSTS)
            act.activation(gates[:], gates[:], ACT.Tanh).then_inc(gates_ready, 1)
            act.activation(keep[0:1, 1:2], keep[0:1, 0:1], ACT.Sigmoid).then_inc(keep_ready, 1)

            def k_hi(n, slot):
                h = slot % 2
                wait_slot(act, c_loaded[h], n, slot, 2, dmas=2)
                wait_item(act, scores_ready, n, back=2, per=DB)
                act.activation(Kp[0][:, h], C[:, h], ACT.Copy).then_inc(khi_ready, 1)

            def q_hi(n, slot):
                h = slot % 2
                wait_item(act, q_ready, n, per=ST)
                wait_item(act, scores_ready, n, back=2, per=DB)
                act.activation(Qp[0][:, h], Q[:, h], ACT.Copy).then_inc(qhi_ready, 1)

            def exps(n, slot):
                h = slot % 2
                wait_item(act, out_ready, n, back=2, per=ST)
                for e in range(DB):
                    wait_item(act, bias_ready, n, per=DB, of=e)
                    if e >= 2:
                        wait_item(act, elo_ready, n, per=DB, of=e - 2)
                    else:
                        wait_item(act, elo_ready, n, back=1, per=DB, of=e + DB - 2)
                    act.activation(E[:, e % 2], pS[e][:], ACT.Exp, bias=bias[:, h, e:e + 1], scale=SCALE,
                                   accum_out=zsum[:, h, e:e + 1]).then_inc(exps_ready, 1)
                    wait_item(act, exps_ready, n, per=DB, of=e)
                    act.activation(Ep[0][:, h, e], E[:, e % 2], ACT.Copy).then_inc(ehi_ready, 1)

            run_pipeline(act.Fori, B, U, 2, [(0, k_hi), (1, exps), (0, q_hi)])

        @block.vector
        def _(dve):
            dve.wait_ge(keep_ready, 1)
            dve.wait_ge(const_order, 4)
            dve.tensor_tensor_scan(row[:, ::-1], keep[0:1, 1:2].to_broadcast([1, S]), ones[0:1, 0:1].to_broadcast([1, S]),
                                   0.0, ALU.mult, ALU.add).then_inc(row_ready, 1)
            dve.wait_ge(weights_psum, 1)
            dve.tensor_scalar(wcol[:], pW[:, 0:ST], 1.0 / S, None, ALU.mult).then_inc(weights_ready, 1)
            dve.wait_ge(gates_ready, 1)

            def norm_stats(n, slot):
                h = slot % 2
                wait_slot(dve, x_loaded[slot], n, slot, U)
                for t in range(ST):
                    dve.bn_stats(stats[:, h, t], X[:, slot, t]).then_inc(stats_ready, 1)
                wait_item(dve, rstd_ready, n, back=2)
                wait_item(dve, q_ready, n, back=2, per=ST)
                for t in range(ST):
                    wait_item(dve, stats_ready, n, per=ST, of=t)
                    own_wait(dve, shared["passed_dve"])
                    dve.bn_aggr(mv[:, h, t], stats[:, h, t]).then_inc(mv_ready, 1)

            def norm(n, slot):
                h = slot % 2
                wait_item(dve, rstd_ready, n)
                wait_item(dve, qlo_ready, n, back=2)
                for t in range(ST):
                    dve.tensor_scalar(Q[:, h, t], X[:, slot, t], mv[:, h, t, 0:1], rstd[:, h, t:t + 1],
                                      ALU.subtract, ALU.mult).then_inc(q_ready, 1)

            def q_lo(n, slot):
                h = slot % 2
                wait_item(dve, qhi_ready, n)
                dve.tensor_tensor(Qp[1][:, h], Q[:, h], Qp[0][:, h].bitcast(F32), ALU.subtract)\
                    .then_inc(qlo_ready, 1)

            def maxima(n, slot):
                h = slot % 2
                for e in range(DB):
                    wait_item(dve, scores_ready, n, per=DB, of=e)
                    dve.tensor_reduce(nmax[:, h, e:e + 1], pS[e][:], AX.X, ALU.max, negate=True)\
                        .then_inc(nmax_ready, 1)
                    wait_item(dve, nmax_ready, n, per=DB, of=e)
                    dve.tensor_scalar(bias[:, h, e:e + 1], nmax[:, h, e:e + 1], SCALE, None, ALU.mult)\
                        .then_inc(bias_ready, 1)

            def scale_v(n, slot):
                h = slot % 2
                wait_item(dve, out_ready, n, back=2, per=ST)
                for e in range(DB):
                    wait_item(dve, exps_ready, n, per=DB, of=e)
                    wait_item(dve, ehi_ready, n, per=DB, of=e)
                    dve.reciprocal(rz[:, h, e:e + 1], zsum[:, h, e:e + 1]).then_inc(rz_ready, 1)
                    wait_item(dve, rz_ready, n, per=DB, of=e)
                    dve.tensor_scalar(Vp[0][:, h, e], CT[:, h, e], rz[:, h, e:e + 1], None, ALU.mult)\
                        .then_inc(vhi_ready, 1)
                    wait_item(dve, vhi_ready, n, per=DB, of=e)
                    last = dve.scalar_tensor_tensor(out=Vp[1][:, h, e], in0=CT[:, h, e], scalar=rz[:, h, e:e + 1],
                                                    in1=Vp[0][:, h, e].bitcast(F32), op0=ALU.mult, op1=ALU.subtract)
                last.then_inc(v_ready, 1)

            def add_out(n, slot):
                for t in range(ST):
                    wait_item(dve, out_ready, n, per=ST, of=t)
                    dve.scalar_tensor_tensor(out=X[:, slot, t], in0=pO[t][:], scalar=gates[:, 0:1],
                                             in1=X[:, slot, t], op0=ALU.mult, op1=ALU.add).then_inc(out_added, 1)

            run_pipeline(dve.Fori, B, U, 2, [(0, norm_stats), (1, maxima), (0, norm), (1, scale_v), (0, q_lo),
                                             (2, add_out)])

            dve.wait_ge(cw_ready, 1)
            dve.tensor_copy(cw[:], pC[:, 0:DB * B].rearrange("p (e b) -> p e b", e=DB)).then_inc(states_ready, 1)
            dve.tensor_copy(sumw[:], pW[:, 8:9]).then_inc(states_ready, 1)
            dve.wait_ge(states_ready, 2)
            dve.tensor_scalar(bw[:], bin_[:], sumw[:, 0:1], None, ALU.mult).then_inc(states_ready, 1)
            dve.wait_ge(states_psum, 1)
            dve.wait_ge(states_ready, 3)
            for e in range(DB):
                dve.tensor_scalar(states[:, e], pS[e][:, 0:B], bw[:, e:e + 1], None, ALU.add).then_inc(states_ready, 1)
            dve.wait_ge(summary_psum, 1)
            dve.tensor_copy(summ[:], pO[0][0:B, :]).then_inc(summary_ready, 1)

        @block.tensor
        def _(pe):
            pe.wait_ge(row_ready, 1)
            for t in range(ST):
                mm = pe.matmul(pW[:, t:t + 1], row[0:1, t * P:(t + 1) * P], ones[0:1, 0:1], start=True, stop=True)
            mm.then_inc(weights_psum, 1)
            pe.wait_ge(weights_ready, 1)
            for t in range(ST):
                pe.matmul(pW[:, 8:9], ones[:], wcol[:, t:t + 1], start=t == 0, stop=t == ST - 1)

            def scores(n, slot):
                h = slot % 2
                wait_slot(pe, c_loaded[h], n, slot, 2, dmas=2)
                for e in range(DB):
                    for t in range(ST):
                        pe.matmul(pC[:, e * B + n:e * B + n + 1] if isinstance(n, int) else pC[:, bass.ds(n + e * B, 1)],
                                  C[:, h, t, e * P:(e + 1) * P], wcol[:, t:t + 1], start=t == 0, stop=t == ST - 1)
                wait_item(pe, klo_ready, n)
                wait_item(pe, qlo_ready, n)
                for e in range(DB):
                    wait_item(pe, exps_ready, n, back=1, per=DB, of=e)
                    for t in range(ST):
                        mm = split_matmul(pe, pS[e][:], [k[:, h, t, e * P:(e + 1) * P] for k in Kp],
                                          [q[:, h, t] for q in Qp], t == 0, t == ST - 1)
                    mm.then_inc(scores_ready, 1)

            def out(n, slot):
                h = slot % 2
                wait_item(pe, v_ready, n)
                for t in range(ST):
                    wait_item(pe, out_added, n, back=1, per=ST, of=t)
                    for e in range(DB):
                        wait_item(pe, elo_ready, n, per=DB, of=e)
                        mm = split_matmul(pe, pO[t][:], [v[:, h, e, t * P:(t + 1) * P] for v in Vp],
                                          [x[:, h, e] for x in Ep], e == 0, e == DB - 1)
                    mm.then_inc(out_ready, 1)

            run_pipeline(pe.Fori, B, U, 2, [(1, scores), (2, out)])

            pe.nop().then_inc(cw_ready, 1)
            pe.wait_ge(states_ready, 1)
            for e in range(DB):
                for h in range(DB):
                    mm = pe.matmul(pS[e][:, 0:B], WinT[:, h, e * P:(e + 1) * P], cw[:, h], start=h == 0, stop=h == DB - 1)
            mm.then_inc(states_psum, 1)
            pe.wait_ge(states_ready, 3 + DB)
            wait_item(pe, out_added, B - 1, per=ST)
            for e in range(DB):
                pe.matmul(pO[0][0:B, :], states[:, e], WoutT[:, e], start=e == 0, stop=False)
            pe.matmul(pO[0][0:B, :], ones[0:1, 0:B], bout[:], start=False, stop=True).then_inc(summary_psum, 1)


def mx_front(dve, order, first, src, V, M, scale, rinv, ready):
    blocks = src.rearrange("p (k i) -> p k i", i=BLOCK)
    Vb = V.rearrange("p (k i) -> p k i", i=BLOCK)
    dve.tensor_reduce(scale, blocks, AX.X, ALU.max, apply_absolute_value=True).then_inc(order, 1)
    dve.wait_ge(order, first + 1)
    dve.tensor_scalar(scale, scale, 1.0 / FP8_MAX, SCALE_MIN, ALU.mult, ALU.max).then_inc(order, 1)
    dve.wait_ge(order, first + 2)
    dve.reciprocal(rinv, scale).then_inc(order, 1)
    dve.wait_ge(order, first + 3)
    dve.tensor_tensor(Vb, blocks, rinv.unsqueeze(2).to_broadcast([P, 512 // BLOCK, BLOCK]), ALU.mult).then_inc(order, 1)
    dve.wait_ge(order, first + 4)
    dve.tensor_scalar(M.bitcast(I32), V.bitcast(I32), EXPONENT, HALF_BIT, ALU.bitwise_and,
                      ALU.bitwise_or).then_inc(order, 1)
    dve.wait_ge(order, first + 5)
    dve.tensor_scalar(M, M, 1.5 * 2.0 ** -6, 2.0 ** 20, ALU.max, ALU.mult).then_inc(order, 1)
    dve.wait_ge(order, first + 6)
    dve.tensor_tensor(V, V, M, ALU.add).then_inc(ready, 1)


MX_STEPS = 6


def mx_weights(nc, io, shared, W):
    (Gp, Dp) = W
    F, D = io["down_w"].shape[1], io["down_w"].shape[0]
    NG = 2 * F // P
    DT = D // P
    ND = DT * F // 512
    U, KB = 4, 512 // P
    with ExitStack() as ctx:
        m = Memory(nc, ctx)
        L = m.sbuf("w_tiles", [P, U, 512])
        V = m.sbuf("w_quantised", [P, 2, 512])
        M = m.sbuf("w_rounders", [P, 2, 512])
        scale = m.sbuf("w_scales", [P, 2, 512 // BLOCK])
        rinv = m.sbuf("w_scale_inverses", [P, 512 // BLOCK])
        pT = [m.psum(f"pWT{i}") for i in range(U)]
        w_loaded = m.sems("w_loaded", U)
        w_order, w_front, w_sub, w_deq = m.sem("w_order"), m.sem("w_front"), m.sem("w_sub"), m.sem("w_deq")
        w_turned, w_hi, w_lo = m.sem("w_turned"), m.sem("w_hi"), m.sem("w_lo")
        block = ctx.enter_context(nc.Block())

        def place_gu(part, n, slot):
            return Gp[part][:, :, bass.ds(n * P, P)]

        def place_d(part, n, slot):
            c = slot % (F // 512)
            return Dp[part][:, c * KB:(c + 1) * KB, bass.ds((n - c) * (P // U), P)]

        passes = [(0, NG, place_gu), (NG, ND, place_d)]

        def source(first, n, slot):
            if first == 0:
                return io["gate_up_w"][bass.ds(n * P, P), :]
            c = slot % (F // 512)
            return io["down_w"][bass.ds((n - c) * (P // U), P), c * 512:(c + 1) * 512]

        @block.sync
        def _(sp):
            for first, count, _ in passes:
                def load(n, slot, first=first):
                    wait_item(sp, w_front, n + first, back=U)
                    sp.dma_start(L[:, slot], source(first, n, slot)).then_inc(w_loaded[slot], 16)
                run_pipeline(sp.Fori, count, U, U, [(0, load)])

        @block.vector
        def _(dve):
            for first, count, place in passes:
                def quantise(n, slot, first=first):
                    i, h = n + first, slot % 2
                    wait_slot(dve, w_loaded[slot], i, slot, U)
                    wait_item(dve, w_turned, i, back=2)
                    wait_item(dve, w_deq, i, back=2)
                    mx_front(dve, w_order, i * MX_STEPS, L[:, slot], V[:, h], M[:, h], scale[:, h], rinv[:], w_front)

                def lo(n, slot, first=first, place=place):
                    wait_item(dve, w_hi, n + first)
                    dve.tensor_tensor(place(1, n, slot), pT[slot][:].rearrange("p (k i) -> p k i", i=P),
                                      place(0, n, slot).bitcast(F32), ALU.subtract).then_inc(w_lo, 1)
                run_pipeline(dve.Fori, count, U, 2, [(0, quantise), (2, lo)])

        @block.gpsimd
        def _(pool):
            for first, count, _ in passes:
                def dequantise(n, slot, first=first):
                    i, h = n + first, slot % 2
                    wait_item(pool, w_front, i)
                    pool.tensor_tensor(V[:, h], V[:, h], M[:, h], ALU.subtract).then_inc(w_sub, 1)
                    wait_item(pool, w_sub, i)
                    Vb = V[:, h].rearrange("p (k i) -> p k i", i=BLOCK)
                    pool.tensor_tensor(Vb, Vb, scale[:, h].unsqueeze(2).to_broadcast([P, 512 // BLOCK, BLOCK]),
                                       ALU.mult).then_inc(w_deq, 1)
                run_pipeline(pool.Fori, count, U, 0, [(0, dequantise)])

        @block.tensor
        def _(pe):
            for first, count, _ in passes:
                def turn(n, slot, first=first):
                    i, h = n + first, slot % 2
                    wait_item(pe, w_deq, i)
                    wait_item(pe, w_lo, i, back=U)
                    for k in range(KB):
                        mm = pe.transpose(pT[slot][:, k * P:(k + 1) * P], V[:, h, k * P:(k + 1) * P], shared["ident"][:])
                    mm.then_inc(w_turned, 1)
                run_pipeline(pe.Fori, count, U, U, [(0, turn)])

        @block.scalar
        def _(act):
            for first, count, place in passes:
                def hi(n, slot, first=first, place=place):
                    wait_item(act, w_turned, n + first)
                    act.activation(place(0, n, slot), pT[slot][:].rearrange("p (k i) -> p k i", i=P),
                                   ACT.Copy).then_inc(w_hi, 1)
                run_pipeline(act.Fori, count, U, 0, [(0, hi)])


def mx_ffn(nc, io, shared, W):
    Gp, Dp = W
    F, D = io["down_w"].shape[1], io["down_w"].shape[0]
    T = shared["x1"].shape[0]
    NT, DB, NC, KB = T // P, D // P, F // 512, 512 // P
    U = 4
    with ExitStack() as ctx:
        m = Memory(nc, ctx)
        X = m.sbuf("x_tiles2", [P, U, D])
        XV = m.sbuf("x_quantised", [P, D])
        V = m.sbuf("h_quantised", [P, 2, 512])
        M = m.sbuf("rounders", [P, 512])
        XT = [m.sbuf(f"xT_{s}", [P, 2, DB, P], F32R) for s in ("hi", "lo")]
        HT = [m.sbuf(f"hT_{s}", [P, KB, P], F32R) for s in ("hi", "lo")]
        stats, mv = m.sbuf("ln_stats2", [P, 6]), m.sbuf("mean_var2", [P, 2])
        veps, rstd = m.sbuf("var_eps2", [P, 1]), m.sbuf("rstd2", [P, 1])
        hscale = m.sbuf("h_scales", [P, 2, 512 // BLOCK])
        xscale = m.sbuf("x_scales", [P, 512 // BLOCK])
        rinv = m.sbuf("scale_inverses", [P, 512 // BLOCK])
        pG = [m.psum(f"pGate{i}") for i in range(2)]
        pU = [m.psum(f"pUp{i}") for i in range(2)]
        pY = [m.psum(f"pY{i}") for i in range(2)]
        pH, pX = m.psum("pHT"), m.psum("pXT")

        x_loaded, x_stored = m.sems("x_loaded2", U), m.sems("x_stored2", U)
        stats_ready, mv_ready, veps_ready = m.sem("stats_ready2"), m.sem("mv_ready2"), m.sem("veps_ready2")
        rstd_ready, normed = m.sem("rstd_ready2"), m.sem("normed")
        x_order, x_front, x_sub, x_deq = m.sem("x_order"), m.sem("x_front"), m.sem("x_sub"), m.sem("x_deq")
        x_turned, x_hi, x_lo = m.sem("x_turned"), m.sem("x_hi"), m.sem("x_lo")
        gu_ready, silu_ready, h_ready = m.sem("gate_up_ready"), m.sem("silu_ready"), m.sem("h_ready")
        h_order, h_front, h_sub, h_deq = m.sem("h_order"), m.sem("h_front"), m.sem("h_sub"), m.sem("h_deq")
        h_turned, h_hi, h_lo = m.sem("h_turned"), m.sem("h_hi"), m.sem("h_lo")
        down_done, y_added = m.sem("down_done"), m.sem("y_added")
        block = ctx.enter_context(nc.Block())

        def per_chunk(lag, body, c):
            return lag, lambda n, slot: body(n, slot, c)

        @block.sync
        def _(sp):
            def load(n, slot):
                sp.dma_start(X[:, slot], shared["x1"][bass.ds(n * P, P), :]).then_inc(x_loaded[slot], 16)

            def store(n, slot):
                wait_item(sp, y_added, n)
                sp.dma_start(shared["x2"][bass.ds(n * P, P), :], X[:, slot]).then_inc(x_stored[slot], 16)

            for n in range(U):
                load(n, n)
            with sp.Fori(0, NT - 2 * U + 1, U) as base:
                for j in range(U):
                    store(base + j, j)
                    wait_slot(sp, x_stored[j], base + j, j, U)
                    load(base + (j + U), j)
            for j in range(U):
                store(NT - U + j, j)
            for j in range(U):
                wait_slot(sp, x_stored[j], NT - U + j, j, U)

        @block.tensor
        def _(pe):
            def turn_x(n, slot):
                wait_item(pe, x_deq, n)
                wait_item(pe, x_lo, n, back=1)
                for k in range(DB):
                    mm = pe.transpose(pX[:, k * P:(k + 1) * P], XV[:, k * P:(k + 1) * P], shared["ident"][:])
                mm.then_inc(x_turned, 1)

            def gate_up(n, slot, c):
                if c == 0:
                    wait_item(pe, x_hi, n)
                    wait_item(pe, x_lo, n)
                if c < 2:
                    wait_item(pe, h_ready, n, back=1, per=NC, of=c + 2)
                else:
                    wait_item(pe, h_ready, n, per=NC, of=c - 2)
                for out, first in ((pG[c % 2], 0), (pU[c % 2], F)):
                    for k in range(DB):
                        mm = split_matmul(pe, out[:], [x[:, slot % 2, k] for x in XT],
                                          [w[:, k, first + c * 512:first + (c + 1) * 512] for w in Gp],
                                          k == 0, k == DB - 1)
                mm.then_inc(gu_ready, 1)

            def turn_h(n, slot, c):
                wait_item(pe, h_deq, n, per=NC, of=c)
                if c:
                    wait_item(pe, h_lo, n, per=NC, of=c - 1)
                else:
                    wait_item(pe, h_lo, n, back=1, per=NC)
                for k in range(KB):
                    mm = pe.transpose(pH[:, k * P:(k + 1) * P], V[:, c % 2, k * P:(k + 1) * P], shared["ident"][:])
                mm.then_inc(h_turned, 1)

            def down(n, slot, c):
                wait_item(pe, h_hi, n, per=NC, of=c)
                wait_item(pe, h_lo, n, per=NC, of=c)
                if c == 0:
                    wait_item(pe, y_added, n, back=2)
                for k in range(KB):
                    mm = split_matmul(pe, pY[slot % 2][:], [h[:, k] for h in HT], [w[:, c * KB + k] for w in Dp],
                                      c == 0 and k == 0, c == NC - 1 and k == KB - 1)
                mm.then_inc(down_done, 1)

            stages = []
            for c in range(NC):
                stages.append(per_chunk(2, turn_h, c + 1) if c + 1 < NC else per_chunk(1, turn_h, 0))
                stages.append(per_chunk(2, down, c))
                if c == NC - 1:
                    stages.append((0, turn_x))
                stages.append(per_chunk(1, gate_up, c))
            run_pipeline(pe.Fori, NT, U, 2, stages)

        @block.scalar
        def _(act):
            def silu(n, slot, c):
                wait_item(act, gu_ready, n, per=NC, of=c)
                if c < 2:
                    wait_item(act, h_turned, n, back=1, per=NC, of=c + 2)
                else:
                    wait_item(act, h_turned, n, per=NC, of=c - 2)
                act.activation(V[:, c % 2], pG[c % 2][:], ACT.Silu).then_inc(silu_ready, 1)

            def h_part(n, slot, c):
                wait_item(act, h_turned, n, per=NC, of=c)
                if c:
                    wait_item(act, down_done, n, per=NC, of=c - 1)
                else:
                    wait_item(act, down_done, n, back=1, per=NC)
                act.activation(HT[0][:], pH[:].rearrange("p (k i) -> p k i", i=P), ACT.Copy).then_inc(h_hi, 1)

            def x_part(n, slot):
                wait_item(act, x_turned, n)
                wait_item(act, gu_ready, n, back=2, per=NC)
                act.activation(XT[0][:, slot % 2], pX[:].rearrange("p (k i) -> p k i", i=P), ACT.Copy).then_inc(x_hi, 1)

            stages = []
            for c in range(NC):
                stages.append(per_chunk(1, silu, c - 1) if c else per_chunk(2, silu, NC - 1))
                stages.append(per_chunk(2, h_part, c + 1) if c + 1 < NC else per_chunk(1, h_part, 0))
            stages.append((0, x_part))
            run_pipeline(act.Fori, NT, U, 2, stages)

        @block.vector
        def _(dve):
            def norm_stats(n, slot):
                wait_slot(dve, x_loaded[slot], n, slot, U)
                dve.bn_stats(stats[:], X[:, slot]).then_inc(stats_ready, 1)
                wait_item(dve, stats_ready, n)
                wait_item(dve, normed, n, back=1)
                own_wait(dve, shared["passed_dve"])
                dve.bn_aggr(mv[:], stats[:]).then_inc(mv_ready, 1)

            def norm_quantise(n, slot):
                wait_item(dve, rstd_ready, n)
                wait_item(dve, x_turned, n, back=1)
                dve.tensor_scalar(XV[:], X[:, slot], mv[:, 0:1], rstd[:, 0:1], ALU.subtract, ALU.mult).then_inc(normed, 1)
                wait_item(dve, normed, n)
                wait_item(dve, h_sub, n, back=1, per=NC, of=1)
                mx_front(dve, x_order, n * MX_STEPS, XV[:], XV[:], M[:], xscale[:], rinv[:], x_front)

            def hidden(n, slot, c):
                wait_item(dve, silu_ready, n, per=NC, of=c)
                V_ = V[:, c % 2]
                dve.tensor_tensor(V_, V_, pU[c % 2][:], ALU.mult).then_inc(h_ready, 1)
                wait_item(dve, h_ready, n, per=NC, of=c)
                if c:
                    wait_item(dve, h_sub, n, per=NC, of=c - 1)
                else:
                    wait_item(dve, h_sub, n, back=1, per=NC)
                if c == 2:
                    wait_item(dve, x_sub, n + 1 if not isinstance(n, int) else min(n + 1, NT - 1))
                mx_front(dve, h_order, (n * NC + c) * MX_STEPS, V_, V_, M[:], hscale[:, c % 2], rinv[:], h_front)

            def h_part(n, slot, c):
                wait_item(dve, h_hi, n, per=NC, of=c)
                dve.tensor_tensor(HT[1][:], pH[:].rearrange("p (k i) -> p k i", i=P), HT[0][:].bitcast(F32),
                                  ALU.subtract).then_inc(h_lo, 1)

            def x_part(n, slot):
                wait_item(dve, x_hi, n)
                dve.tensor_tensor(XT[1][:, slot % 2], pX[:].rearrange("p (k i) -> p k i", i=P),
                                  XT[0][:, slot % 2].bitcast(F32), ALU.subtract).then_inc(x_lo, 1)

            def add_y(n, slot):
                wait_item(dve, down_done, n, per=NC)
                dve.scalar_tensor_tensor(out=X[:, slot], in0=pY[slot % 2][:], scalar=shared["gates"][:, 2:3],
                                         in1=X[:, slot], op0=ALU.mult, op1=ALU.add).then_inc(y_added, 1)

            stages = []
            for c in range(NC):
                stages.append(per_chunk(1, hidden, c - 1) if c else per_chunk(2, hidden, NC - 1))
                stages.append(per_chunk(2, h_part, c + 1) if c + 1 < NC else per_chunk(1, h_part, 0))
                if c == 0:
                    stages.append((0, norm_stats))
                if c == 2:
                    stages.append((0, norm_quantise))
            stages.append((2, add_y))
            stages.append((0, x_part))
            run_pipeline(dve.Fori, NT, U, 2, stages)

        @block.gpsimd
        def _(pool):
            def rstd_of(n, slot):
                wait_item(pool, mv_ready, n)
                own_wait(pool, shared["passed_pool"])
                pool.tensor_scalar(veps[:], mv[:, 1:2], LN_EPS, None, ALU.add).then_inc(veps_ready, 1)
                wait_item(pool, veps_ready, n)
                pool.tensor_tensor(rstd[:], veps[:], shared["minus_half"][:, 0:1], ALU.pow).then_inc(rstd_ready, 1)

            def back(front, sub, deq, i, V_, scale):
                Vb = V_.rearrange("p (k i) -> p k i", i=BLOCK)
                pool.wait_ge(front, i + 1)
                pool.tensor_tensor(V_, V_, M[:], ALU.subtract).then_inc(sub, 1)
                pool.wait_ge(sub, i + 1)
                pool.tensor_tensor(Vb, Vb, scale.unsqueeze(2).to_broadcast([P, 512 // BLOCK, BLOCK]),
                                   ALU.mult).then_inc(deq, 1)

            def x_back(n, slot):
                back(x_front, x_sub, x_deq, n, XV[:], xscale[:])

            def h_back(n, slot, c):
                back(h_front, h_sub, h_deq, n * NC + c, V[:, c % 2], hscale[:, c % 2])

            stages = []
            for c in range(NC):
                stages.append(per_chunk(1, h_back, c - 1) if c else per_chunk(2, h_back, NC - 1))
                if c == 0:
                    stages.append((0, rstd_of))
                if c == 2:
                    stages.append((0, x_back))
            run_pipeline(pool.Fori, NT, U, 2, stages)


def mx_layer(nc, io, shared):
    F, D = io["down_w"].shape[1], io["down_w"].shape[0]
    with ExitStack() as ctx:
        m = Memory(nc, ctx)
        W = ([m.sbuf(f"gate_upT_{s}", [P, D // P, 2 * F], F32R) for s in ("hi", "lo")],
             [m.sbuf(f"downT_{s}", [P, F // P, D], F32R) for s in ("hi", "lo")])
        mx_weights(nc, io, shared, W)
        mx_ffn(nc, io, shared, W)


def fp4_weights(nc, io, shared, Wp):
    total = Wp[0].shape[1]
    CH = 1408
    N = total // CH
    with ExitStack() as ctx:
        m = Memory(nc, ctx)
        words = m.sbuf("fp4_words", [P, 2, CH], I32)
        scales = m.sbuf("fp4_scales", [P, 2, CH], F16)
        code = m.sbuf("fp4_codes", [P, 2, CH], I32)
        sign = m.sbuf("fp4_signs", [P, 2, CH], I32)
        half = m.sbuf("code_by_2", [P, 2, CH])
        twice = m.sbuf("code_twice_less_8", [P, 2, CH])
        val = m.sbuf("fp4_values", [P, 2, CH])
        shift = m.sbuf("nibble_shifts", [P, 2], I32)
        less_8 = m.sbuf("less_8", [P, 1])
        shifts_loaded = m.sem("shifts_loaded")
        words_loaded = m.sems("words_loaded", 2)
        less_8_ready = m.sem("less_8_ready")
        code_ready, sign_ready = m.sem("code_ready"), m.sem("sign_ready")
        act_parts, mid_ready, mag_ready = m.sem("act_parts"), m.sem("mid_ready"), m.sem("mag_ready")
        scaled, signed = m.sem("scaled"), m.sem("signed")
        whi_ready, wlo_ready = m.sem("w3_hi_ready"), m.sem("w3_lo_ready")
        block = ctx.enter_context(nc.Block())

        def span(n):
            return bass.ds(n * CH, CH)

        @block.sync
        def _(sp):
            sp.dma_start(shift[:], io["nibble_shifts"]).then_inc(shifts_loaded, 16)

            def load(n, slot):
                wait_item(sp, sign_ready, n, back=2)
                wait_item(sp, scaled, n, back=2)
                sp.dma_start(words[:, slot], io["fp4_packed"][:, span(n)]).then_inc(words_loaded[slot], 16)
                sp.dma_start(scales[:, slot], io["fp4_scales"][0:1, span(n)].to_broadcast([P, CH]))\
                    .then_inc(words_loaded[slot], 16)
            run_pipeline(sp.Fori, N, 2, 2, [(0, load)])

        @block.vector
        def _(dve):
            dve.memset(less_8[:], -8.0).then_inc(less_8_ready, 1)
            dve.wait_ge(shifts_loaded, 16)

            def codes(n, slot):
                wait_slot(dve, words_loaded[slot], n, slot, 2, dmas=2)
                wait_item(dve, act_parts, n, back=2, per=2)
                wait_item(dve, mid_ready, n, back=2)
                dve.tensor_scalar(code[:, slot], words[:, slot], shift[:, 0:1], 7, ALU.logical_shift_right,
                                  ALU.bitwise_and).then_inc(code_ready, 1)
                wait_item(dve, signed, n, back=2)
                dve.tensor_scalar(sign[:, slot], words[:, slot], shift[:, 1:2], -2147483648, ALU.logical_shift_left,
                                  ALU.bitwise_and).then_inc(sign_ready, 1)

            def values(n, slot):
                wait_item(dve, act_parts, n, per=2)
                wait_item(dve, wlo_ready, n, back=2)
                dve.scalar_tensor_tensor(out=half[:, slot], in0=code[:, slot], scalar=2.0, in1=half[:, slot],
                                         op0=ALU.subtract, op1=ALU.max).then_inc(mid_ready, 1)
                wait_item(dve, mid_ready, n)
                dve.tensor_tensor(half[:, slot], half[:, slot], twice[:, slot], ALU.max).then_inc(mag_ready, 1)
                wait_item(dve, mag_ready, n)
                dve.tensor_tensor(val[:, slot], half[:, slot], scales[:, slot], ALU.mult).then_inc(scaled, 1)
                wait_item(dve, scaled, n)
                dve.tensor_tensor(val[:, slot].bitcast(I32), val[:, slot].bitcast(I32), sign[:, slot],
                                  ALU.bitwise_xor).then_inc(signed, 1)

            run_pipeline(dve.Fori, N, 2, 2, [(0, codes), (1, values)])

        @block.scalar
        def _(act):
            act.wait_ge(less_8_ready, 1)

            def parts(n, slot):
                wait_item(act, code_ready, n)
                wait_item(act, scaled, n, back=2)
                act.activation(half[:, slot], code[:, slot], ACT.Copy, scale=0.5).then_inc(act_parts, 1)
                act.activation(twice[:, slot], code[:, slot], ACT.Identity, bias=less_8[:, 0:1], scale=2.0)\
                    .then_inc(act_parts, 1)

            def hi(n, slot):
                wait_item(act, signed, n)
                act.activation(Wp[0][:, span(n)], val[:, slot], ACT.Copy).then_inc(whi_ready, 1)

            run_pipeline(act.Fori, N, 2, 2, [(0, parts), (1, hi)])

        @block.gpsimd
        def _(pool):
            def lo(n, slot):
                wait_item(pool, whi_ready, n)
                pool.tensor_tensor(Wp[1][:, span(n)], val[:, slot], Wp[0][:, span(n)].bitcast(F32), ALU.subtract)\
                    .then_inc(wlo_ready, 1)
            run_pipeline(pool.Fori, N, 2, 0, [(0, lo)])


def fp4_ffn(nc, io, shared, Wp, out):
    B = shared["summary"].shape[0]
    T, D = shared["x2"].shape
    F = io["fp4_inner"]
    DB, FB = D // P, F // P
    GT = 512 // P
    NG = T // (GT * P)
    GB = B // NG
    U = 2
    USES = FB + 2
    down_at = DB * 2 * F
    with ExitStack() as ctx:
        m = Memory(nc, ctx)
        X = m.sbuf("x_groups", [P, U, GT, D])
        Z = m.sbuf("z_group", [P, GT, D])
        summ = m.sbuf("summary_bc", [P, U, GB, D])
        gamma, beta = m.sbuf("gamma_bc", [P, D]), m.sbuf("beta_bc", [P, D])
        XT = [m.sbuf(f"x3T_{s}", [P, U, DB, GT * P], F32R) for s in ("hi", "lo")]
        H = m.sbuf("h3", [P, 2, GT * P])
        HT = [m.sbuf(f"h3_{s}", [P, 2, GT * P], F32R) for s in ("hi", "lo")]
        stats, mv = m.sbuf("ln_stats3", [P, GT, 6]), m.sbuf("mean_var3", [P, GT, 2])
        veps, rstd = m.sbuf("var_eps3", [P, GT]), m.sbuf("rstd3", [P, GT])
        squares, sums = m.sbuf("y_squares", [P, 2, D]), m.sbuf("y_square_sums", [P, GT])
        meps, rrms, grms = m.sbuf("mean_square_eps", [P, GT]), m.sbuf("rms_inverse", [P, GT]), m.sbuf("gated_rms", [P, GT])
        pG = [m.psum(f"p3G{i}") for i in range(2)]
        pU = [m.psum(f"p3U{i}") for i in range(2)]
        pY = [m.psum(f"p3Y{i}") for i in range(GT)]

        consts_loaded = m.sem("consts3_loaded")
        x_loaded, s_loaded, stored = m.sems("x3_loaded", U), m.sems("s_loaded", U), m.sems("x3_stored", U)
        affine_ready = m.sem("affine_ready")
        stats_ready, mv_ready, veps_ready, rstd_ready = (m.sem(n + "3") for n in ("stats_r", "mv_r", "veps_r", "rstd_r"))
        normed, summed, scaled, shifted, mixed = (m.sem(n + "3") for n in ("normed", "summed", "scaled", "shifted", "mixed"))
        x_turned, x_hi, x_lo = m.sem("x3_turned"), m.sem("x3_hi"), m.sem("x3_lo")
        gu_ready, silu_ready, h_ready = m.sem("gu3_ready"), m.sem("silu3_ready"), m.sem("h3_ready")
        h_hi, h_lo, down_done = m.sem("h3_hi"), m.sem("h3_lo"), m.sem("down3_done")
        squared, meps_ready, rrms_ready, grms_ready = (m.sem(n) for n in ("squared", "meps_r", "rrms_r", "grms_r"))
        y_added = m.sem("y3_added")
        block = ctx.enter_context(nc.Block())
        gates, minus_half = shared["gates"], shared["minus_half"]

        x_in = shared["x2"].rearrange("(g t p) d -> g p t d", p=P, t=GT)
        x_out = out.rearrange("b (t p) d -> (b t) p d", p=P).rearrange("(g t) p d -> g p t d", t=GT)

        def gate_w(part, g, b, up):
            at = g * 2 * F + up * F + b * P
            return Wp[part][:, at:at + P]

        def down_w(part, b):
            return Wp[part][:, down_at + b * D:down_at + (b + 1) * D]

        @block.sync
        def _(sp):
            def load(n, slot):
                sp.dma_start(X[:, slot], x_in[n]).then_inc(x_loaded[slot], 16)
                for b in range(GB):
                    sp.dma_start(summ[:, slot, b], shared["summary"][bass.ds(n * GB + b, 1), :].to_broadcast([P, D]))\
                        .then_inc(s_loaded[slot], 16)

            def store(n, slot):
                wait_item(sp, y_added, n, per=GT)
                sp.dma_start(x_out[n], X[:, slot]).then_inc(stored[slot], 16)

            sp.dma_start(gamma[:], io["gamma"].rearrange("(a n) -> a n", a=1).to_broadcast([P, D])).then_inc(consts_loaded, 16)
            sp.dma_start(beta[:], io["beta"].rearrange("(a n) -> a n", a=1).to_broadcast([P, D])).then_inc(consts_loaded, 16)
            load(0, 0)
            load(1, 1)
            with sp.Fori(0, NG - 2 * U + 1, U) as base:
                for j in range(U):
                    store(base + j, j)
                    wait_slot(sp, stored[j], base + j, j, U)
                    load(base + (j + U), j)
            for j in range(U):
                store(NG - U + j, j)
            for j in range(U):
                wait_slot(sp, stored[j], NG - U + j, j, U)

        @block.vector
        def _(dve):
            dve.wait_ge(consts_loaded, 32)
            dve.tensor_scalar(gamma[:], gamma[:], gates[:, 1:2], None, ALU.mult).then_inc(affine_ready, 1)
            dve.tensor_scalar(beta[:], beta[:], gates[:, 1:2], None, ALU.mult).then_inc(affine_ready, 1)
            dve.wait_ge(affine_ready, 2)

            def statistics(src, n, k):
                wait_item(dve, normed, n, per=3, of=k - 1) if k else wait_item(dve, normed, n, back=1, per=3)
                for t in range(GT):
                    ins = dve.bn_stats(stats[:, t], src[:, t])
                ins.then_inc(stats_ready, 1)
                wait_item(dve, stats_ready, n, per=3, of=k)
                own_wait(dve, shared["passed_dve"])
                for t in range(GT):
                    ins = dve.bn_aggr(mv[:, t], stats[:, t])
                ins.then_inc(mv_ready, 1)

            def normalise(dst, src, n, k):
                wait_item(dve, rstd_ready, n, per=3, of=k)
                for t in range(GT):
                    ins = dve.tensor_scalar(dst[:, t], src[:, t], mv[:, t, 0:1], rstd[:, t:t + 1], ALU.subtract, ALU.mult)
                ins.then_inc(normed, 1)

            def mix_1(n, slot):
                wait_slot(dve, x_loaded[slot], n, slot, U)
                statistics(X[:, slot], n, 0)

            def mix_2(n, slot):
                wait_item(dve, x_turned, n, back=1, per=GT)
                normalise(Z, X[:, slot], n, 0)

            def mix_3(n, slot):
                wait_item(dve, summed, n)
                statistics(Z, n, 1)

            def mix_4(n, slot):
                normalise(Z, Z, n, 1)

            def mix_5(n, slot):
                wait_item(dve, scaled, n)
                dve.tensor_tensor(Z[:], Z[:], beta[:].unsqueeze(1).to_broadcast([P, GT, D]), ALU.add).then_inc(shifted, 1)
                wait_item(dve, shifted, n)
                dve.tensor_tensor(X[:, slot], X[:, slot], Z[:], ALU.add).then_inc(mixed, 1)
                wait_item(dve, mixed, n)
                statistics(X[:, slot], n, 2)

            def mix_6(n, slot):
                normalise(Z[:].rearrange("p t (g j w) -> p t g w j", g=DB, j=8),
                          X[:, slot].rearrange("p t (g w j) -> p t g w j", g=DB, j=8), n, 2)

            def x_part(n, slot):
                for t in range(GT):
                    wait_item(dve, x_hi, n, per=GT, of=t)
                    use = (slot - 1) % U * USES + FB + t // 2
                    bank = (pG, pU)[t % 2][use % 2]
                    dve.tensor_tensor(XT[1][:, slot, :, t * P:(t + 1) * P], bank[:].rearrange("p (k i) -> p k i", i=P),
                                      XT[0][:, slot, :, t * P:(t + 1) * P].bitcast(F32), ALU.subtract).then_inc(x_lo, 1)

            def hidden(n, slot, b):
                use = slot * USES + b
                h = b % 2
                wait_item(dve, silu_ready, n, per=FB, of=b)
                dve.tensor_tensor(H[:, h], H[:, h], pU[use % 2][:], ALU.mult).then_inc(h_ready, 1)
                wait_item(dve, h_hi, n, per=FB, of=b)
                dve.tensor_tensor(HT[1][:, h], H[:, h], HT[0][:, h].bitcast(F32), ALU.subtract).then_inc(h_lo, 1)

            def add_y(n, slot):
                wait_item(dve, rrms_ready, n)
                dve.tensor_scalar(grms[:], rrms[:], gates[:, 3:4], None, ALU.mult).then_inc(grms_ready, 1)
                wait_item(dve, grms_ready, n)
                for t in range(GT):
                    dve.scalar_tensor_tensor(out=X[:, slot, t], in0=pY[t][:], scalar=grms[:, t:t + 1], in1=X[:, slot, t],
                                             op0=ALU.mult, op1=ALU.add).then_inc(y_added, 1)

            between = {1: (0, mix_1), 2: (0, mix_2), 4: (0, mix_3), 5: (0, mix_4), 7: (0, mix_5), 8: (0, mix_6)}
            stages = []
            for b in range(FB):
                stages.append((1, lambda n, slot, b=b: hidden(n, slot, b)))
                if b in between:
                    stages.append(between[b])
            run_pipeline(dve.Fori, NG, U, 2, stages + [(0, x_part), (1, add_y)])

        @block.gpsimd
        def _(pool):
            pool.wait_ge(affine_ready, 2)

            def rstd_of(n, slot, k):
                wait_item(pool, mv_ready, n, per=3, of=k)
                own_wait(pool, shared["passed_pool"])
                pool.tensor_scalar(veps[:], mv[:, :, 1], LN_EPS, None, ALU.add).then_inc(veps_ready, 1)
                wait_item(pool, veps_ready, n, per=3, of=k)
                pool.tensor_tensor(rstd[:], veps[:], minus_half[:], ALU.pow).then_inc(rstd_ready, 1)

            def mix(n, slot):
                rstd_of(n, slot, 0)
                wait_item(pool, normed, n, per=3, of=0)
                wait_slot(pool, s_loaded[slot], n, slot, U, dmas=GB)
                Zb = Z[:].rearrange("p (b t) d -> p b t d", b=GB)
                for b in range(GB):
                    ins = pool.tensor_tensor(Zb[:, b], Zb[:, b],
                                             summ[:, slot, b].unsqueeze(1).to_broadcast([P, GT // GB, D]), ALU.add)
                ins.then_inc(summed, 1)
                rstd_of(n, slot, 1)
                wait_item(pool, normed, n, per=3, of=1)
                pool.tensor_tensor(Z[:], Z[:], gamma[:].unsqueeze(1).to_broadcast([P, GT, D]), ALU.mult).then_inc(scaled, 1)
                rstd_of(n, slot, 2)

            def rms(n, slot):
                wait_item(pool, squared, n, per=GT)
                own_wait(pool, shared["passed_pool"])
                pool.tensor_scalar(meps[:], sums[:], 1.0 / D, RMS_EPS, ALU.mult, ALU.add).then_inc(meps_ready, 1)
                wait_item(pool, meps_ready, n)
                pool.tensor_tensor(rrms[:], meps[:], minus_half[:], ALU.pow).then_inc(rrms_ready, 1)

            run_pipeline(pool.Fori, NG, U, 2, [(0, mix), (1, rms)])

        @block.scalar
        def _(act):
            def silu(n, slot, b):
                use = slot * USES + b
                h = b % 2
                wait_item(act, gu_ready, n, per=FB, of=b)
                if b >= 2:
                    wait_item(act, h_lo, n, per=FB, of=b - 2)
                else:
                    wait_item(act, h_lo, n, back=1, per=FB)
                act.activation(H[:, h], pG[use % 2][:], ACT.Silu).then_inc(silu_ready, 1)
                wait_item(act, h_ready, n, per=FB, of=b)
                if b >= 2:
                    wait_item(act, down_done, n, per=FB, of=b - 2)
                else:
                    wait_item(act, down_done, n, back=1, per=FB)
                act.activation(HT[0][:, h], H[:, h], ACT.Copy).then_inc(h_hi, 1)

            def x_part(n, slot):
                for t in range(GT):
                    use = (slot - 1) % U * USES + FB + t // 2
                    bank = (pG, pU)[t % 2][use % 2]
                    wait_item(act, x_turned, n, per=GT, of=t)
                    act.activation(XT[0][:, slot, :, t * P:(t + 1) * P], bank[:].rearrange("p (k i) -> p k i", i=P),
                                   ACT.Copy).then_inc(x_hi, 1)

            def squares_of(n, slot):
                wait_item(act, down_done, n, per=FB)
                wait_item(act, meps_ready, n, back=1)
                for t in range(GT):
                    if t >= 2:
                        wait_item(act, squared, n, per=GT, of=t - 2)
                    act.activation(squares[:, t % 2], pY[t][:], ACT.Square, accum_out=sums[:, t:t + 1]).then_inc(squared, 1)

            stages = [(1, lambda n, slot, b=b: silu(n, slot, b)) for b in range(FB)]
            run_pipeline(act.Fori, NG, U, 2, stages + [(0, x_part), (1, squares_of)])

        @block.tensor
        def _(pe):
            def gate_up(n, slot, b):
                use = slot * USES + b
                if b == 0:
                    wait_item(pe, x_hi, n, per=GT)
                    wait_item(pe, x_lo, n, per=GT)
                if b >= 2:
                    wait_item(pe, h_ready, n, per=FB, of=b - 2)
                for bank, up in ((pG[use % 2], 0), (pU[use % 2], 1)):
                    for g in range(DB):
                        mm = split_matmul(pe, bank[:], [gate_w(s, g, b, up) for s in (0, 1)],
                                          [x[:, slot, g] for x in XT], g == 0, g == DB - 1)
                mm.then_inc(gu_ready, 1)

            def down(n, slot, b):
                wait_item(pe, h_hi, n, per=FB, of=b)
                wait_item(pe, h_lo, n, per=FB, of=b)
                for t in range(GT):
                    if b == 0:
                        wait_item(pe, y_added, n, back=1, per=GT, of=t)
                    mm = split_matmul(pe, pY[t][:], [h[:, b % 2, t * P:(t + 1) * P] for h in HT],
                                      [down_w(s, b) for s in (0, 1)], b == 0, b == FB - 1)
                mm.then_inc(down_done, 1)

            def turn(n, slot):
                wait_item(pe, normed, n, per=3)
                for t in range(GT):
                    use = (slot - 1) % U * USES + FB + t // 2
                    bank = (pG, pU)[t % 2][use % 2]
                    if t % 2 == 0:
                        wait_item(pe, h_ready, n, back=1, per=FB, of=FB - 2 + t // 2)
                    for g in range(DB):
                        mm = pe.transpose(bank[:, g * P:(g + 1) * P], Z[:, t, g * P:(g + 1) * P], shared["ident"][:])
                    mm.then_inc(x_turned, 1)

            stages = []
            for b in range(FB):
                stages.append((1, lambda n, slot, b=b: gate_up(n, slot, b)))
                if b:
                    stages.append((1, lambda n, slot, b=b: down(n, slot, b - 1)))
            stages.append((0, turn))
            stages.append((1, lambda n, slot: down(n, slot, FB - 1)))
            run_pipeline(pe.Fori, NG, U, 2, stages)


def fp4_layer(nc, io, shared, out):
    D, F = shared["x2"].shape[1], io["fp4_inner"]
    with ExitStack() as ctx:
        m = Memory(nc, ctx)
        Wp = [m.sbuf(f"fp4_w_{s}", [P, (D // P) * 2 * F + (F // P) * D], F32R) for s in ("hi", "lo")]
        fp4_weights(nc, io, shared, Wp)
        fp4_ffn(nc, io, shared, Wp, out)


def build(nc, io, out, debug=None):
    B, S, D = io["x"].shape
    T = B * S
    with ExitStack() as ctx:
        m = Memory(nc, ctx)
        shared = {
            "gates": m.sbuf("tanh_gates", [P, 4]), "ident": m.sbuf("identity", [P, P]),
            "minus_half": m.sbuf("minus_half", [P, 4]),
            **{f"passed_{e}": m.sem(f"passed_{e}") for e in ("sp", "dve", "pool")},
            "x1": nc.dram_tensor("x_after_attention", [T, D], F32, kind="Internal").ap(),
            "x2": nc.dram_tensor("x_after_mx_ffn", [T, D], F32, kind="Internal").ap(),
            "summary": nc.dram_tensor("summary", [B, D], F32, kind="Internal").ap(),
        }
        attend(nc, io, shared)
        mx_layer(nc, io, shared)
        fp4_layer(nc, io, shared, out)


def kernel(**inputs):
    import concourse.bacc as bacc
    import numpy as np
    from concourse.bass_utils import run_bass_kernel_spmd

    a = {name: np.asarray(value) for name, value in inputs.items()}
    D = a["x"].shape[-1]
    F4 = a["L1_ffn_down_packed"].shape[1] * 8
    gate_up = a["L1_ffn_gate_up_packed"].T.reshape(D // P, 16, 2 * F4)
    down = a["L1_ffn_down_packed"].T.reshape(F4 // P, 16, D)
    order = (np.arange(2 * F4).reshape(-1, 16, 8)).transpose(0, 2, 1).reshape(-1)
    words = np.concatenate([gate_up[:, :, order].transpose(1, 0, 2).reshape(16, -1),
                            down.transpose(1, 0, 2).reshape(16, -1)], axis=1)
    scales = np.concatenate([a["L1_ffn_gate_up_scales"][:, order].reshape(1, -1),
                             a["L1_ffn_down_scales"].reshape(1, -1)], axis=1)
    nibble = 4 * (np.arange(P, dtype=np.int32) // 16)
    arrays = {
        "x": a["x"], "ctx": a["ctx_2048"], "ctxT": a["ctx_2048"].transpose(0, 2, 1),
        "g_xattn": a["g_xattn"], "g_ffn": a["g_ffn"],
        "gate_up_w": np.concatenate([a["L0_ffn_gate_w"], a["L0_ffn_up_w"]]), "down_w": a["L0_ffn_down_w"],
        "decay": a["L1_xattn_decay"].reshape(1, 1), "W_inT": a["L1_xattn_W_in"].T, "W_outT": a["L1_xattn_W_out"].T,
        "b_in": a["L1_xattn_b_in"].reshape(D // P, P).T, "b_out": a["L1_xattn_b_out"],
        "gamma": a["L1_xattn_gamma"], "beta": a["L1_xattn_beta"],
        "fp4_packed": np.tile(words, (8, 1)), "fp4_scales": scales,
        "nibble_shifts": np.stack([nibble, 28 - nibble], axis=1),
    }
    arrays = {f"in_{name}": np.ascontiguousarray(value) for name, value in arrays.items()}
    nc = bacc.Bacc("TRN2", target_bir_lowering=False, num_devices=1, dynamic_dma_scratch_size=1024)
    io = {name[3:]: nc.dram_tensor(name, value.shape, mybir.dt.from_np(value.dtype), kind="ExternalInput").ap()
          for name, value in arrays.items()}
    io["fp4_inner"] = F4
    out = nc.dram_tensor("out", a["x"].shape, F32, kind="ExternalOutput").ap()
    build(nc, io, out)
    return run_bass_kernel_spmd(nc, [arrays], core_ids=[0]).results[0]["out"]
```

```python
from contextlib import ExitStack

import concourse.bass as bass
from concourse import mybir
from concourse.alu_op_type import AluOpType as ALU

F32 = mybir.dt.float32
F32R = mybir.dt.float32r
F16 = mybir.dt.float16
F8E5 = mybir.dt.float8e5
I32 = mybir.dt.int32
ACT = mybir.ActivationFunctionType
AX = mybir.AxisListType

P = 128
LN_EPS = 1e-5
RMS_EPS = 1e-6
W_STEPS = 5
BLOCK = 32
FP8_MAX = 448.0
SCALE_MIN = 1e-30
EXPONENT = 0x7F800000
HALF_BIT = 0x00400000
HIHI_HILO_LOHI = ((0, 0), (0, 1), (1, 0))


def run_pipeline(loop, n_items, unroll, peel, stages):
    most = max(lag for lag, _ in stages)
    start = most + peel
    rounds = max(0, n_items - start) // unroll

    def tick(t, base):
        for lag, body in stages:
            if base is not None:
                body(base + (t - lag), (t - lag) % unroll)
            elif 0 <= t - lag < n_items:
                body(t - lag, (t - lag) % unroll)

    for t in range(start):
        tick(t, None)
    if rounds:
        with loop(0, (rounds - 1) * unroll + 1, unroll) as base:
            for t in range(start, start + unroll):
                tick(t, base)
    for t in range(start + rounds * unroll, n_items + most):
        tick(t, None)


def wait_item(eng, sem, n, back=0, per=1, of=None):
    if isinstance(n, int) and n < back:
        return
    eng.wait_ge(sem, (n - back) * per + (per if of is None else of + 1))


def signed(bits):
    return bits - (bits >> 31 << 32)


def wait_slot(eng, sem, n, slot, slots, dmas=1):
    eng.wait_ge(sem, (n - slot % slots) * (16 * dmas // slots) + 16 * dmas)


def own_wait(eng, passed):
    eng.sem_inc(passed, 1)


class Memory:

    def __init__(self, nc, ctx):
        self.nc, self.ctx = nc, ctx

    def sbuf(self, name, shape, dtype=F32, side=None):
        return self.ctx.enter_context(self.nc.sbuf_tensor(name, shape, dtype, side=side))

    def psum(self, name, shape=(P, 512)):
        return self.ctx.enter_context(self.nc.psum_tensor(name, list(shape), F32))

    def sem(self, name):
        return self.ctx.enter_context(self.nc.semaphore(name))

    def sems(self, name, n):
        return [self.sem(f"{name}{i}") for i in range(n)]


def split_matmul(pe, out, stationary, moving, first, last):
    for n, (a, b) in enumerate(HIHI_HILO_LOHI):
        mm = pe.matmul(out, stationary[a], moving[b], start=first and n == 0, stop=last and n == 2)
    return mm


def attend(nc, io, shared):
    B, S, D = io["x"].shape
    ST, DB = S // P, D // P
    U = 4
    SCALE = float(D) ** -0.5
    Qgu, Qdn, w_scales = shared["gate_up_q"], shared["down_q"], shared["w_scales"]
    GUT = Qgu.shape[1] // B
    WT = GUT + Qdn.shape[1] // B
    WB = WT * 512 // BLOCK
    with ExitStack() as ctx:
        m = Memory(nc, ctx)
        X = m.sbuf("x_tiles", [P, U, ST, D])
        C = m.sbuf("ctx_tiles", [P, 2, ST, D])
        CT = m.sbuf("ctx_transposed", [P, 2, DB, S])
        Q = m.sbuf("q", [P, 2, ST, D])
        Qp = [m.sbuf(f"q_{s}", [P, 2, ST, D], F32R) for s in ("hi", "lo")]
        Kp = [m.sbuf(f"k_{s}", [P, 2, ST, D], F32R) for s in ("hi", "lo")]
        Vp = [m.sbuf(f"vT_{s}", [P, 2, DB, S], F32R) for s in ("hi", "lo")]
        E = m.sbuf("exps", [P, 2, D])
        Ep = [m.sbuf(f"exp_{s}", [P, 2, DB, D], F32R) for s in ("hi", "lo")]
        L = m.sbuf("w_tiles", [P, 2, WT, 512])
        M = m.sbuf("w_rounders", [P, 2, WT, 512])
        w_rinv = m.sbuf("w_scale_inverses", [P, WB])
        stats = m.sbuf("ln_stats", [P, 2, ST, 6])
        mv = m.sbuf("mean_var", [P, 2, ST, 2])
        veps = m.sbuf("var_eps", [P, 2, ST])
        rstd = m.sbuf("rstd", [P, 2, ST])
        nmax = m.sbuf("neg_max", [P, 2, DB])
        bias = m.sbuf("exp_bias", [P, 2, DB])
        zsum = m.sbuf("exp_sum", [P, 2, DB])
        rz = m.sbuf("exp_sum_inverse", [P, 2, DB])
        ones = m.sbuf("ones", [P, P])
        keep = m.sbuf("keep", [1, 2])
        row = m.sbuf("decay_row", [1, S])
        wcol = m.sbuf("state_weights", [P, ST])
        WinT = m.sbuf("W_inT_sb", [P, DB, D])
        WoutT = m.sbuf("W_outT_sb", [P, DB, D])
        bin_ = m.sbuf("b_in_columns", [P, DB])
        bout = m.sbuf("b_out_row", [1, D])
        bw = m.sbuf("b_in_weighted", [P, DB])
        sumw = m.sbuf("state_weight_sum", [P, 1])
        cw = m.sbuf("ctx_weighted", [P, DB, B])
        states = m.sbuf("mean_states", [P, DB, B])
        summ = m.sbuf("summary_rows", [B, D])
        pS = [m.psum(f"pScores{i}") for i in range(DB)]
        pO = [m.psum(f"pOut{i}") for i in range(ST)]
        pC = m.psum("pCtxWeighted")
        pW = m.psum("pSmall")

        consts_loaded = m.sem("consts_loaded")
        x_loaded, x_stored = m.sems("x_loaded", U), m.sems("x_stored", U)
        c_loaded = m.sems("c_loaded", 2)
        summary_stored = m.sem("summary_stored")
        gates_ready, keep_ready, row_ready = m.sem("gates_ready"), m.sem("keep_ready"), m.sem("row_ready")
        weights_psum, weights_ready = m.sem("weights_psum"), m.sem("weights_ready")
        stats_ready, mv_ready, veps_ready = m.sem("stats_ready"), m.sem("mv_ready"), m.sem("veps_ready")
        rstd_ready, q_ready = m.sem("rstd_ready"), m.sem("q_ready")
        qhi_ready, qlo_ready = m.sem("qhi_ready"), m.sem("qlo_ready")
        khi_ready, klo_ready = m.sem("khi_ready"), m.sem("klo_ready")
        scores_ready, nmax_ready, bias_ready = m.sem("scores_ready"), m.sem("nmax_ready"), m.sem("bias_ready")
        exps_ready, ehi_ready, elo_ready = m.sem("exps_ready"), m.sem("ehi_ready"), m.sem("elo_ready")
        rz_ready, vhi_ready, v_ready = m.sem("rz_ready"), m.sem("vhi_ready"), m.sem("v_ready")
        out_ready, out_added = m.sem("out_ready"), m.sem("out_added")
        const_order = m.sem("const_order")
        w_loaded = m.sems("w_loaded", 2)
        w_order, w_front, w_rounded, w_quantised = (m.sem(n) for n in ("w_order", "w_front", "w_rounded", "w_quantised"))
        cw_ready, states_psum, states_ready = m.sem("cw_ready"), m.sem("states_psum"), m.sem("states_ready")
        summary_psum, summary_ready = m.sem("summary_psum"), m.sem("summary_ready")
        block = ctx.enter_context(nc.Block())

        x_in = io["x"].rearrange("b (t p) d -> b p t d", p=P)
        c_in = io["ctx"].rearrange("b (t p) d -> b p t d", p=P)
        ct_in = io["ctxT"].rearrange("b (e p) s -> b p e s", p=P)
        x_out = shared["x1"].rearrange("(b t p) d -> b p t d", p=P, t=ST)
        gu_in = io["gate_up_w"].rearrange("(b k p) d -> b p k d", p=P, k=GUT)
        dn_in = io["down_tiles"].rearrange("(b k p) d -> b p k d", p=P, k=WT - GUT)
        gates, ident = shared["gates"], shared["ident"]
        CONSTS = 7

        @block.sync
        def _(sp):
            def load_x(n, slot):
                sp.dma_start(X[:, slot], x_in[n]).then_inc(x_loaded[slot], 16)

            def load_ctx(n, slot):
                sp.dma_start(C[:, slot % 2], c_in[n]).then_inc(c_loaded[slot % 2], 16)
                sp.dma_start(CT[:, slot % 2], ct_in[n]).then_inc(c_loaded[slot % 2], 16)

            def const(dst, src):
                sp.dma_start(dst, src).then_inc(consts_loaded, 16)

            def next_ctx(n, slot):
                wait_item(sp, scores_ready, n, per=DB)
                own_wait(sp, shared["passed_sp"])
                wait_item(sp, v_ready, n)
                own_wait(sp, shared["passed_sp"])
                load_ctx(n + 2, slot)

            def load_w(n, slot):
                sp.dma_start(L[:, slot % 2, 0:GUT], gu_in[n]).then_inc(w_loaded[slot % 2], 16)
                sp.dma_start(L[:, slot % 2, GUT:WT], dn_in[n]).then_inc(w_loaded[slot % 2], 16)

            def next_w(n, slot):
                wait_item(sp, w_quantised, n)
                own_wait(sp, shared["passed_sp"])
                load_w(n + 2, slot)

            def store_x(n, slot):
                wait_item(sp, out_added, n, per=ST)
                sp.dma_start(x_out[n], X[:, slot]).then_inc(x_stored[slot], 16)

            def next_x(n, slot):
                wait_slot(sp, x_stored[slot], n, slot, U)
                load_x(n + U, slot)

            load_x(0, 0)
            load_ctx(0, 0)
            const(gates[:, 0:2], io["g_xattn"].rearrange("(a n) -> a n", a=1).to_broadcast([P, 2]))
            const(gates[:, 2:4], io["g_ffn"].rearrange("(a n) -> a n", a=1).to_broadcast([P, 2]))
            const(keep[0:1, 0:1], io["decay"])
            const(bin_[:], io["b_in"])
            const(bout[:], io["b_out"].rearrange("(a n) -> a n", a=1))
            load_w(0, 0)
            load_x(1, 1)
            load_ctx(1, 1)
            load_w(1, 1)
            load_x(2, 2)
            load_x(3, 3)
            const(WinT[:], io["W_inT"].rearrange("(e p) n -> p e n", p=P))
            const(WoutT[:], io["W_outT"].rearrange("(e p) n -> p e n", p=P))
            next_ctx(0, 0)
            next_w(0, 0)
            with sp.Fori(0, B - 2 * U + 1, U) as base:
                for j in range(U):
                    next_ctx(base + (j + 1), (j + 1) % U)
                    next_w(base + (j + 1), (j + 1) % U)
                    store_x(base + j, j)
                    next_x(base + j, j)
            for n in range(B - U, B):
                if n + 3 < B:
                    next_ctx(n + 1, (n + 1) % U)
                    next_w(n + 1, (n + 1) % U)
                store_x(n, n % U)
            for j in range(U):
                wait_slot(sp, x_stored[j], B - U + j, j, U)
            sp.wait_ge(summary_ready, 1)
            sp.dma_start(shared["summary"], summ[:]).then_inc(summary_stored, 16)
            sp.wait_ge(summary_stored, 16)

        @block.gpsimd
        def _(pool):
            pool.memset(ident[:], 0.0).then_inc(const_order, 1)
            pool.memset(shared["minus_half"][:], -0.5).then_inc(const_order, 1)
            pool.memset(ones[:], 1.0).then_inc(const_order, 1)
            pool.wait_ge(const_order, 3)
            pool.affine_select(out=ident[:], in_=ident[:], compare_op=ALU.not_equal, fill=1.0,
                               base=0, pattern=[[-1, P]], channel_multiplier=1).then_inc(const_order, 1)

            def rstd_of(n, slot):
                h = slot % 2
                wait_item(pool, mv_ready, n, per=ST)
                wait_item(pool, q_ready, n, back=2, per=ST)
                own_wait(pool, shared["passed_pool"])
                pool.tensor_scalar(veps[:, h], mv[:, h, :, 1], LN_EPS, None, ALU.add).then_inc(veps_ready, 1)
                wait_item(pool, veps_ready, n)
                pool.tensor_tensor(rstd[:, h], veps[:, h], shared["minus_half"][:, 0:ST],
                                   ALU.pow).then_inc(rstd_ready, 1)

            def k_lo(n, slot):
                h = slot % 2
                wait_item(pool, khi_ready, n)
                pool.tensor_tensor(Kp[1][:, h], C[:, h], Kp[0][:, h].bitcast(F32), ALU.subtract)\
                    .then_inc(klo_ready, 1)

            def e_lo(n, slot):
                h = slot % 2
                for e in range(DB):
                    wait_item(pool, ehi_ready, n, per=DB, of=e)
                    pool.tensor_tensor(Ep[1][:, h, e], E[:, e % 2], Ep[0][:, h, e].bitcast(F32),
                                       ALU.subtract).then_inc(elo_ready, 1)

            def w_values(n, slot):
                h = slot % 2
                wait_item(pool, w_front, n)
                pool.tensor_tensor(L[:, h], L[:, h], M[:, h], ALU.add).then_inc(w_rounded, 1)
                wait_item(pool, w_rounded, n)
                pool.tensor_tensor(Qgu[:, n * GUT:(n + 1) * GUT] if isinstance(n, int) else Qgu[:, bass.ds(n * GUT, GUT)],
                                   L[:, h, 0:GUT], M[:, h, 0:GUT], ALU.subtract)
                pool.tensor_tensor(Qdn[:, n:n + 1] if isinstance(n, int) else Qdn[:, bass.ds(n, 1)],
                                   L[:, h, GUT:WT], M[:, h, GUT:WT], ALU.subtract).then_inc(w_quantised, 1)

            run_pipeline(pool.Fori, B, U, 2, [(0, rstd_of), (0, k_lo), (1, e_lo), (1, w_values)])

        @block.scalar
        def _(act):
            act.wait_ge(consts_loaded, 16 * CONSTS)
            act.activation(gates[:], gates[:], ACT.Tanh).then_inc(gates_ready, 1)
            act.activation(keep[0:1, 1:2], keep[0:1, 0:1], ACT.Sigmoid).then_inc(keep_ready, 1)

            def k_hi(n, slot):
                h = slot % 2
                wait_slot(act, c_loaded[h], n, slot, 2, dmas=2)
                wait_item(act, scores_ready, n, back=2, per=DB)
                act.activation(Kp[0][:, h], C[:, h], ACT.Copy).then_inc(khi_ready, 1)

            def q_hi(n, slot):
                h = slot % 2
                wait_item(act, q_ready, n, per=ST)
                wait_item(act, scores_ready, n, back=2, per=DB)
                act.activation(Qp[0][:, h], Q[:, h], ACT.Copy).then_inc(qhi_ready, 1)

            def exps(n, slot):
                h = slot % 2
                wait_item(act, out_ready, n, back=2, per=ST)
                for e in range(DB):
                    wait_item(act, bias_ready, n, per=DB, of=e)
                    if e >= 2:
                        wait_item(act, elo_ready, n, per=DB, of=e - 2)
                    else:
                        wait_item(act, elo_ready, n, back=1, per=DB, of=e + DB - 2)
                    act.activation(E[:, e % 2], pS[e][:], ACT.Exp, bias=bias[:, h, e:e + 1], scale=SCALE,
                                   accum_out=zsum[:, h, e:e + 1]).then_inc(exps_ready, 1)
                    wait_item(act, exps_ready, n, per=DB, of=e)
                    act.activation(Ep[0][:, h, e], E[:, e % 2], ACT.Copy).then_inc(ehi_ready, 1)

            run_pipeline(act.Fori, B, U, 2, [(0, k_hi), (1, exps), (0, q_hi)])

        @block.vector
        def _(dve):
            dve.wait_ge(keep_ready, 1)
            dve.wait_ge(const_order, 4)
            dve.tensor_tensor_scan(row[:, ::-1], keep[0:1, 1:2].to_broadcast([1, S]), ones[0:1, 0:1].to_broadcast([1, S]),
                                   0.0, ALU.mult, ALU.add).then_inc(row_ready, 1)
            dve.wait_ge(weights_psum, 1)
            dve.tensor_scalar(wcol[:], pW[:, 0:ST], 1.0 / S, None, ALU.mult).then_inc(weights_ready, 1)
            dve.wait_ge(gates_ready, 1)

            def norm_stats(n, slot):
                h = slot % 2
                wait_slot(dve, x_loaded[slot], n, slot, U)
                for t in range(ST):
                    dve.bn_stats(stats[:, h, t], X[:, slot, t]).then_inc(stats_ready, 1)
                wait_item(dve, rstd_ready, n, back=2)
                wait_item(dve, q_ready, n, back=2, per=ST)
                for t in range(ST):
                    wait_item(dve, stats_ready, n, per=ST, of=t)
                    own_wait(dve, shared["passed_dve"])
                    dve.bn_aggr(mv[:, h, t], stats[:, h, t]).then_inc(mv_ready, 1)

            def norm(n, slot):
                h = slot % 2
                wait_item(dve, rstd_ready, n)
                wait_item(dve, qlo_ready, n, back=2)
                for t in range(ST):
                    dve.tensor_scalar(Q[:, h, t], X[:, slot, t], mv[:, h, t, 0:1], rstd[:, h, t:t + 1],
                                      ALU.subtract, ALU.mult).then_inc(q_ready, 1)

            def q_lo(n, slot):
                h = slot % 2
                wait_item(dve, qhi_ready, n)
                dve.tensor_tensor(Qp[1][:, h], Q[:, h], Qp[0][:, h].bitcast(F32), ALU.subtract)\
                    .then_inc(qlo_ready, 1)

            def maxima(n, slot):
                h = slot % 2
                for e in range(DB):
                    wait_item(dve, scores_ready, n, per=DB, of=e)
                    dve.tensor_reduce(nmax[:, h, e:e + 1], pS[e][:], AX.X, ALU.max, negate=True)\
                        .then_inc(nmax_ready, 1)
                    wait_item(dve, nmax_ready, n, per=DB, of=e)
                    dve.tensor_scalar(bias[:, h, e:e + 1], nmax[:, h, e:e + 1], SCALE, None, ALU.mult)\
                        .then_inc(bias_ready, 1)

            def scale_v(n, slot):
                h = slot % 2
                wait_item(dve, out_ready, n, back=2, per=ST)
                for e in range(DB):
                    wait_item(dve, exps_ready, n, per=DB, of=e)
                    wait_item(dve, ehi_ready, n, per=DB, of=e)
                    dve.reciprocal(rz[:, h, e:e + 1], zsum[:, h, e:e + 1]).then_inc(rz_ready, 1)
                    wait_item(dve, rz_ready, n, per=DB, of=e)
                    dve.tensor_scalar(Vp[0][:, h, e], CT[:, h, e], rz[:, h, e:e + 1], None, ALU.mult)\
                        .then_inc(vhi_ready, 1)
                    wait_item(dve, vhi_ready, n, per=DB, of=e)
                    last = dve.scalar_tensor_tensor(out=Vp[1][:, h, e], in0=CT[:, h, e], scalar=rz[:, h, e:e + 1],
                                                    in1=Vp[0][:, h, e].bitcast(F32), op0=ALU.mult, op1=ALU.subtract)
                last.then_inc(v_ready, 1)

            def add_out(n, slot):
                for t in range(ST):
                    wait_item(dve, out_ready, n, per=ST, of=t)
                    dve.scalar_tensor_tensor(out=X[:, slot, t], in0=pO[t][:], scalar=gates[:, 0:1],
                                             in1=X[:, slot, t], op0=ALU.mult, op1=ALU.add).then_inc(out_added, 1)

            def w_blocks(slot):
                return L[:, slot % 2].rearrange("p t (k i) -> p (t k) i", i=BLOCK)

            def scales_of(n):
                return w_scales[:, n * WB:(n + 1) * WB] if isinstance(n, int) else w_scales[:, bass.ds(n * WB, WB)]

            def w_step(n, of):
                wait_item(dve, w_order, n, per=W_STEPS, of=of)

            def w_max(n, slot):
                wait_slot(dve, w_loaded[slot % 2], n, slot, 2, dmas=2)
                dve.tensor_reduce(scales_of(n), w_blocks(slot), AX.X, ALU.max, apply_absolute_value=True).then_inc(w_order, 1)

            def w_scale(n, slot):
                w_step(n, 0)
                dve.tensor_scalar(scales_of(n), scales_of(n), 1.0 / FP8_MAX, SCALE_MIN, ALU.mult, ALU.max).then_inc(w_order, 1)

            def w_inverse(n, slot):
                w_step(n, 1)
                own_wait(dve, shared["passed_dve"])
                dve.reciprocal(w_rinv[:], scales_of(n)).then_inc(w_order, 1)

            def w_v(n, slot):
                w_step(n, 2)
                dve.tensor_tensor(w_blocks(slot), w_blocks(slot), w_rinv[:].unsqueeze(2).to_broadcast([P, WB, BLOCK]),
                                  ALU.mult).then_inc(w_order, 1)

            def w_exponent(n, slot):
                w_step(n, 3)
                dve.tensor_scalar(M[:, slot % 2].bitcast(I32), L[:, slot % 2].bitcast(I32), EXPONENT, HALF_BIT,
                                  ALU.bitwise_and, ALU.bitwise_or).then_inc(w_order, 1)

            def w_rounder(n, slot):
                w_step(n, 4)
                dve.tensor_scalar(M[:, slot % 2], M[:, slot % 2], 1.5 * 2.0 ** -6, 2.0 ** 20, ALU.max,
                                  ALU.mult).then_inc(w_front, 1)

            run_pipeline(dve.Fori, B, U, 2, [(0, norm_stats), (0, w_max), (1, maxima), (0, w_scale), (0, norm),
                                             (0, w_inverse), (1, scale_v), (0, w_v), (0, q_lo), (0, w_exponent),
                                             (2, add_out), (0, w_rounder)])

            dve.wait_ge(cw_ready, 1)
            dve.tensor_copy(cw[:], pC[:, 0:DB * B].rearrange("p (e b) -> p e b", e=DB)).then_inc(states_ready, 1)
            dve.tensor_copy(sumw[:], pW[:, 8:9]).then_inc(states_ready, 1)
            dve.wait_ge(states_ready, 2)
            dve.tensor_scalar(bw[:], bin_[:], sumw[:, 0:1], None, ALU.mult).then_inc(states_ready, 1)
            dve.wait_ge(states_psum, 1)
            dve.wait_ge(states_ready, 3)
            for e in range(DB):
                dve.tensor_scalar(states[:, e], pS[e][:, 0:B], bw[:, e:e + 1], None, ALU.add).then_inc(states_ready, 1)
            dve.wait_ge(summary_psum, 1)
            dve.tensor_copy(summ[:], pO[0][0:B, :]).then_inc(summary_ready, 1)

        @block.tensor
        def _(pe):
            pe.wait_ge(row_ready, 1)
            for t in range(ST):
                mm = pe.matmul(pW[:, t:t + 1], row[0:1, t * P:(t + 1) * P], ones[0:1, 0:1], start=True, stop=True)
            mm.then_inc(weights_psum, 1)
            pe.wait_ge(weights_ready, 1)
            for t in range(ST):
                pe.matmul(pW[:, 8:9], ones[:], wcol[:, t:t + 1], start=t == 0, stop=t == ST - 1)

            def scores(n, slot):
                h = slot % 2
                wait_slot(pe, c_loaded[h], n, slot, 2, dmas=2)
                for e in range(DB):
                    for t in range(ST):
                        pe.matmul(pC[:, e * B + n:e * B + n + 1] if isinstance(n, int) else pC[:, bass.ds(n + e * B, 1)],
                                  C[:, h, t, e * P:(e + 1) * P], wcol[:, t:t + 1], start=t == 0, stop=t == ST - 1)
                wait_item(pe, klo_ready, n)
                wait_item(pe, qlo_ready, n)
                for e in range(DB):
                    wait_item(pe, exps_ready, n, back=1, per=DB, of=e)
                    for t in range(ST):
                        mm = split_matmul(pe, pS[e][:], [k[:, h, t, e * P:(e + 1) * P] for k in Kp],
                                          [q[:, h, t] for q in Qp], t == 0, t == ST - 1)
                    mm.then_inc(scores_ready, 1)

            def out(n, slot):
                h = slot % 2
                wait_item(pe, v_ready, n)
                for t in range(ST):
                    wait_item(pe, out_added, n, back=1, per=ST, of=t)
                    for e in range(DB):
                        wait_item(pe, elo_ready, n, per=DB, of=e)
                        mm = split_matmul(pe, pO[t][:], [v[:, h, e, t * P:(t + 1) * P] for v in Vp],
                                          [x[:, h, e] for x in Ep], e == 0, e == DB - 1)
                    mm.then_inc(out_ready, 1)

            run_pipeline(pe.Fori, B, U, 2, [(1, scores), (2, out)])

            pe.nop().then_inc(cw_ready, 1)
            pe.wait_ge(states_ready, 1)
            for e in range(DB):
                for h in range(DB):
                    mm = pe.matmul(pS[e][:, 0:B], WinT[:, h, e * P:(e + 1) * P], cw[:, h], start=h == 0, stop=h == DB - 1)
            mm.then_inc(states_psum, 1)
            pe.wait_ge(states_ready, 3 + DB)
            wait_item(pe, out_added, B - 1, per=ST)
            for e in range(DB):
                pe.matmul(pO[0][0:B, :], states[:, e], WoutT[:, e], start=e == 0, stop=False)
            pe.matmul(pO[0][0:B, :], ones[0:1, 0:B], bout[:], start=False, stop=True).then_inc(summary_psum, 1)


def mx_front(dve, order, first, src, V, M, scale, rinv, ready):
    blocks = src.rearrange("p (k i) -> p k i", i=BLOCK)
    Vb = V.rearrange("p (k i) -> p k i", i=BLOCK)
    dve.tensor_reduce(scale, blocks, AX.X, ALU.max, apply_absolute_value=True).then_inc(order, 1)
    dve.wait_ge(order, first + 1)
    dve.tensor_scalar(scale, scale, 1.0 / FP8_MAX, SCALE_MIN, ALU.mult, ALU.max).then_inc(order, 1)
    dve.wait_ge(order, first + 2)
    dve.reciprocal(rinv, scale).then_inc(order, 1)
    dve.wait_ge(order, first + 3)
    dve.tensor_tensor(Vb, blocks, rinv.unsqueeze(2).to_broadcast([P, 512 // BLOCK, BLOCK]), ALU.mult).then_inc(order, 1)
    dve.wait_ge(order, first + 4)
    dve.tensor_scalar(M.bitcast(I32), V.bitcast(I32), EXPONENT, HALF_BIT, ALU.bitwise_and,
                      ALU.bitwise_or).then_inc(order, 1)
    dve.wait_ge(order, first + 5)
    dve.tensor_scalar(M, M, 1.5 * 2.0 ** -6, 2.0 ** 20, ALU.max, ALU.mult).then_inc(order, 1)
    dve.wait_ge(order, first + 6)
    dve.tensor_tensor(V, V, M, ALU.add).then_inc(ready, 1)


MX_STEPS = 6


def mx_weights(nc, shared, what, source, scale_at, place):
    U, KB = 4, 512 // P
    NT, NS = source.shape[1], 512 // BLOCK
    with ExitStack() as ctx:
        m = Memory(nc, ctx)
        V = m.sbuf(f"w_{what}", [P, U, 512])
        pT = [m.psum(f"p_{what}T{i}") for i in range(U)]
        scaled = m.sems(f"w_{what}_scaled", U)
        turned, hi_ready, lo_ready = (m.sem(f"w_{what}_{s}") for s in ("turned", "hi", "lo"))
        block = ctx.enter_context(nc.Block())
        ON_VECTOR = U - 1

        def scale_values(eng, n, slot):
            wait_item(eng, turned, n, back=U)
            values = source[:, n] if isinstance(n, int) else source[:, bass.ds(n, 1)].rearrange("p a d -> p (a d)")
            at = scale_at(n, slot)
            scales = shared["w_scales"][:, at:at + NS] if isinstance(n, int) else shared["w_scales"][:, bass.ds(at, NS)]
            eng.tensor_tensor(V[:, slot].rearrange("p (k i) -> p k i", i=BLOCK), values.rearrange("p (k i) -> p k i", i=BLOCK),
                              scales.unsqueeze(2).to_broadcast([P, NS, BLOCK]), ALU.mult).then_inc(scaled[slot], U)

        @block.gpsimd
        def _(pool):
            def scale(n, slot):
                if slot != ON_VECTOR:
                    scale_values(pool, n, slot)
            run_pipeline(pool.Fori, NT, U, U, [(0, scale)])

        @block.vector
        def _(dve):
            def scale(n, slot):
                if slot == ON_VECTOR:
                    scale_values(dve, n, slot)

            def lo(n, slot):
                wait_item(dve, hi_ready, n)
                dve.tensor_tensor(place(1, n, slot), pT[slot][:].rearrange("p (k i) -> p k i", i=P),
                                  place(0, n, slot).bitcast(F32), ALU.subtract).then_inc(lo_ready, 1)
            run_pipeline(dve.Fori, NT, U, U, [(0, scale), (2, lo)])

        @block.tensor
        def _(pe):
            def turn(n, slot):
                pe.wait_ge(scaled[slot], n - slot + U)
                wait_item(pe, lo_ready, n, back=U)
                for k in range(KB):
                    mm = pe.transpose(pT[slot][:, k * P:(k + 1) * P], V[:, slot, k * P:(k + 1) * P], shared["ident"][:])
                mm.then_inc(turned, 1)
            run_pipeline(pe.Fori, NT, U, U, [(0, turn)])

        @block.scalar
        def _(act):
            def hi(n, slot):
                wait_item(act, turned, n)
                act.activation(place(0, n, slot), pT[slot][:].rearrange("p (k i) -> p k i", i=P),
                               ACT.Copy).then_inc(hi_ready, 1)
            run_pipeline(act.Fori, NT, U, 0, [(0, hi)])


def mx_ffn(nc, io, shared, W):
    Gp, Dp = W
    F, D = io["down_w_shape"][1], io["down_w_shape"][0]
    T = shared["x1"].shape[0]
    NT, DB, NC, KB = T // P, D // P, F // 512, 512 // P
    U = 4
    with ExitStack() as ctx:
        m = Memory(nc, ctx)
        X = m.sbuf("x_tiles2", [P, U, D])
        XV = m.sbuf("x_quantised", [P, D])
        V = m.sbuf("h_quantised", [P, 2, 512])
        M = m.sbuf("rounders", [P, 512])
        XT = [m.sbuf(f"xT_{s}", [P, 2, DB, P], F32R) for s in ("hi", "lo")]
        HT = [m.sbuf(f"hT_{s}", [P, KB, P], F32R) for s in ("hi", "lo")]
        stats, mv = m.sbuf("ln_stats2", [P, 6]), m.sbuf("mean_var2", [P, 2])
        veps, rstd = m.sbuf("var_eps2", [P, 1]), m.sbuf("rstd2", [P, 1])
        hscale = m.sbuf("h_scales", [P, 2, 512 // BLOCK])
        xscale = m.sbuf("x_scales", [P, 512 // BLOCK])
        rinv = m.sbuf("scale_inverses", [P, 512 // BLOCK])
        pG = [m.psum(f"pGate{i}") for i in range(2)]
        pU = [m.psum(f"pUp{i}") for i in range(2)]
        pY = [m.psum(f"pY{i}") for i in range(2)]
        pH, pX = m.psum("pHT"), m.psum("pXT")

        x_loaded, x_stored = m.sems("x_loaded2", U), m.sems("x_stored2", U)
        stats_ready, mv_ready, veps_ready = m.sem("stats_ready2"), m.sem("mv_ready2"), m.sem("veps_ready2")
        rstd_ready, normed = m.sem("rstd_ready2"), m.sem("normed")
        x_order, x_front, x_sub, x_deq = m.sem("x_order"), m.sem("x_front"), m.sem("x_sub"), m.sem("x_deq")
        x_turned, x_hi, x_lo = m.sem("x_turned"), m.sem("x_hi"), m.sem("x_lo")
        gu_ready, silu_ready, h_ready = m.sem("gate_up_ready"), m.sem("silu_ready"), m.sem("h_ready")
        h_order, h_front, h_sub, h_deq = m.sem("h_order"), m.sem("h_front"), m.sem("h_sub"), m.sem("h_deq")
        h_turned, h_hi, h_lo = m.sem("h_turned"), m.sem("h_hi"), m.sem("h_lo")
        down_done, y_added = m.sem("down_done"), m.sem("y_added")
        block = ctx.enter_context(nc.Block())

        def per_chunk(lag, body, c):
            return lag, lambda n, slot: body(n, slot, c)

        @block.sync
        def _(sp):
            def load(n, slot):
                sp.dma_start(X[:, slot], shared["x1"][bass.ds(n * P, P), :]).then_inc(x_loaded[slot], 16)

            def store(n, slot):
                wait_item(sp, y_added, n)
                sp.dma_start(shared["x2"][bass.ds(n * P, P), :], X[:, slot]).then_inc(x_stored[slot], 16)

            for n in range(U):
                load(n, n)
            with sp.Fori(0, NT - 2 * U + 1, U) as base:
                for j in range(U):
                    store(base + j, j)
                    wait_slot(sp, x_stored[j], base + j, j, U)
                    load(base + (j + U), j)
            for j in range(U):
                store(NT - U + j, j)
            for j in range(U):
                wait_slot(sp, x_stored[j], NT - U + j, j, U)

        @block.tensor
        def _(pe):
            def turn_x(n, slot):
                wait_item(pe, x_deq, n)
                wait_item(pe, x_lo, n, back=1)
                for k in range(DB):
                    mm = pe.transpose(pX[:, k * P:(k + 1) * P], XV[:, k * P:(k + 1) * P], shared["ident"][:])
                mm.then_inc(x_turned, 1)

            def gate_up(n, slot, c):
                if c == 0:
                    wait_item(pe, x_hi, n)
                    wait_item(pe, x_lo, n)
                if c < 2:
                    wait_item(pe, h_ready, n, back=1, per=NC, of=c + 2)
                else:
                    wait_item(pe, h_ready, n, per=NC, of=c - 2)
                for out, first in ((pG[c % 2], 0), (pU[c % 2], F)):
                    for k in range(DB):
                        mm = split_matmul(pe, out[:], [x[:, slot % 2, k] for x in XT],
                                          [w[:, k, first + c * 512:first + (c + 1) * 512] for w in Gp],
                                          k == 0, k == DB - 1)
                mm.then_inc(gu_ready, 1)

            def turn_h(n, slot, c):
                wait_item(pe, h_deq, n, per=NC, of=c)
                if c:
                    wait_item(pe, h_lo, n, per=NC, of=c - 1)
                else:
                    wait_item(pe, h_lo, n, back=1, per=NC)
                for k in range(KB):
                    mm = pe.transpose(pH[:, k * P:(k + 1) * P], V[:, c % 2, k * P:(k + 1) * P], shared["ident"][:])
                mm.then_inc(h_turned, 1)

            def down(n, slot, c):
                wait_item(pe, h_hi, n, per=NC, of=c)
                wait_item(pe, h_lo, n, per=NC, of=c)
                if c == 0:
                    wait_item(pe, y_added, n, back=2)
                for k in range(KB):
                    mm = split_matmul(pe, pY[slot % 2][:], [h[:, k] for h in HT], [w[:, c * KB + k] for w in Dp],
                                      c == 0 and k == 0, c == NC - 1 and k == KB - 1)
                mm.then_inc(down_done, 1)

            stages = []
            for c in range(NC):
                stages.append(per_chunk(2, turn_h, c + 1) if c + 1 < NC else per_chunk(1, turn_h, 0))
                stages.append(per_chunk(2, down, c))
                if c == NC - 1:
                    stages.append((0, turn_x))
                stages.append(per_chunk(1, gate_up, c))
            run_pipeline(pe.Fori, NT, U, 2, stages)

        @block.scalar
        def _(act):
            def silu(n, slot, c):
                wait_item(act, gu_ready, n, per=NC, of=c)
                if c < 2:
                    wait_item(act, h_turned, n, back=1, per=NC, of=c + 2)
                else:
                    wait_item(act, h_turned, n, per=NC, of=c - 2)
                act.activation(V[:, c % 2], pG[c % 2][:], ACT.Silu).then_inc(silu_ready, 1)

            def h_part(n, slot, c):
                wait_item(act, h_turned, n, per=NC, of=c)
                if c:
                    wait_item(act, down_done, n, per=NC, of=c - 1)
                else:
                    wait_item(act, down_done, n, back=1, per=NC)
                act.activation(HT[0][:], pH[:].rearrange("p (k i) -> p k i", i=P), ACT.Copy).then_inc(h_hi, 1)

            def x_part(n, slot):
                wait_item(act, x_turned, n)
                wait_item(act, gu_ready, n, back=2, per=NC)
                act.activation(XT[0][:, slot % 2], pX[:].rearrange("p (k i) -> p k i", i=P), ACT.Copy).then_inc(x_hi, 1)

            stages = []
            for c in range(NC):
                stages.append(per_chunk(1, silu, c - 1) if c else per_chunk(2, silu, NC - 1))
                stages.append(per_chunk(2, h_part, c + 1) if c + 1 < NC else per_chunk(1, h_part, 0))
            stages.append((0, x_part))
            run_pipeline(act.Fori, NT, U, 2, stages)

        @block.vector
        def _(dve):
            def norm_stats(n, slot):
                wait_slot(dve, x_loaded[slot], n, slot, U)
                dve.bn_stats(stats[:], X[:, slot]).then_inc(stats_ready, 1)
                wait_item(dve, stats_ready, n)
                wait_item(dve, normed, n, back=1)
                own_wait(dve, shared["passed_dve"])
                dve.bn_aggr(mv[:], stats[:]).then_inc(mv_ready, 1)

            def norm_quantise(n, slot):
                wait_item(dve, rstd_ready, n)
                wait_item(dve, x_turned, n, back=1)
                dve.tensor_scalar(XV[:], X[:, slot], mv[:, 0:1], rstd[:, 0:1], ALU.subtract, ALU.mult).then_inc(normed, 1)
                wait_item(dve, normed, n)
                wait_item(dve, h_sub, n, back=1, per=NC, of=1)
                mx_front(dve, x_order, n * MX_STEPS, XV[:], XV[:], M[:], xscale[:], rinv[:], x_front)

            def hidden(n, slot, c):
                wait_item(dve, silu_ready, n, per=NC, of=c)
                V_ = V[:, c % 2]
                dve.tensor_tensor(V_, V_, pU[c % 2][:], ALU.mult).then_inc(h_ready, 1)
                wait_item(dve, h_ready, n, per=NC, of=c)
                if c:
                    wait_item(dve, h_sub, n, per=NC, of=c - 1)
                else:
                    wait_item(dve, h_sub, n, back=1, per=NC)
                if c == 2:
                    wait_item(dve, x_sub, n + 1 if not isinstance(n, int) else min(n + 1, NT - 1))
                mx_front(dve, h_order, (n * NC + c) * MX_STEPS, V_, V_, M[:], hscale[:, c % 2], rinv[:], h_front)

            def h_part(n, slot, c):
                wait_item(dve, h_hi, n, per=NC, of=c)
                dve.tensor_tensor(HT[1][:], pH[:].rearrange("p (k i) -> p k i", i=P), HT[0][:].bitcast(F32),
                                  ALU.subtract).then_inc(h_lo, 1)

            def x_part(n, slot):
                wait_item(dve, x_hi, n)
                dve.tensor_tensor(XT[1][:, slot % 2], pX[:].rearrange("p (k i) -> p k i", i=P),
                                  XT[0][:, slot % 2].bitcast(F32), ALU.subtract).then_inc(x_lo, 1)

            def add_y(n, slot):
                wait_item(dve, down_done, n, per=NC)
                dve.scalar_tensor_tensor(out=X[:, slot], in0=pY[slot % 2][:], scalar=shared["gates"][:, 2:3],
                                         in1=X[:, slot], op0=ALU.mult, op1=ALU.add).then_inc(y_added, 1)

            stages = []
            for c in range(NC):
                stages.append(per_chunk(1, hidden, c - 1) if c else per_chunk(2, hidden, NC - 1))
                stages.append(per_chunk(2, h_part, c + 1) if c + 1 < NC else per_chunk(1, h_part, 0))
                if c == 0:
                    stages.append((0, norm_stats))
                if c == 2:
                    stages.append((0, norm_quantise))
            stages.append((2, add_y))
            stages.append((0, x_part))
            run_pipeline(dve.Fori, NT, U, 2, stages)

        @block.gpsimd
        def _(pool):
            def rstd_of(n, slot):
                wait_item(pool, mv_ready, n)
                own_wait(pool, shared["passed_pool"])
                pool.tensor_scalar(veps[:], mv[:, 1:2], LN_EPS, None, ALU.add).then_inc(veps_ready, 1)
                wait_item(pool, veps_ready, n)
                pool.tensor_tensor(rstd[:], veps[:], shared["minus_half"][:, 0:1], ALU.pow).then_inc(rstd_ready, 1)

            def back(front, sub, deq, i, V_, scale):
                Vb = V_.rearrange("p (k i) -> p k i", i=BLOCK)
                pool.wait_ge(front, i + 1)
                pool.tensor_tensor(V_, V_, M[:], ALU.subtract).then_inc(sub, 1)
                pool.wait_ge(sub, i + 1)
                pool.tensor_tensor(Vb, Vb, scale.unsqueeze(2).to_broadcast([P, 512 // BLOCK, BLOCK]),
                                   ALU.mult).then_inc(deq, 1)

            def x_back(n, slot):
                back(x_front, x_sub, x_deq, n, XV[:], xscale[:])

            def h_back(n, slot, c):
                back(h_front, h_sub, h_deq, n * NC + c, V[:, c % 2], hscale[:, c % 2])

            stages = []
            for c in range(NC):
                stages.append(per_chunk(1, h_back, c - 1) if c else per_chunk(2, h_back, NC - 1))
                if c == 0:
                    stages.append((0, rstd_of))
                if c == 2:
                    stages.append((0, x_back))
            run_pipeline(pool.Fori, NT, U, 2, stages)


def first_parts(nc, io, shared):
    F, D = io["down_w_shape"][1], io["down_w_shape"][0]
    B = io["x"].shape[0]
    GU_TILES, D_TILES = 2 * F * D // (P * 512), F * D // (P * 512)
    NS, PER_BATCH = 512 // BLOCK, (GU_TILES + D_TILES) // B
    GUT, KB, FC = GU_TILES // B, 512 // P, F // 512
    with ExitStack() as weights, ExitStack() as down_values:
        far, near = Memory(nc, down_values), Memory(nc, weights)
        shared["w_scales"] = far.sbuf("w_scales", [P, B * PER_BATCH * NS], side="right")
        shared["down_q"] = far.sbuf("down_e4m3", [P, D_TILES, 512], F16, side="right")
        with ExitStack() as gate_up_values:
            shared["gate_up_q"] = Memory(nc, gate_up_values).sbuf("gate_up_e4m3", [P, GU_TILES, 512], F16, side="right")
            attend(nc, io, shared)
            Gp = [near.sbuf(f"gate_upT_{s}", [P, D // P, 2 * F], F32R) for s in ("hi", "lo")]
            mx_weights(nc, shared, "gate_up", shared["gate_up_q"],
                       lambda n, slot: (n - slot % GUT) * (PER_BATCH * NS // GUT) + slot % GUT * NS,
                       lambda part, n, slot: Gp[part][:, :, bass.ds(n * P, P)])
        Dp = [near.sbuf(f"downT_{s}", [P, F // P, D], F32R) for s in ("hi", "lo")]
        mx_weights(nc, shared, "down", shared["down_q"],
                   lambda n, slot: n * (PER_BATCH * NS) + GUT * NS,
                   lambda part, n, slot: Dp[part][:, slot % FC * KB:(slot % FC + 1) * KB,
                                                  bass.ds((n - slot % FC) * (P // FC), P)])
        down_values.close()
        mx_ffn(nc, io, shared, (Gp, Dp))


def fp4_ffn(nc, io, shared, Wp, out):
    B = shared["summary"].shape[0]
    T, D = shared["x2"].shape
    F = io["fp4_inner"]
    DB, FB = D // P, F // P
    GT = 512 // P
    NG = T // (GT * P)
    GB = B // NG
    U = 2
    USES = FB + 2
    BLOCK_COLS = 2 * DB * P + D
    CH = 512
    BCH = BLOCK_COLS // CH
    AHEAD = 3
    EXP5_UP = 2.0 ** 14
    with ExitStack() as ctx:
        m = Memory(nc, ctx)
        words = m.sbuf("fp4_bytes", [P, 2, BLOCK_COLS // 4], I32)
        mid = m.sbuf("fp4_magnitudes", [P, BLOCK_COLS // 4], I32)
        scales = m.sbuf("fp4_scales_bc", [P, 2, CH], F16)
        value = m.sbuf("fp4_values", [P, 2, CH])
        shift = m.sbuf("nibble_shifts_sb", [P, 1], I32)
        X = m.sbuf("x_groups", [P, U, GT, D])
        Z = m.sbuf("z_group", [P, GT, D])
        summ = m.sbuf("summary_bc", [P, GB, D])
        gamma, beta = m.sbuf("gamma_bc", [P, D]), m.sbuf("beta_bc", [P, D])
        XT = [m.sbuf(f"x3T_{s}", [P, U, DB, GT * P], F32R) for s in ("hi", "lo")]
        H = m.sbuf("h3", [P, 2, GT * P])
        HT = [m.sbuf(f"h3_{s}", [P, 2, GT * P], F32R) for s in ("hi", "lo")]
        stats, mv = m.sbuf("ln_stats3", [P, GT, 6]), m.sbuf("mean_var3", [P, GT, 2])
        veps, rstd = m.sbuf("var_eps3", [P, GT]), m.sbuf("rstd3", [P, GT])
        sums = m.sbuf("y_square_sums", [P, GT])
        meps, rrms, grms = m.sbuf("mean_square_eps", [P, GT]), m.sbuf("rms_inverse", [P, GT]), m.sbuf("gated_rms", [P, GT])
        pG = [m.psum(f"p3G{i}") for i in range(2)]
        pU = [m.psum(f"p3U{i}") for i in range(2)]
        pY = [m.psum(f"p3Y{i}") for i in range(GT)]

        shift_loaded = m.sem("shift_loaded")
        words_loaded, scales_loaded = m.sems("words_loaded", 2), m.sems("scales_loaded", 2)
        nibble_ready, mid_ready, e5_ready, value_ready = (m.sem(n) for n in ("nibble_ready", "mid_ready", "e5_ready", "value_ready"))
        whi_ready, wlo_ready = m.sem("w3_hi_ready"), m.sem("w3_lo_ready")
        consts_loaded = m.sem("consts3_loaded")
        x_loaded, stored = m.sems("x3_loaded", U), m.sems("x3_stored", U)
        s_loaded = m.sem("s_loaded")
        affine_ready = m.sem("affine_ready")
        stats_ready, mv_ready, veps_ready, rstd_ready = (m.sem(n + "3") for n in ("stats_r", "mv_r", "veps_r", "rstd_r"))
        normed, summed, scaled, shifted, mixed = (m.sem(n + "3") for n in ("normed", "summed", "scaled", "shifted", "mixed"))
        x_turned, x_hi, x_lo = m.sem("x3_turned"), m.sem("x3_hi"), m.sem("x3_lo")
        gu_ready, silu_ready, h_ready = m.sem("gu3_ready"), m.sem("silu3_ready"), m.sem("h3_ready")
        h_hi, h_lo, down_done = m.sem("h3_hi"), m.sem("h3_lo"), m.sem("down3_done")
        squared, meps_ready, rrms_ready, grms_ready = (m.sem(n) for n in ("squared", "meps_r", "rrms_r", "grms_r"))
        y_added = m.sem("y3_added")
        block = ctx.enter_context(nc.Block())
        gates, minus_half = shared["gates"], shared["minus_half"]

        x_in = shared["x2"].rearrange("(g t p) d -> g p t d", p=P, t=GT)
        x_out = out.rearrange("b (t p) d -> (b t) p d", p=P).rearrange("(g t) p d -> g p t d", t=GT)

        def gate_w(part, g, b, up):
            at = b * BLOCK_COLS + (up * DB + g) * P
            return Wp[part][:, at:at + P]

        def down_w(part, b):
            return Wp[part][:, (b + 1) * BLOCK_COLS - D:(b + 1) * BLOCK_COLS]

        def first_group(body, b):
            def stage(n, slot):
                if isinstance(n, int) and n == 0 and b < FB:
                    for i in range(b * BCH, (b + 1) * BCH):
                        body(i)
            return stage

        @block.sync
        def _(sp):
            def load(n, slot):
                sp.dma_start(X[:, slot], x_in[n]).then_inc(x_loaded[slot], 16)

            def load_summary(n):
                wait_item(sp, summed, n, back=1)
                for b in range(GB):
                    sp.dma_start(summ[:, b], shared["summary"][bass.ds(n * GB + b, 1), :].to_broadcast([P, D]))\
                        .then_inc(s_loaded, 16)

            def load_words(b):
                if b >= 2:
                    wait_item(sp, value_ready, b - 2, per=BCH)
                sp.dma_start(words[:, b % 2], io["fp4_packed"][:, b * (BLOCK_COLS // 4):(b + 1) * (BLOCK_COLS // 4)])\
                    .then_inc(words_loaded[b % 2], 16)

            def load_scales(i):
                if i >= 2:
                    wait_item(sp, value_ready, i - 2)
                sp.dma_start(scales[:, i % 2], io["fp4_scales"][0:1, i * CH:(i + 1) * CH].to_broadcast([P, CH]))\
                    .then_inc(scales_loaded[i % 2], 16)

            def store(n, slot):
                wait_item(sp, y_added, n, per=GT)
                sp.dma_start(x_out[n], X[:, slot]).then_inc(stored[slot], 16)

            sp.dma_start(gamma[:], io["gamma"].rearrange("(a n) -> a n", a=1).to_broadcast([P, D])).then_inc(consts_loaded, 16)
            sp.dma_start(beta[:], io["beta"].rearrange("(a n) -> a n", a=1).to_broadcast([P, D])).then_inc(consts_loaded, 16)
            sp.dma_start(shift[:], io["nibble_shift"]).then_inc(shift_loaded, 16)
            load(0, 0)
            load_words(0)
            load_summary(0)
            for b in range(FB):
                for i in range(b * BCH, (b + 1) * BCH):
                    load_scales(i)
                    if i == b * BCH and b + 1 < FB:
                        load_words(b + 1)
                if b == AHEAD:
                    load(1, 1)
                    load_summary(1)
            with sp.Fori(0, NG - 2 * U + 1, U) as base:
                for j in range(U):
                    load_summary(base + (j + 2))
                    store(base + j, j)
                    wait_slot(sp, stored[j], base + j, j, U)
                    load(base + (j + U), j)
            for j in range(U):
                store(NG - U + j, j)
            for j in range(U):
                wait_slot(sp, stored[j], NG - U + j, j, U)

        @block.vector
        def _(dve):
            dve.wait_ge(shift_loaded, 16)

            def codes(b):
                w = words[:, b % 2]
                wait_slot(dve, words_loaded[b % 2], b, b, 2)
                dve.tensor_scalar(w, w, shift[:, 0:1], signed(0xF0F0F0F0), ALU.logical_shift_left,
                                  ALU.bitwise_and).then_inc(nibble_ready, 1)
                wait_item(dve, nibble_ready, b)
                wait_item(dve, e5_ready, b, back=1)
                dve.tensor_scalar(mid[:], w, 3, 0x0E0E0E0E, ALU.logical_shift_right,
                                  ALU.bitwise_and).then_inc(mid_ready, 1)
                wait_item(dve, mid_ready, b)
                dve.scalar_tensor_tensor(out=w, in0=w, scalar=signed(0x80808080), in1=mid[:],
                                         op0=ALU.bitwise_and, op1=ALU.bitwise_or).then_inc(e5_ready, 1)

            def weights(i):
                b, c = i // BCH, i % BCH
                if c == 0:
                    codes(b)
                wait_slot(dve, scales_loaded[i % 2], i, i, 2)
                wait_item(dve, wlo_ready, i, back=2)
                wait_item(dve, e5_ready, b)
                dve.scalar_tensor_tensor(out=value[:, i % 2], in0=words[:, b % 2].bitcast(F8E5)[:, c * CH:(c + 1) * CH],
                                         scalar=EXP5_UP, in1=scales[:, i % 2], op0=ALU.mult,
                                         op1=ALU.mult).then_inc(value_ready, 1)

            dve.wait_ge(consts_loaded, 32)
            dve.tensor_scalar(gamma[:], gamma[:], gates[:, 1:2], None, ALU.mult).then_inc(affine_ready, 1)
            dve.tensor_scalar(beta[:], beta[:], gates[:, 1:2], None, ALU.mult).then_inc(affine_ready, 1)
            dve.wait_ge(affine_ready, 2)

            def statistics(src, n, k):
                wait_item(dve, normed, n, per=3, of=k - 1) if k else wait_item(dve, normed, n, back=1, per=3)
                for t in range(GT):
                    ins = dve.bn_stats(stats[:, t], src[:, t])
                ins.then_inc(stats_ready, 1)
                wait_item(dve, stats_ready, n, per=3, of=k)
                own_wait(dve, shared["passed_dve"])
                for t in range(GT):
                    ins = dve.bn_aggr(mv[:, t], stats[:, t])
                ins.then_inc(mv_ready, 1)

            def normalise(dst, src, n, k):
                wait_item(dve, rstd_ready, n, per=3, of=k)
                for t in range(GT):
                    ins = dve.tensor_scalar(dst[:, t], src[:, t], mv[:, t, 0:1], rstd[:, t:t + 1], ALU.subtract, ALU.mult)
                ins.then_inc(normed, 1)

            def mix_1(n, slot):
                wait_slot(dve, x_loaded[slot], n, slot, U)
                statistics(X[:, slot], n, 0)

            def mix_2(n, slot):
                wait_item(dve, x_turned, n, back=1, per=GT)
                normalise(Z, X[:, slot], n, 0)

            def mix_3(n, slot):
                wait_item(dve, summed, n)
                statistics(Z, n, 1)

            def mix_4(n, slot):
                normalise(Z, Z, n, 1)

            def mix_5(n, slot):
                wait_item(dve, scaled, n)
                dve.tensor_tensor(Z[:], Z[:], beta[:].unsqueeze(1).to_broadcast([P, GT, D]), ALU.add).then_inc(shifted, 1)
                wait_item(dve, shifted, n)
                dve.tensor_tensor(X[:, slot], X[:, slot], Z[:], ALU.add).then_inc(mixed, 1)
                wait_item(dve, mixed, n)
                statistics(X[:, slot], n, 2)

            def mix_6(n, slot):
                normalise(Z, X[:, slot], n, 2)

            def x_part(n, slot):
                for t in range(GT):
                    wait_item(dve, x_hi, n, per=GT, of=t)
                    use = (slot - 1) % U * USES + FB + t // 2
                    bank = (pG, pU)[t % 2][use % 2]
                    dve.tensor_tensor(XT[1][:, slot, :, t * P:(t + 1) * P], bank[:].rearrange("p (k i) -> p k i", i=P),
                                      XT[0][:, slot, :, t * P:(t + 1) * P].bitcast(F32), ALU.subtract).then_inc(x_lo, 1)

            def hidden(n, slot, b):
                use = slot * USES + b
                h = b % 2
                wait_item(dve, silu_ready, n, per=FB, of=b)
                dve.tensor_tensor(H[:, h], H[:, h], pU[use % 2][:], ALU.mult).then_inc(h_ready, 1)
                wait_item(dve, h_hi, n, per=FB, of=b)
                dve.tensor_tensor(HT[1][:, h], H[:, h], HT[0][:, h].bitcast(F32), ALU.subtract).then_inc(h_lo, 1)

            def add_y(n, slot):
                wait_item(dve, rrms_ready, n)
                dve.tensor_scalar(grms[:], rrms[:], gates[:, 3:4], None, ALU.mult).then_inc(grms_ready, 1)
                wait_item(dve, grms_ready, n)
                for t in range(GT):
                    dve.scalar_tensor_tensor(out=X[:, slot, t], in0=pY[t][:], scalar=grms[:, t:t + 1], in1=X[:, slot, t],
                                             op0=ALU.mult, op1=ALU.add).then_inc(y_added, 1)

            between = {1: mix_1, 2: mix_2, 4: mix_3, 5: mix_4, 7: mix_5, 8: mix_6}
            early = {2: 0, 5: 1, 8: 2}
            stages = []
            for b in range(FB):
                stages.append((1, first_group(weights, b + AHEAD)))
                stages.append((1, lambda n, slot, b=b: hidden(n, slot, b)))
                if b in between:
                    stages.append((0, between[b]))
                if b in early:
                    stages.append((0, first_group(weights, early[b])))
            run_pipeline(dve.Fori, NG, U, 2, stages + [(0, x_part), (1, add_y)])

        @block.gpsimd
        def _(pool):
            pool.wait_ge(affine_ready, 2)

            def rstd_of(n, slot, k):
                wait_item(pool, mv_ready, n, per=3, of=k)
                own_wait(pool, shared["passed_pool"])
                pool.tensor_scalar(veps[:], mv[:, :, 1], LN_EPS, None, ALU.add).then_inc(veps_ready, 1)
                wait_item(pool, veps_ready, n, per=3, of=k)
                pool.tensor_tensor(rstd[:], veps[:], minus_half[:], ALU.pow).then_inc(rstd_ready, 1)

            def rstd_1(n, slot):
                rstd_of(n, slot, 0)

            def add_summary(n, slot):
                wait_item(pool, normed, n, per=3, of=0)
                pool.wait_ge(s_loaded, n * (16 * GB) + 16 * GB)
                Zb = Z[:].rearrange("p (b t) d -> p b t d", b=GB)
                for b in range(GB):
                    ins = pool.tensor_tensor(Zb[:, b], Zb[:, b],
                                             summ[:, b].unsqueeze(1).to_broadcast([P, GT // GB, D]), ALU.add)
                ins.then_inc(summed, 1)

            def rstd_2(n, slot):
                rstd_of(n, slot, 1)

            def times_gamma(n, slot):
                wait_item(pool, normed, n, per=3, of=1)
                pool.tensor_tensor(Z[:], Z[:], gamma[:].unsqueeze(1).to_broadcast([P, GT, D]), ALU.mult).then_inc(scaled, 1)

            def rstd_3(n, slot):
                rstd_of(n, slot, 2)

            def rms(n, slot):
                wait_item(pool, squared, n, per=GT)
                own_wait(pool, shared["passed_pool"])
                pool.tensor_scalar(meps[:], sums[:], 1.0 / D, RMS_EPS, ALU.mult, ALU.add).then_inc(meps_ready, 1)
                wait_item(pool, meps_ready, n)
                pool.tensor_tensor(rrms[:], meps[:], minus_half[:], ALU.pow).then_inc(rrms_ready, 1)

            def w_lo(i):
                wait_item(pool, whi_ready, i)
                pool.tensor_tensor(Wp[1][:, i * CH:(i + 1) * CH], value[:, i % 2], Wp[0][:, i * CH:(i + 1) * CH].bitcast(F32),
                                   ALU.subtract).then_inc(wlo_ready, 1)

            between = {1: rstd_1, 2: add_summary, 4: rstd_2, 5: times_gamma, 7: rstd_3}
            early = {2: 0, 5: 1, 8: 2}
            stages = []
            for b in range(FB):
                stages.append((1, first_group(w_lo, b + AHEAD)))
                if b in between:
                    stages.append((0, between[b]))
                if b in early:
                    stages.append((0, first_group(w_lo, early[b])))
            run_pipeline(pool.Fori, NG, U, 2, stages + [(1, rms)])

        @block.scalar
        def _(act):
            def silu(n, slot, b):
                use = slot * USES + b
                h = b % 2
                wait_item(act, gu_ready, n, per=FB, of=b)
                if b >= 2:
                    wait_item(act, h_lo, n, per=FB, of=b - 2)
                else:
                    wait_item(act, h_lo, n, back=1, per=FB)
                    wait_item(act, squared, n, back=1, per=GT)
                act.activation(H[:, h], pG[use % 2][:], ACT.Silu).then_inc(silu_ready, 1)
                wait_item(act, h_ready, n, per=FB, of=b)
                if b >= 2:
                    wait_item(act, down_done, n, per=FB, of=b - 2)
                else:
                    wait_item(act, down_done, n, back=1, per=FB)
                act.activation(HT[0][:, h], H[:, h], ACT.Copy).then_inc(h_hi, 1)

            def x_part(n, slot):
                for t in range(GT):
                    use = (slot - 1) % U * USES + FB + t // 2
                    bank = (pG, pU)[t % 2][use % 2]
                    wait_item(act, x_turned, n, per=GT, of=t)
                    act.activation(XT[0][:, slot, :, t * P:(t + 1) * P], bank[:].rearrange("p (k i) -> p k i", i=P),
                                   ACT.Copy).then_inc(x_hi, 1)

            def squares_of(n, slot):
                wait_item(act, down_done, n, per=FB)
                wait_item(act, meps_ready, n, back=1)
                for t in range(GT):
                    if t >= 2:
                        wait_item(act, squared, n, per=GT, of=t - 2)
                    act.activation(H[:, t % 2], pY[t][:], ACT.Square, accum_out=sums[:, t:t + 1]).then_inc(squared, 1)

            def w_hi(i):
                wait_item(act, value_ready, i)
                act.activation(Wp[0][:, i * CH:(i + 1) * CH], value[:, i % 2], ACT.Copy).then_inc(whi_ready, 1)

            stages = [(0, first_group(w_hi, b)) for b in range(AHEAD)]
            for b in range(FB):
                stages.append((1, first_group(w_hi, b + AHEAD)))
                stages.append((1, lambda n, slot, b=b: silu(n, slot, b)))
            run_pipeline(act.Fori, NG, U, 2, stages + [(0, x_part), (1, squares_of)])

        @block.tensor
        def _(pe):
            def gate_up(n, slot, b):
                use = slot * USES + b
                if b == 0:
                    wait_item(pe, x_hi, n, per=GT)
                    wait_item(pe, x_lo, n, per=GT)
                if isinstance(n, int) and n == 0:
                    wait_item(pe, whi_ready, b, per=BCH)
                    wait_item(pe, wlo_ready, b, per=BCH)
                if b >= 2:
                    wait_item(pe, h_ready, n, per=FB, of=b - 2)
                for bank, up in ((pG[use % 2], 0), (pU[use % 2], 1)):
                    for g in range(DB):
                        mm = split_matmul(pe, bank[:], [gate_w(s, g, b, up) for s in (0, 1)],
                                          [x[:, slot, g] for x in XT], g == 0, g == DB - 1)
                mm.then_inc(gu_ready, 1)

            def down(n, slot, b):
                wait_item(pe, h_hi, n, per=FB, of=b)
                wait_item(pe, h_lo, n, per=FB, of=b)
                for t in range(GT):
                    if b == 0:
                        wait_item(pe, y_added, n, back=1, per=GT, of=t)
                    mm = split_matmul(pe, pY[t][:], [h[:, b % 2, t * P:(t + 1) * P] for h in HT],
                                      [down_w(s, b) for s in (0, 1)], b == 0, b == FB - 1)
                mm.then_inc(down_done, 1)

            def turn(n, slot):
                wait_item(pe, normed, n, per=3)
                for t in range(GT):
                    use = (slot - 1) % U * USES + FB + t // 2
                    bank = (pG, pU)[t % 2][use % 2]
                    if t % 2 == 0:
                        wait_item(pe, h_ready, n, back=1, per=FB, of=FB - 2 + t // 2)
                    for g in range(DB):
                        mm = pe.transpose(bank[:, g * P:(g + 1) * P], Z[:, t, g * P:(g + 1) * P], shared["ident"][:])
                    mm.then_inc(x_turned, 1)

            stages = []
            for b in range(FB):
                stages.append((1, lambda n, slot, b=b: gate_up(n, slot, b)))
                if b:
                    stages.append((1, lambda n, slot, b=b: down(n, slot, b - 1)))
            stages.append((0, turn))
            stages.append((1, lambda n, slot: down(n, slot, FB - 1)))
            run_pipeline(pe.Fori, NG, U, 2, stages)


def fp4_layer(nc, io, shared, out):
    D, F = shared["x2"].shape[1], io["fp4_inner"]
    with ExitStack() as ctx:
        m = Memory(nc, ctx)
        Wp = [m.sbuf(f"fp4_w_{s}", [P, (D // P) * 2 * F + (F // P) * D], F32R) for s in ("hi", "lo")]
        fp4_ffn(nc, io, shared, Wp, out)


def build(nc, io, out, debug=None):
    B, S, D = io["x"].shape
    T = B * S
    with ExitStack() as ctx:
        m = Memory(nc, ctx)
        shared = {
            "gates": m.sbuf("tanh_gates", [P, 4]), "ident": m.sbuf("identity", [P, P]),
            "minus_half": m.sbuf("minus_half", [P, 4]),
            **{f"passed_{e}": m.sem(f"passed_{e}") for e in ("sp", "dve", "pool")},
            "x1": nc.dram_tensor("x_after_attention", [T, D], F32, kind="Internal").ap(),
            "x2": nc.dram_tensor("x_after_mx_ffn", [T, D], F32, kind="Internal").ap(),
            "summary": nc.dram_tensor("summary", [B, D], F32, kind="Internal").ap(),
        }
        first_parts(nc, io, shared)
        fp4_layer(nc, io, shared, out)


def kernel(**inputs):
    import concourse.bacc as bacc
    import numpy as np
    from concourse.bass_utils import run_bass_kernel_spmd

    a = {name: np.asarray(value) for name, value in inputs.items()}
    D = a["x"].shape[-1]
    F4 = a["L1_ffn_down_packed"].shape[1] * 8
    def by_feature(packed):
        return np.repeat(np.ascontiguousarray(packed).view(np.uint8).T, 2, axis=0)

    gate_up = by_feature(a["L1_ffn_gate_up_packed"]).reshape(D // P, P, 2, F4 // P, P).transpose(1, 3, 2, 0, 4)
    down = by_feature(a["L1_ffn_down_packed"]).reshape(F4 // P, P, D).transpose(1, 0, 2)
    nibbles = np.concatenate([gate_up.reshape(P, F4 // P, -1), down], axis=2).reshape(P, -1)
    gate_up_scales = a["L1_ffn_gate_up_scales"].reshape(D // P, 2, F4 // P, P).transpose(2, 1, 0, 3)
    scales = np.concatenate([gate_up_scales.reshape(F4 // P, -1), a["L1_ffn_down_scales"]], axis=1).reshape(1, -1)
    arrays = {
        "x": a["x"], "ctx": a["ctx_2048"], "ctxT": a["ctx_2048"].transpose(0, 2, 1),
        "g_xattn": a["g_xattn"], "g_ffn": a["g_ffn"],
        "gate_up_w": np.concatenate([a["L0_ffn_gate_w"], a["L0_ffn_up_w"]]), 
        "down_tiles": a["L0_ffn_down_w"].reshape(D // P, P, -1, 512).transpose(0, 2, 1, 3).reshape(-1, 512),
        "decay": a["L1_xattn_decay"].reshape(1, 1), "W_inT": a["L1_xattn_W_in"].T, "W_outT": a["L1_xattn_W_out"].T,
        "b_in": a["L1_xattn_b_in"].reshape(D // P, P).T, "b_out": a["L1_xattn_b_out"],
        "gamma": a["L1_xattn_gamma"], "beta": a["L1_xattn_beta"],
        "fp4_packed": np.ascontiguousarray(nibbles).view(np.int32), "fp4_scales": scales,
        "nibble_shift": (4 - 4 * (np.arange(P, dtype=np.int32) % 2)).reshape(P, 1),
    }
    arrays = {f"in_{name}": np.ascontiguousarray(value) for name, value in arrays.items()}
    nc = bacc.Bacc("TRN2", target_bir_lowering=False, num_devices=1, dynamic_dma_scratch_size=1024)
    io = {name[3:]: nc.dram_tensor(name, value.shape, mybir.dt.from_np(value.dtype), kind="ExternalInput").ap()
          for name, value in arrays.items()}
    io["fp4_inner"] = F4
    io["down_w_shape"] = a["L0_ffn_down_w"].shape
    out = nc.dram_tensor("out", a["x"].shape, F32, kind="ExternalOutput").ap()
    build(nc, io, out)
    return run_bass_kernel_spmd(nc, [arrays], core_ids=[0]).results[0]["out"]
```

```python
from contextlib import ExitStack

import concourse.bass as bass
from concourse import mybir
from concourse.alu_op_type import AluOpType as ALU

F32 = mybir.dt.float32
F32R = mybir.dt.float32r
F16 = mybir.dt.float16
F8E5 = mybir.dt.float8e5
I32 = mybir.dt.int32
ACT = mybir.ActivationFunctionType
AX = mybir.AxisListType

P = 128
LN_EPS = 1e-5
RMS_EPS = 1e-6
W_STEPS = 5
BLOCK = 32
FP8_MAX = 448.0
SCALE_MIN = 1e-30
EXPONENT = 0x7F800000
HALF_BIT = 0x00400000
HIHI_HILO_LOHI = ((0, 0), (0, 1), (1, 0))


def run_pipeline(loop, n_items, unroll, peel, stages):
    most = max(lag for lag, _ in stages)
    start = most + peel
    rounds = max(0, n_items - start) // unroll

    def tick(t, base):
        for lag, body in stages:
            if base is not None:
                body(base + (t - lag), (t - lag) % unroll)
            elif 0 <= t - lag < n_items:
                body(t - lag, (t - lag) % unroll)

    for t in range(start):
        tick(t, None)
    if rounds:
        with loop(0, (rounds - 1) * unroll + 1, unroll) as base:
            for t in range(start, start + unroll):
                tick(t, base)
    for t in range(start + rounds * unroll, n_items + most):
        tick(t, None)


def wait_item(eng, sem, n, back=0, per=1, of=None):
    if isinstance(n, int) and n < back:
        return
    eng.wait_ge(sem, (n - back) * per + (per if of is None else of + 1))


def signed(bits):
    return bits - (bits >> 31 << 32)


def wait_slot(eng, sem, n, slot, slots, dmas=1):
    eng.wait_ge(sem, (n - slot % slots) * (16 * dmas // slots) + 16 * dmas)


def own_wait(eng, passed):
    eng.sem_inc(passed, 1)


class Memory:

    def __init__(self, nc, ctx):
        self.nc, self.ctx = nc, ctx

    def sbuf(self, name, shape, dtype=F32, side=None):
        return self.ctx.enter_context(self.nc.sbuf_tensor(name, shape, dtype, side=side))

    def psum(self, name, shape=(P, 512)):
        return self.ctx.enter_context(self.nc.psum_tensor(name, list(shape), F32))

    def sem(self, name):
        return self.ctx.enter_context(self.nc.semaphore(name))

    def sems(self, name, n):
        return [self.sem(f"{name}{i}") for i in range(n)]


def split_matmul(pe, out, stationary, moving, first, last):
    for n, (a, b) in enumerate(HIHI_HILO_LOHI):
        mm = pe.matmul(out, stationary[a], moving[b], start=first and n == 0, stop=last and n == 2)
    return mm


def attend(nc, io, shared):
    B, S, D = io["x"].shape
    ST, DB = S // P, D // P
    U = 4
    Qgu, Qdn, w_scales = shared["gate_up_q"], shared["down_q"], shared["w_scales"]
    GUT = Qgu.shape[1] // B
    WT = GUT + Qdn.shape[1] // B
    WB = WT * 512 // BLOCK
    with ExitStack() as ctx:
        m = Memory(nc, ctx)
        X = m.sbuf("x_tiles", [P, U, ST, D])
        C = m.sbuf("ctx_tiles", [P, 2, ST, D])
        CT = m.sbuf("ctx_transposed", [P, 2, DB, S])
        Q = m.sbuf("q", [P, 2, ST, D])
        Qp = [m.sbuf(f"q_{s}", [P, 2, ST, D], F32R) for s in ("hi", "lo")]
        Kp = [m.sbuf(f"k_{s}", [P, 2, ST, D], F32R) for s in ("hi", "lo")]
        Vp = [m.sbuf(f"vT_{s}", [P, 2, DB, S], F32R) for s in ("hi", "lo")]
        E = m.sbuf("exps", [P, 2, D])
        Ep = [m.sbuf(f"exp_{s}", [P, 2, DB, D], F32R) for s in ("hi", "lo")]
        L = m.sbuf("w_tiles", [P, 2, WT, 512])
        M = [shared["w_work"][:, 0:WT], m.sbuf("w_rounders", [P, WT, 512])[:]]
        w_rinv = m.sbuf("w_scale_inverses", [P, WB])
        stats = m.sbuf("ln_stats", [P, 2, ST, 6])
        mv = m.sbuf("mean_var", [P, 2, ST, 2])
        minus_mean = m.sbuf("minus_mean", [P, 2, ST])
        veps = m.sbuf("var_eps", [P, 2, ST])
        rstd = m.sbuf("rstd", [P, 2, ST])
        nmax = m.sbuf("neg_max", [P, 2, DB])
        zsum = m.sbuf("exp_sum", [P, 2, DB])
        rz = m.sbuf("exp_sum_inverse", [P, 2, DB])
        ones = m.sbuf("ones", [P, P])
        keep = m.sbuf("keep", [1, 2])
        row = m.sbuf("decay_row", [1, S])
        wcol = m.sbuf("state_weights", [P, ST])
        WinT = m.sbuf("W_inT_sb", [P, DB, D])
        WoutT = m.sbuf("W_outT_sb", [P, DB, D])
        bin_ = m.sbuf("b_in_columns", [P, DB])
        bout = m.sbuf("b_out_row", [1, D])
        bw = m.sbuf("b_in_weighted", [P, DB])
        sumw = m.sbuf("state_weight_sum", [P, 1])
        cw = m.sbuf("ctx_weighted", [P, DB, B])
        states = m.sbuf("mean_states", [P, DB, B])
        summ = Q[0:B, 0, 0]
        pS = [m.psum(f"pScores{i}") for i in range(DB)]
        pO = [m.psum(f"pOut{i}") for i in range(ST)]
        pC = m.psum("pCtxWeighted")
        pW = m.psum("pSmall")

        consts_loaded = m.sem("consts_loaded")
        x_loaded, x_stored = m.sems("x_loaded", U), m.sems("x_stored", U)
        c_loaded = m.sems("c_loaded", 2)
        projections_loaded, summary_stored = m.sem("projections_loaded"), m.sem("summary_stored")
        gates_ready, keep_ready, row_ready = m.sem("gates_ready"), m.sem("keep_ready"), m.sem("row_ready")
        weights_psum, weights_ready = m.sem("weights_psum"), m.sem("weights_ready")
        stats_ready, mv_ready, veps_ready = m.sem("stats_ready"), m.sem("mv_ready"), m.sem("veps_ready")
        minus_mean_ready, centred = m.sem("minus_mean_ready"), m.sem("centred")
        rstd_ready, q_ready = m.sem("rstd_ready"), m.sem("q_ready")
        qhi_ready, qlo_ready = m.sem("qhi_ready"), m.sem("qlo_ready")
        khi_ready, klo_ready = m.sem("khi_ready"), m.sem("klo_ready")
        scores_ready, nmax_ready = m.sem("scores_ready"), m.sem("nmax_ready")
        exps_ready, ehi_ready, elo_ready = m.sem("exps_ready"), m.sem("ehi_ready"), m.sem("elo_ready")
        rz_ready, vhi_ready, v_ready = m.sem("rz_ready"), m.sem("vhi_ready"), m.sem("v_ready")
        out_ready, out_added = m.sem("out_ready"), m.sem("out_added")
        const_order = m.sem("const_order")
        w_loaded = m.sems("w_loaded", 2)
        w_order, w_front, w_rounded, w_quantised = (m.sem(n) for n in ("w_order", "w_front", "w_rounded", "w_quantised"))
        cw_ready, states_psum, states_ready = m.sem("cw_ready"), m.sem("states_psum"), m.sem("states_ready")
        summary_psum, summary_ready = m.sem("summary_psum"), m.sem("summary_ready")
        block = ctx.enter_context(nc.Block())

        x_in = io["x"].rearrange("b (t p) d -> b p t d", p=P)
        c_in = io["ctx"].rearrange("b (t p) d -> b p t d", p=P)
        ct_in = io["ctxT"].rearrange("b (e p) s -> b p e s", p=P)
        x_out = shared["x1"].rearrange("(b t p) d -> b p t d", p=P, t=ST)
        gu_in = io["gate_up_w"].rearrange("(b k p) d -> b p k d", p=P, k=GUT)
        dn_in = io["down_tiles"].rearrange("(b k p) d -> b p k d", p=P, k=WT - GUT)
        gates, ident = shared["gates"], shared["ident"]
        CONSTS = 3

        @block.sync
        def _(sp):
            def load_x(n, slot):
                sp.dma_start(X[:, slot], x_in[n]).then_inc(x_loaded[slot], 16)

            def load_ctx(n, slot):
                sp.dma_start(C[:, slot % 2], c_in[n]).then_inc(c_loaded[slot % 2], 16)
                sp.dma_start(CT[:, slot % 2], ct_in[n]).then_inc(c_loaded[slot % 2], 16)

            def const(dst, src, loaded=consts_loaded):
                sp.dma_start(dst, src).then_inc(loaded, 16)

            def next_ctx(n, slot):
                wait_item(sp, scores_ready, n, per=DB)
                own_wait(sp, shared["passed_sp"])
                wait_item(sp, v_ready, n)
                own_wait(sp, shared["passed_sp"])
                load_ctx(n + 2, slot)

            def load_w(n, slot):
                sp.dma_start(L[:, slot % 2, 0:GUT], gu_in[n]).then_inc(w_loaded[slot % 2], 16)
                sp.dma_start(L[:, slot % 2, GUT:WT], dn_in[n]).then_inc(w_loaded[slot % 2], 16)

            def next_w(n, slot):
                wait_item(sp, w_quantised, n)
                own_wait(sp, shared["passed_sp"])
                load_w(n + 2, slot)

            def store_x(n, slot):
                wait_item(sp, out_added, n, per=ST)
                sp.dma_start(x_out[n], X[:, slot]).then_inc(x_stored[slot], 16)

            def next_x(n, slot):
                wait_slot(sp, x_stored[slot], n, slot, U)
                load_x(n + U, slot)

            load_x(0, 0)
            const(keep[0:1, 0:1], io["decay"])
            load_ctx(0, 0)
            const(gates[:, 0:2], io["g_xattn"].rearrange("(a n) -> a n", a=1).to_broadcast([P, 2]))
            const(gates[:, 2:4], io["g_ffn"].rearrange("(a n) -> a n", a=1).to_broadcast([P, 2]))
            load_w(0, 0)
            load_x(1, 1)
            load_ctx(1, 1)
            load_w(1, 1)
            load_x(2, 2)
            load_x(3, 3)
            const(WinT[:], io["W_inT"].rearrange("(e p) n -> p e n", p=P), projections_loaded)
            const(WoutT[:], io["W_outT"].rearrange("(e p) n -> p e n", p=P), projections_loaded)
            const(bin_[:], io["b_in"], projections_loaded)
            const(bout[:], io["b_out"].rearrange("(a n) -> a n", a=1), projections_loaded)
            next_ctx(0, 0)
            next_w(0, 0)
            with sp.Fori(0, B - 2 * U + 1, U) as base:
                for j in range(U):
                    next_ctx(base + (j + 1), (j + 1) % U)
                    next_w(base + (j + 1), (j + 1) % U)
                    store_x(base + j, j)
                    next_x(base + j, j)
            for n in range(B - U, B):
                if n + 3 < B:
                    next_ctx(n + 1, (n + 1) % U)
                    next_w(n + 1, (n + 1) % U)
                store_x(n, n % U)
            for j in range(U):
                wait_slot(sp, x_stored[j], B - U + j, j, U)
            sp.wait_ge(summary_ready, 1)
            sp.dma_start(shared["summary"], summ).then_inc(summary_stored, 16)
            sp.wait_ge(summary_stored, 16)

        @block.gpsimd
        def _(pool):
            pool.memset(ident[:], 0.0).then_inc(const_order, 1)
            pool.memset(shared["minus_half"][:], -0.5).then_inc(const_order, 1)
            pool.memset(ones[:], 1.0).then_inc(const_order, 1)
            pool.wait_ge(const_order, 3)
            pool.affine_select(out=ident[:], in_=ident[:], compare_op=ALU.not_equal, fill=1.0,
                               base=0, pattern=[[-1, P]], channel_multiplier=1).then_inc(const_order, 1)

            def rstd_of(n, slot):
                h = slot % 2
                wait_item(pool, mv_ready, n, per=ST)
                wait_item(pool, q_ready, n, back=2, per=ST)
                own_wait(pool, shared["passed_pool"])
                pool.tensor_scalar(veps[:, h], mv[:, h, :, 1], LN_EPS, float(D), ALU.add, ALU.mult).then_inc(veps_ready, 1)
                wait_item(pool, veps_ready, n)
                pool.tensor_tensor(rstd[:, h], veps[:, h], shared["minus_half"][:, 0:ST],
                                   ALU.pow).then_inc(rstd_ready, 1)

            def k_lo(n, slot):
                h = slot % 2
                wait_item(pool, khi_ready, n)
                pool.tensor_tensor(Kp[1][:, h], C[:, h], Kp[0][:, h].bitcast(F32), ALU.subtract)\
                    .then_inc(klo_ready, 1)

            def e_lo(n, slot):
                h = slot % 2
                for e in range(DB):
                    wait_item(pool, ehi_ready, n, per=DB, of=e)
                    pool.tensor_tensor(Ep[1][:, h, e], E[:, e % 2], Ep[0][:, h, e].bitcast(F32),
                                       ALU.subtract).then_inc(elo_ready, 1)

            def w_values(n, slot):
                h = slot % 2
                wait_item(pool, w_front, n)
                pool.tensor_tensor(L[:, h], L[:, h], M[h], ALU.add).then_inc(w_rounded, 1)
                wait_item(pool, w_rounded, n)
                pool.tensor_tensor(Qgu[:, n * GUT:(n + 1) * GUT] if isinstance(n, int) else Qgu[:, bass.ds(n * GUT, GUT)],
                                   L[:, h, 0:GUT], M[h][:, 0:GUT], ALU.subtract)
                pool.tensor_tensor(Qdn[:, n:n + 1] if isinstance(n, int) else Qdn[:, bass.ds(n, 1)],
                                   L[:, h, GUT:WT], M[h][:, GUT:WT], ALU.subtract).then_inc(w_quantised, 1)

            run_pipeline(pool.Fori, B, U, 2, [(0, rstd_of), (0, k_lo), (1, e_lo), (1, w_values)])

        @block.scalar
        def _(act):
            act.wait_ge(consts_loaded, 16 * CONSTS)
            act.activation(gates[:], gates[:], ACT.Tanh).then_inc(gates_ready, 1)
            act.activation(keep[0:1, 1:2], keep[0:1, 0:1], ACT.Sigmoid).then_inc(keep_ready, 1)

            def k_hi(n, slot):
                h = slot % 2
                wait_slot(act, c_loaded[h], n, slot, 2, dmas=2)
                wait_item(act, scores_ready, n, back=2, per=DB)
                act.activation(Kp[0][:, h], C[:, h], ACT.Copy).then_inc(khi_ready, 1)

            def centre(n, slot):
                h = slot % 2
                wait_slot(act, x_loaded[slot], n, slot, U)
                wait_item(act, minus_mean_ready, n)
                wait_item(act, qlo_ready, n, back=2)
                for t in range(ST):
                    act.activation(Q[:, h, t], X[:, slot, t], ACT.Identity, bias=minus_mean[:, h, t:t + 1]).then_inc(centred, 1)

            def norm(n, slot):
                h = slot % 2
                wait_item(act, rstd_ready, n)
                wait_item(act, centred, n, per=ST)
                for t in range(ST):
                    act.activation(Q[:, h, t], Q[:, h, t], ACT.Copy, scale=rstd[:, h, t:t + 1]).then_inc(q_ready, 1)

            def q_hi(n, slot):
                h = slot % 2
                wait_item(act, q_ready, n, per=ST)
                wait_item(act, scores_ready, n, back=2, per=DB)
                act.activation(Qp[0][:, h], Q[:, h], ACT.Copy).then_inc(qhi_ready, 1)

            def exps(n, slot):
                h = slot % 2
                wait_item(act, out_ready, n, back=2, per=ST)
                for e in range(DB):
                    wait_item(act, nmax_ready, n, per=DB, of=e)
                    if e >= 2:
                        wait_item(act, elo_ready, n, per=DB, of=e - 2)
                    else:
                        wait_item(act, elo_ready, n, back=1, per=DB, of=e + DB - 2)
                    act.activation(E[:, e % 2], pS[e][:], ACT.Exp, bias=nmax[:, h, e:e + 1],
                                   accum_out=zsum[:, h, e:e + 1]).then_inc(exps_ready, 1)
                    wait_item(act, exps_ready, n, per=DB, of=e)
                    act.activation(Ep[0][:, h, e], E[:, e % 2], ACT.Copy).then_inc(ehi_ready, 1)

            def v_hi(n, slot):
                h = slot % 2
                wait_item(act, rz_ready, n)
                wait_item(act, out_ready, n, back=2, per=ST)
                for e in range(DB):
                    act.activation(Vp[0][:, h, e], CT[:, h, e], ACT.Copy, scale=rz[:, h, e:e + 1]).then_inc(vhi_ready, 1)

            run_pipeline(act.Fori, B, U, 2, [(0, k_hi), (0, centre), (1, exps), (0, norm), (1, v_hi), (0, q_hi)])

        @block.vector
        def _(dve):
            dve.wait_ge(keep_ready, 1)
            dve.wait_ge(const_order, 4)
            dve.tensor_tensor_scan(row[:, ::-1], keep[0:1, 1:2].to_broadcast([1, S]), ones[0:1, 0:1].to_broadcast([1, S]),
                                   0.0, ALU.mult, ALU.add).then_inc(row_ready, 1)
            dve.wait_ge(weights_psum, 1)
            dve.tensor_scalar(wcol[:], pW[:, 0:ST], 1.0 / S, None, ALU.mult).then_inc(weights_ready, 1)
            dve.wait_ge(gates_ready, 1)

            def norm_stats(n, slot):
                h = slot % 2
                wait_slot(dve, x_loaded[slot], n, slot, U)
                for t in range(ST):
                    dve.bn_stats(stats[:, h, t], X[:, slot, t]).then_inc(stats_ready, 1)
                wait_item(dve, rstd_ready, n, back=2)
                wait_item(dve, q_ready, n, back=2, per=ST)
                for t in range(ST):
                    wait_item(dve, stats_ready, n, per=ST, of=t)
                    own_wait(dve, shared["passed_dve"])
                    dve.bn_aggr(mv[:, h, t], stats[:, h, t]).then_inc(mv_ready, 1)
                wait_item(dve, mv_ready, n, per=ST)
                dve.tensor_scalar(minus_mean[:, h], mv[:, h, :, 0], -1.0, None, ALU.mult).then_inc(minus_mean_ready, 1)

            def q_lo(n, slot):
                h = slot % 2
                wait_item(dve, qhi_ready, n)
                dve.tensor_tensor(Qp[1][:, h], Q[:, h], Qp[0][:, h].bitcast(F32), ALU.subtract)\
                    .then_inc(qlo_ready, 1)

            def maxima(n, slot, e):
                wait_item(dve, scores_ready, n, per=DB, of=e)
                dve.tensor_reduce(nmax[:, slot % 2, e:e + 1], pS[e][:], AX.X, ALU.max, negate=True).then_inc(nmax_ready, 1)

            def inverse_sums(n, slot):
                wait_item(dve, exps_ready, n, per=DB)
                dve.reciprocal(rz[:, slot % 2], zsum[:, slot % 2]).then_inc(rz_ready, 1)

            def v_lo(n, slot):
                h = slot % 2
                wait_item(dve, out_ready, n, back=2, per=ST)
                for e in range(DB):
                    wait_item(dve, vhi_ready, n, per=DB, of=e)
                    last = dve.scalar_tensor_tensor(out=Vp[1][:, h, e], in0=CT[:, h, e], scalar=rz[:, h, e:e + 1],
                                                    in1=Vp[0][:, h, e].bitcast(F32), op0=ALU.mult, op1=ALU.subtract)
                last.then_inc(v_ready, 1)

            def add_out(n, slot):
                for t in range(ST):
                    wait_item(dve, out_ready, n, per=ST, of=t)
                    dve.scalar_tensor_tensor(out=X[:, slot, t], in0=pO[t][:], scalar=gates[:, 0:1],
                                             in1=X[:, slot, t], op0=ALU.mult, op1=ALU.add).then_inc(out_added, 1)

            def w_blocks(slot):
                return L[:, slot % 2].rearrange("p t (k i) -> p (t k) i", i=BLOCK)

            def scales_of(n):
                return w_scales[:, n * WB:(n + 1) * WB] if isinstance(n, int) else w_scales[:, bass.ds(n * WB, WB)]

            def w_step(n, of):
                wait_item(dve, w_order, n, per=W_STEPS, of=of)

            def w_max(n, slot):
                wait_slot(dve, w_loaded[slot % 2], n, slot, 2, dmas=2)
                dve.tensor_reduce(scales_of(n), w_blocks(slot), AX.X, ALU.max, apply_absolute_value=True).then_inc(w_order, 1)

            def w_scale(n, slot):
                w_step(n, 0)
                dve.tensor_scalar(scales_of(n), scales_of(n), 1.0 / FP8_MAX, SCALE_MIN, ALU.mult, ALU.max).then_inc(w_order, 1)

            def w_inverse(n, slot):
                w_step(n, 1)
                own_wait(dve, shared["passed_dve"])
                dve.reciprocal(w_rinv[:], scales_of(n)).then_inc(w_order, 1)

            def w_v(n, slot):
                w_step(n, 2)
                dve.tensor_tensor(w_blocks(slot), w_blocks(slot), w_rinv[:].unsqueeze(2).to_broadcast([P, WB, BLOCK]),
                                  ALU.mult).then_inc(w_order, 1)

            def w_exponent(n, slot):
                w_step(n, 3)
                dve.tensor_scalar(M[slot % 2].bitcast(I32), L[:, slot % 2].bitcast(I32), EXPONENT, HALF_BIT,
                                  ALU.bitwise_and, ALU.bitwise_or).then_inc(w_order, 1)

            def w_rounder(n, slot):
                w_step(n, 4)
                dve.tensor_scalar(M[slot % 2], M[slot % 2], 1.5 * 2.0 ** -6, 2.0 ** 20, ALU.max,
                                  ALU.mult).then_inc(w_front, 1)

            highest = [(1, lambda n, slot, e=e: maxima(n, slot, e)) for e in range(DB)]
            run_pipeline(dve.Fori, B, U, 2, [(0, norm_stats), *highest[:3], (0, w_max),
                                             *highest[3:], (0, w_scale), (0, w_inverse), (0, w_v), (1, inverse_sums),
                                             (0, w_exponent), (1, v_lo), (0, q_lo), (2, add_out), (0, w_rounder)])

            dve.wait_ge(cw_ready, 1)
            dve.tensor_copy(cw[:], pC[:, 0:DB * B].rearrange("p (e b) -> p e b", e=DB)).then_inc(states_ready, 1)
            dve.tensor_copy(sumw[:], pW[:, 8:9]).then_inc(states_ready, 1)
            dve.wait_ge(states_ready, 2)
            dve.wait_ge(projections_loaded, 16 * 4)
            dve.tensor_scalar(bw[:], bin_[:], sumw[:, 0:1], None, ALU.mult).then_inc(states_ready, 1)
            dve.wait_ge(states_psum, 1)
            dve.wait_ge(states_ready, 3)
            for e in range(DB):
                dve.tensor_scalar(states[:, e], pS[e][:, 0:B], bw[:, e:e + 1], None, ALU.add).then_inc(states_ready, 1)
            dve.wait_ge(summary_psum, 1)
            dve.tensor_copy(summ, pO[0][0:B, :]).then_inc(summary_ready, 1)

        @block.tensor
        def _(pe):
            pe.wait_ge(row_ready, 1)
            for t in range(ST):
                mm = pe.matmul(pW[:, t:t + 1], row[0:1, t * P:(t + 1) * P], ones[0:1, 0:1], start=True, stop=True)
            mm.then_inc(weights_psum, 1)
            pe.wait_ge(weights_ready, 1)
            for t in range(ST):
                pe.matmul(pW[:, 8:9], ones[:], wcol[:, t:t + 1], start=t == 0, stop=t == ST - 1)

            def scores(n, slot):
                h = slot % 2
                wait_slot(pe, c_loaded[h], n, slot, 2, dmas=2)
                for e in range(DB):
                    for t in range(ST):
                        pe.matmul(pC[:, e * B + n:e * B + n + 1] if isinstance(n, int) else pC[:, bass.ds(n + e * B, 1)],
                                  C[:, h, t, e * P:(e + 1) * P], wcol[:, t:t + 1], start=t == 0, stop=t == ST - 1)
                wait_item(pe, klo_ready, n)
                wait_item(pe, qlo_ready, n)
                for e in range(DB):
                    wait_item(pe, exps_ready, n, back=1, per=DB, of=e)
                    for t in range(ST):
                        mm = split_matmul(pe, pS[e][:], [k[:, h, t, e * P:(e + 1) * P] for k in Kp],
                                          [q[:, h, t] for q in Qp], t == 0, t == ST - 1)
                    mm.then_inc(scores_ready, 1)

            def out(n, slot):
                h = slot % 2
                wait_item(pe, v_ready, n)
                for t in range(ST):
                    wait_item(pe, out_added, n, back=1, per=ST, of=t)
                    for e in range(DB):
                        wait_item(pe, elo_ready, n, per=DB, of=e)
                        mm = split_matmul(pe, pO[t][:], [v[:, h, e, t * P:(t + 1) * P] for v in Vp],
                                          [x[:, h, e] for x in Ep], e == 0, e == DB - 1)
                    mm.then_inc(out_ready, 1)

            run_pipeline(pe.Fori, B, U, 2, [(1, scores), (2, out)])

            pe.nop().then_inc(cw_ready, 1)
            pe.wait_ge(projections_loaded, 16 * 4)
            pe.wait_ge(states_ready, 1)
            for e in range(DB):
                for h in range(DB):
                    mm = pe.matmul(pS[e][:, 0:B], WinT[:, h, e * P:(e + 1) * P], cw[:, h], start=h == 0, stop=h == DB - 1)
            mm.then_inc(states_psum, 1)
            pe.wait_ge(states_ready, 3 + DB)
            wait_item(pe, out_added, B - 1, per=ST)
            for e in range(DB):
                pe.matmul(pO[0][0:B, :], states[:, e], WoutT[:, e], start=e == 0, stop=False)
            pe.matmul(pO[0][0:B, :], ones[0:1, 0:B], bout[:], start=False, stop=True).then_inc(summary_psum, 1)


def mx_front(dve, order, first, src, V, M, scale, rinv, ready):
    blocks = src.rearrange("p (k i) -> p k i", i=BLOCK)
    Vb = V.rearrange("p (k i) -> p k i", i=BLOCK)
    dve.tensor_reduce(scale, blocks, AX.X, ALU.max, apply_absolute_value=True).then_inc(order, 1)
    dve.wait_ge(order, first + 1)
    dve.tensor_scalar(scale, scale, 1.0 / FP8_MAX, SCALE_MIN, ALU.mult, ALU.max).then_inc(order, 1)
    dve.wait_ge(order, first + 2)
    dve.reciprocal(rinv, scale).then_inc(order, 1)
    dve.wait_ge(order, first + 3)
    dve.tensor_tensor(Vb, blocks, rinv.unsqueeze(2).to_broadcast([P, 512 // BLOCK, BLOCK]), ALU.mult).then_inc(order, 1)
    dve.wait_ge(order, first + 4)
    dve.tensor_scalar(M.bitcast(I32), V.bitcast(I32), EXPONENT, HALF_BIT, ALU.bitwise_and,
                      ALU.bitwise_or).then_inc(order, 1)
    dve.wait_ge(order, first + 5)
    dve.tensor_scalar(M, M, 1.5 * 2.0 ** -6, 2.0 ** 20, ALU.max, ALU.mult).then_inc(order, 1)
    dve.wait_ge(order, first + 6)
    dve.tensor_tensor(V, V, M, ALU.add).then_inc(ready, 1)


MX_STEPS = 6


def mx_weights(nc, shared, passes):
    U, VS, KB, NS = 8, 4, 512 // P, 512 // BLOCK
    counts = [source.shape[1] for source, _, _ in passes]
    passes = [(sum(counts[:k]), counts[k], *each) for k, each in enumerate(passes)]
    with ExitStack() as ctx:
        m = Memory(nc, ctx)
        V = shared["w_work"]
        pT = [m.psum(f"pWT{i}") for i in range(U)]
        scaled = m.sems("w_scaled", VS)
        turned, hi_ready, lo_ready = m.sem("w_turned"), m.sem("w_hi"), m.sem("w_lo")
        block = ctx.enter_context(nc.Block())
        ON_VECTOR = VS - 1

        def scale_values(eng, first, source, scale_at, n, slot):
            wait_item(eng, turned, n + first, back=VS)
            values = source[:, n] if isinstance(n, int) else source[:, bass.ds(n, 1)].rearrange("p a d -> p (a d)")
            at = scale_at(n, slot)
            scales = shared["w_scales"][:, at:at + NS] if isinstance(n, int) else shared["w_scales"][:, bass.ds(at, NS)]
            eng.tensor_tensor(V[:, slot % VS].rearrange("p (k i) -> p k i", i=BLOCK), values.rearrange("p (k i) -> p k i", i=BLOCK),
                              scales.unsqueeze(2).to_broadcast([P, NS, BLOCK]), ALU.mult).then_inc(scaled[slot % VS], VS)

        @block.gpsimd
        def _(pool):
            for first, count, source, scale_at, _ in passes:
                def scale(n, slot):
                    if slot % VS != ON_VECTOR:
                        scale_values(pool, first, source, scale_at, n, slot)
                run_pipeline(pool.Fori, count, U, U, [(0, scale)])

        @block.vector
        def _(dve):
            for first, count, source, scale_at, place in passes:
                def scale(n, slot):
                    if slot % VS == ON_VECTOR:
                        scale_values(dve, first, source, scale_at, n, slot)

                def lo(n, slot):
                    wait_item(dve, hi_ready, n + first)
                    dve.tensor_tensor(place(1, n, slot), pT[slot][:].rearrange("p (k i) -> p k i", i=P),
                                      place(0, n, slot).bitcast(F32), ALU.subtract).then_inc(lo_ready, 1)
                run_pipeline(dve.Fori, count, U, U, [(0, scale), (3, lo)])

        @block.tensor
        def _(pe):
            for first, count, _, _, _ in passes:
                def turn(n, slot):
                    pe.wait_ge(scaled[slot % VS], n + first - slot % VS + VS)
                    wait_item(pe, lo_ready, n + first, back=U)
                    for k in range(KB):
                        mm = pe.transpose(pT[slot][:, k * P:(k + 1) * P], V[:, slot % VS, k * P:(k + 1) * P], shared["ident"][:])
                    mm.then_inc(turned, 1)
                run_pipeline(pe.Fori, count, U, U, [(0, turn)])

        @block.scalar
        def _(act):
            for first, count, _, _, place in passes:
                def hi(n, slot):
                    wait_item(act, turned, n + first)
                    act.activation(place(0, n, slot), pT[slot][:].rearrange("p (k i) -> p k i", i=P),
                                   ACT.Copy).then_inc(hi_ready, 1)
                run_pipeline(act.Fori, count, U, 0, [(0, hi)])


def mx_ffn(nc, io, shared, W):
    Gp, Dp = W
    F, D = io["down_w_shape"][1], io["down_w_shape"][0]
    T = shared["x1"].shape[0]
    NT, DB, NC, KB = T // P, D // P, F // 512, 512 // P
    U = 4
    with ExitStack() as ctx:
        m = Memory(nc, ctx)
        X = m.sbuf("x_tiles2", [P, U, D])
        XV = m.sbuf("x_quantised", [P, D])
        V = m.sbuf("h_quantised", [P, 2, 512])
        M = m.sbuf("rounders", [P, 512])
        XT = [m.sbuf(f"xT_{s}", [P, 2, DB, P], F32R) for s in ("hi", "lo")]
        HT = [m.sbuf(f"hT_{s}", [P, KB, P], F32R) for s in ("hi", "lo")]
        stats, mv = m.sbuf("ln_stats2", [P, 6]), m.sbuf("mean_var2", [P, 2])
        veps, rstd = m.sbuf("var_eps2", [P, 1]), m.sbuf("rstd2", [P, 1])
        hscale = m.sbuf("h_scales", [P, 2, 512 // BLOCK])
        xscale = m.sbuf("x_scales", [P, 512 // BLOCK])
        rinv = m.sbuf("scale_inverses", [P, 512 // BLOCK])
        pG = [m.psum(f"pGate{i}") for i in range(2)]
        pU = [m.psum(f"pUp{i}") for i in range(2)]
        pY = [m.psum(f"pY{i}") for i in range(2)]
        pH, pX = m.psum("pHT"), m.psum("pXT")

        x_loaded, x_stored = m.sems("x_loaded2", U), m.sems("x_stored2", U)
        stats_ready, mv_ready, veps_ready = m.sem("stats_ready2"), m.sem("mv_ready2"), m.sem("veps_ready2")
        rstd_ready, normed = m.sem("rstd_ready2"), m.sem("normed")
        x_order, x_front, x_sub, x_deq = m.sem("x_order"), m.sem("x_front"), m.sem("x_sub"), m.sem("x_deq")
        x_turned, x_hi, x_lo = m.sem("x_turned"), m.sem("x_hi"), m.sem("x_lo")
        gu_ready, silu_ready, h_ready = m.sem("gate_up_ready"), m.sem("silu_ready"), m.sem("h_ready")
        h_order, h_front, h_sub, h_deq = m.sem("h_order"), m.sem("h_front"), m.sem("h_sub"), m.sem("h_deq")
        h_turned, h_hi, h_lo = m.sem("h_turned"), m.sem("h_hi"), m.sem("h_lo")
        down_done, y_added = m.sem("down_done"), m.sem("y_added")
        block = ctx.enter_context(nc.Block())

        def per_chunk(lag, body, c):
            return lag, lambda n, slot: body(n, slot, c)

        @block.sync
        def _(sp):
            def load(n, slot):
                sp.dma_start(X[:, slot], shared["x1"][bass.ds(n * P, P), :]).then_inc(x_loaded[slot], 16)

            def store(n, slot):
                wait_item(sp, y_added, n)
                sp.dma_start(shared["x2"][bass.ds(n * P, P), :], X[:, slot]).then_inc(x_stored[slot], 16)

            for n in range(U):
                load(n, n)
            with sp.Fori(0, NT - 2 * U + 1, U) as base:
                for j in range(U):
                    store(base + j, j)
                    wait_slot(sp, x_stored[j], base + j, j, U)
                    load(base + (j + U), j)
            for j in range(U):
                store(NT - U + j, j)
            for j in range(U):
                wait_slot(sp, x_stored[j], NT - U + j, j, U)

        @block.tensor
        def _(pe):
            def turn_x(n, slot):
                wait_item(pe, x_deq, n)
                wait_item(pe, x_lo, n, back=1)
                for k in range(DB):
                    mm = pe.transpose(pX[:, k * P:(k + 1) * P], XV[:, k * P:(k + 1) * P], shared["ident"][:])
                mm.then_inc(x_turned, 1)

            def gate_up(n, slot, c):
                if c == 0:
                    wait_item(pe, x_hi, n)
                    wait_item(pe, x_lo, n)
                if c < 2:
                    wait_item(pe, h_ready, n, back=1, per=NC, of=c + 2)
                else:
                    wait_item(pe, h_ready, n, per=NC, of=c - 2)
                for out, first in ((pG[c % 2], 0), (pU[c % 2], F)):
                    for k in range(DB):
                        mm = split_matmul(pe, out[:], [x[:, slot % 2, k] for x in XT],
                                          [w[:, k, first + c * 512:first + (c + 1) * 512] for w in Gp],
                                          k == 0, k == DB - 1)
                mm.then_inc(gu_ready, 1)

            def turn_h(n, slot, c):
                wait_item(pe, h_deq, n, per=NC, of=c)
                if c:
                    wait_item(pe, h_lo, n, per=NC, of=c - 1)
                else:
                    wait_item(pe, h_lo, n, back=1, per=NC)
                for k in range(KB):
                    mm = pe.transpose(pH[:, k * P:(k + 1) * P], V[:, c % 2, k * P:(k + 1) * P], shared["ident"][:])
                mm.then_inc(h_turned, 1)

            def down(n, slot, c):
                wait_item(pe, h_hi, n, per=NC, of=c)
                wait_item(pe, h_lo, n, per=NC, of=c)
                if c == 0:
                    wait_item(pe, y_added, n, back=2)
                for k in range(KB):
                    mm = split_matmul(pe, pY[slot % 2][:], [h[:, k] for h in HT], [w[:, c * KB + k] for w in Dp],
                                      c == 0 and k == 0, c == NC - 1 and k == KB - 1)
                mm.then_inc(down_done, 1)

            stages = []
            for c in range(NC):
                stages.append(per_chunk(2, turn_h, c + 1) if c + 1 < NC else per_chunk(1, turn_h, 0))
                stages.append(per_chunk(2, down, c))
                if c == NC - 1:
                    stages.append((0, turn_x))
                stages.append(per_chunk(1, gate_up, c))
            run_pipeline(pe.Fori, NT, U, 2, stages)

        @block.scalar
        def _(act):
            def silu(n, slot, c):
                wait_item(act, gu_ready, n, per=NC, of=c)
                if c < 2:
                    wait_item(act, h_turned, n, back=1, per=NC, of=c + 2)
                else:
                    wait_item(act, h_turned, n, per=NC, of=c - 2)
                act.activation(V[:, c % 2], pG[c % 2][:], ACT.Silu).then_inc(silu_ready, 1)

            def h_part(n, slot, c):
                wait_item(act, h_turned, n, per=NC, of=c)
                if c:
                    wait_item(act, down_done, n, per=NC, of=c - 1)
                else:
                    wait_item(act, down_done, n, back=1, per=NC)
                act.activation(HT[0][:], pH[:].rearrange("p (k i) -> p k i", i=P), ACT.Copy).then_inc(h_hi, 1)

            def x_part(n, slot):
                wait_item(act, x_turned, n)
                wait_item(act, gu_ready, n, back=2, per=NC)
                act.activation(XT[0][:, slot % 2], pX[:].rearrange("p (k i) -> p k i", i=P), ACT.Copy).then_inc(x_hi, 1)

            stages = []
            for c in range(NC):
                stages.append(per_chunk(1, silu, c - 1) if c else per_chunk(2, silu, NC - 1))
                stages.append(per_chunk(2, h_part, c + 1) if c + 1 < NC else per_chunk(1, h_part, 0))
            stages.append((0, x_part))
            run_pipeline(act.Fori, NT, U, 2, stages)

        @block.vector
        def _(dve):
            def norm_stats(n, slot):
                wait_slot(dve, x_loaded[slot], n, slot, U)
                dve.bn_stats(stats[:], X[:, slot]).then_inc(stats_ready, 1)
                wait_item(dve, stats_ready, n)
                wait_item(dve, normed, n, back=1)
                own_wait(dve, shared["passed_dve"])
                dve.bn_aggr(mv[:], stats[:]).then_inc(mv_ready, 1)

            def norm_quantise(n, slot):
                wait_item(dve, rstd_ready, n)
                wait_item(dve, x_turned, n, back=1)
                dve.tensor_scalar(XV[:], X[:, slot], mv[:, 0:1], rstd[:, 0:1], ALU.subtract, ALU.mult).then_inc(normed, 1)
                wait_item(dve, normed, n)
                wait_item(dve, h_sub, n, back=1, per=NC, of=0)
                mx_front(dve, x_order, n * MX_STEPS, XV[:], XV[:], M[:], xscale[:], rinv[:], x_front)

            def hidden(n, slot, c):
                wait_item(dve, silu_ready, n, per=NC, of=c)
                V_ = V[:, c % 2]
                dve.tensor_tensor(V_, V_, pU[c % 2][:], ALU.mult).then_inc(h_ready, 1)
                wait_item(dve, h_ready, n, per=NC, of=c)
                if c:
                    wait_item(dve, h_sub, n, per=NC, of=c - 1)
                else:
                    wait_item(dve, h_sub, n, back=1, per=NC)
                if c == 1:
                    wait_item(dve, x_sub, n + 1 if not isinstance(n, int) else min(n + 1, NT - 1))
                mx_front(dve, h_order, (n * NC + c) * MX_STEPS, V_, V_, M[:], hscale[:, c % 2], rinv[:], h_front)

            def h_part(n, slot, c):
                wait_item(dve, h_hi, n, per=NC, of=c)
                dve.tensor_tensor(HT[1][:], pH[:].rearrange("p (k i) -> p k i", i=P), HT[0][:].bitcast(F32),
                                  ALU.subtract).then_inc(h_lo, 1)

            def x_part(n, slot):
                wait_item(dve, x_hi, n)
                dve.tensor_tensor(XT[1][:, slot % 2], pX[:].rearrange("p (k i) -> p k i", i=P),
                                  XT[0][:, slot % 2].bitcast(F32), ALU.subtract).then_inc(x_lo, 1)

            def add_y(n, slot):
                wait_item(dve, down_done, n, per=NC)
                dve.scalar_tensor_tensor(out=X[:, slot], in0=pY[slot % 2][:], scalar=shared["gates"][:, 2:3],
                                         in1=X[:, slot], op0=ALU.mult, op1=ALU.add).then_inc(y_added, 1)

            stages = []
            for c in range(NC):
                stages.append(per_chunk(1, hidden, c - 1) if c else per_chunk(2, hidden, NC - 1))
                stages.append(per_chunk(2, h_part, c + 1) if c + 1 < NC else per_chunk(1, h_part, 0))
                if c == 0:
                    stages.append((0, norm_stats))
                if c == 1:
                    stages.append((0, norm_quantise))
            stages.append((2, add_y))
            stages.append((0, x_part))
            run_pipeline(dve.Fori, NT, U, 2, stages)

        @block.gpsimd
        def _(pool):
            def rstd_of(n, slot):
                wait_item(pool, mv_ready, n)
                own_wait(pool, shared["passed_pool"])
                pool.tensor_scalar(veps[:], mv[:, 1:2], LN_EPS, None, ALU.add).then_inc(veps_ready, 1)
                wait_item(pool, veps_ready, n)
                pool.tensor_tensor(rstd[:], veps[:], shared["minus_half"][:, 0:1], ALU.pow).then_inc(rstd_ready, 1)

            def back(front, sub, deq, i, V_, scale):
                Vb = V_.rearrange("p (k i) -> p k i", i=BLOCK)
                pool.wait_ge(front, i + 1)
                pool.tensor_tensor(V_, V_, M[:], ALU.subtract).then_inc(sub, 1)
                pool.wait_ge(sub, i + 1)
                pool.tensor_tensor(Vb, Vb, scale.unsqueeze(2).to_broadcast([P, 512 // BLOCK, BLOCK]),
                                   ALU.mult).then_inc(deq, 1)

            def x_back(n, slot):
                back(x_front, x_sub, x_deq, n, XV[:], xscale[:])

            def h_back(n, slot, c):
                back(h_front, h_sub, h_deq, n * NC + c, V[:, c % 2], hscale[:, c % 2])

            stages = []
            for c in range(NC):
                stages.append(per_chunk(1, h_back, c - 1) if c else per_chunk(2, h_back, NC - 1))
                if c == 0:
                    stages.append((0, rstd_of))
                if c == 1:
                    stages.append((0, x_back))
            run_pipeline(pool.Fori, NT, U, 2, stages)


def first_parts(nc, io, shared):
    F, D = io["down_w_shape"][1], io["down_w_shape"][0]
    B = io["x"].shape[0]
    GU_TILES, D_TILES = 2 * F * D // (P * 512), F * D // (P * 512)
    NS, PER_BATCH = 512 // BLOCK, (GU_TILES + D_TILES) // B
    GUT, KB, FC = GU_TILES // B, 512 // P, F // 512
    with ExitStack() as weights, ExitStack() as down_values:
        far, near = Memory(nc, down_values), Memory(nc, weights)
        shared["w_scales"] = far.sbuf("w_scales", [P, B * PER_BATCH * NS], side="right")
        shared["down_q"] = far.sbuf("down_e4m3", [P, D_TILES, 512], F16, side="right")
        shared["w_work"] = far.sbuf("w_work", [P, 4, 512], side="right")
        with ExitStack() as gate_up_values:
            shared["gate_up_q"] = Memory(nc, gate_up_values).sbuf("gate_up_e4m3", [P, GU_TILES, 512], F16, side="right")
            attend(nc, io, shared)
            Gp = [near.sbuf(f"gate_upT_{s}", [P, D // P, 2 * F], F32R) for s in ("hi", "lo")]
        Dp = [near.sbuf(f"downT_{s}", [P, F // P, D], F32R) for s in ("hi", "lo")]
        mx_weights(nc, shared, [
            (shared["gate_up_q"], lambda n, slot: (n - slot % GUT) * (PER_BATCH * NS // GUT) + slot % GUT * NS,
             lambda part, n, slot: Gp[part][:, :, bass.ds(n * P, P)]),
            (shared["down_q"], lambda n, slot: n * (PER_BATCH * NS) + GUT * NS,
             lambda part, n, slot: Dp[part][:, slot % FC * KB:(slot % FC + 1) * KB,
                                            bass.ds((n - slot % FC) * (P // FC), P)])])
        down_values.close()
        mx_ffn(nc, io, shared, (Gp, Dp))


def fp4_ffn(nc, io, shared, Wp, out):
    B = shared["summary"].shape[0]
    T, D = shared["x2"].shape
    F = io["fp4_inner"]
    DB, FB = D // P, F // P
    GT = 512 // P
    NG = T // (GT * P)
    GB = B // NG
    U = 2
    USES = FB + 2
    BLOCK_COLS = 2 * DB * P + D
    CH = 512
    BCH = BLOCK_COLS // CH
    AHEAD = 3
    LATER = range(4, AHEAD * BCH)
    EXP5_UP = 2.0 ** 14
    with ExitStack() as ctx:
        m = Memory(nc, ctx)
        words = m.sbuf("fp4_bytes", [P, 2, BLOCK_COLS // 4], I32)
        mid = m.sbuf("fp4_magnitudes", [P, BLOCK_COLS // 4], I32)
        scales = m.sbuf("fp4_scales_bc", [P, 2, CH], F16)
        value = m.sbuf("fp4_values", [P, 2, CH])
        shift = m.sbuf("nibble_shifts_sb", [P, 1], I32)
        X = m.sbuf("x_groups", [P, U, GT, D])
        Z = m.sbuf("z_group", [P, GT, D])
        summ = m.sbuf("summary_bc", [P, GB, D])
        gamma, beta = m.sbuf("gamma_bc", [P, D]), m.sbuf("beta_bc", [P, D])
        XT = [m.sbuf(f"x3T_{s}", [P, U, DB, GT * P], F32R) for s in ("hi", "lo")]
        H = m.sbuf("h3", [P, 2, GT * P])
        HT = [m.sbuf(f"h3_{s}", [P, 2, GT * P], F32R) for s in ("hi", "lo")]
        stats, mv = m.sbuf("ln_stats3", [P, GT, 6]), m.sbuf("mean_var3", [P, GT, 2])
        veps, rstd = m.sbuf("var_eps3", [P, GT]), m.sbuf("rstd3", [P, GT])
        sums = m.sbuf("y_square_sums", [P, GT])
        meps, rrms, grms = m.sbuf("mean_square_eps", [P, GT]), m.sbuf("rms_inverse", [P, GT]), m.sbuf("gated_rms", [P, GT])
        pG = [m.psum(f"p3G{i}") for i in range(2)]
        pU = [m.psum(f"p3U{i}") for i in range(2)]
        pY = [m.psum(f"p3Y{i}") for i in range(GT)]

        shift_loaded = m.sem("shift_loaded")
        words_loaded, scales_loaded = m.sems("words_loaded", 2), m.sems("scales_loaded", 2)
        nibble_ready, mid_ready, e5_ready, value_ready = (m.sem(n) for n in ("nibble_ready", "mid_ready", "e5_ready", "value_ready"))
        whi_ready, wlo_ready = m.sem("w3_hi_ready"), m.sem("w3_lo_ready")
        consts_loaded = m.sem("consts3_loaded")
        x_loaded, stored = m.sems("x3_loaded", U), m.sems("x3_stored", U)
        s_loaded = m.sem("s_loaded")
        affine_ready = m.sem("affine_ready")
        stats_ready, mv_ready, veps_ready, rstd_ready = (m.sem(n + "3") for n in ("stats_r", "mv_r", "veps_r", "rstd_r"))
        normed, summed, scaled, shifted, mixed = (m.sem(n + "3") for n in ("normed", "summed", "scaled", "shifted", "mixed"))
        x_turned, x_hi, x_lo = m.sem("x3_turned"), m.sem("x3_hi"), m.sem("x3_lo")
        gu_ready, silu_ready, h_ready = m.sem("gu3_ready"), m.sem("silu3_ready"), m.sem("h3_ready")
        h_hi, h_lo, down_done = m.sem("h3_hi"), m.sem("h3_lo"), m.sem("down3_done")
        squared, meps_ready, rrms_ready, grms_ready = (m.sem(n) for n in ("squared", "meps_r", "rrms_r", "grms_r"))
        y_added = m.sem("y3_added")
        block = ctx.enter_context(nc.Block())
        gates, minus_half = shared["gates"], shared["minus_half"]

        x_in = shared["x2"].rearrange("(g t p) d -> g p t d", p=P, t=GT)
        x_out = out.rearrange("b (t p) d -> (b t) p d", p=P).rearrange("(g t) p d -> g p t d", t=GT)

        def gate_w(part, g, b, up):
            at = b * BLOCK_COLS + (up * DB + g) * P
            return Wp[part][:, at:at + P]

        def down_w(part, b):
            return Wp[part][:, (b + 1) * BLOCK_COLS - D:(b + 1) * BLOCK_COLS]

        def first_chunks(body, chunks):
            def stage(n, slot):
                if isinstance(n, int) and n == 0:
                    for i in chunks:
                        body(i)
            return stage

        def first_group(body, b):
            return first_chunks(body, range(b * BCH, (b + 1) * BCH) if b < FB else ())

        @block.sync
        def _(sp):
            def load(n, slot):
                sp.dma_start(X[:, slot], x_in[n]).then_inc(x_loaded[slot], 16)

            def load_summary(n):
                wait_item(sp, summed, n, back=1)
                for b in range(GB):
                    sp.dma_start(summ[:, b], shared["summary"][bass.ds(n * GB + b, 1), :].to_broadcast([P, D]))\
                        .then_inc(s_loaded, 16)

            def load_words(b):
                if b >= 2:
                    wait_item(sp, value_ready, b - 2, per=BCH)
                sp.dma_start(words[:, b % 2], io["fp4_packed"][:, b * (BLOCK_COLS // 4):(b + 1) * (BLOCK_COLS // 4)])\
                    .then_inc(words_loaded[b % 2], 16)

            def load_scales(i):
                if i >= 2:
                    wait_item(sp, value_ready, i - 2)
                sp.dma_start(scales[:, i % 2], io["fp4_scales"][0:1, i * CH:(i + 1) * CH].to_broadcast([P, CH]))\
                    .then_inc(scales_loaded[i % 2], 16)

            def store(n, slot):
                wait_item(sp, y_added, n, per=GT)
                sp.dma_start(x_out[n], X[:, slot]).then_inc(stored[slot], 16)

            load(0, 0)
            load_words(0)
            sp.dma_start(gamma[:], io["gamma"].rearrange("(a n) -> a n", a=1).to_broadcast([P, D])).then_inc(consts_loaded, 16)
            sp.dma_start(beta[:], io["beta"].rearrange("(a n) -> a n", a=1).to_broadcast([P, D])).then_inc(consts_loaded, 16)
            sp.dma_start(shift[:], io["nibble_shift"]).then_inc(shift_loaded, 16)
            load_summary(0)
            for b in range(FB):
                for i in range(b * BCH, (b + 1) * BCH):
                    load_scales(i)
                    if i == b * BCH and b + 1 < FB:
                        load_words(b + 1)
                if b == AHEAD:
                    load(1, 1)
                    load_summary(1)
            with sp.Fori(0, NG - 2 * U + 1, U) as base:
                for j in range(U):
                    load_summary(base + (j + 2))
                    store(base + j, j)
                    wait_slot(sp, stored[j], base + j, j, U)
                    load(base + (j + U), j)
            for j in range(U):
                store(NG - U + j, j)
            for j in range(U):
                wait_slot(sp, stored[j], NG - U + j, j, U)

        @block.vector
        def _(dve):
            def codes(b):
                w = words[:, b % 2]
                if b == 0:
                    dve.wait_ge(shift_loaded, 16)
                wait_slot(dve, words_loaded[b % 2], b, b, 2)
                dve.tensor_scalar(w, w, shift[:, 0:1], signed(0xF0F0F0F0), ALU.logical_shift_left,
                                  ALU.bitwise_and).then_inc(nibble_ready, 1)
                wait_item(dve, nibble_ready, b)
                wait_item(dve, e5_ready, b, back=1)
                dve.tensor_scalar(mid[:], w, 3, 0x0E0E0E0E, ALU.logical_shift_right,
                                  ALU.bitwise_and).then_inc(mid_ready, 1)
                wait_item(dve, mid_ready, b)
                dve.scalar_tensor_tensor(out=w, in0=w, scalar=signed(0x80808080), in1=mid[:],
                                         op0=ALU.bitwise_and, op1=ALU.bitwise_or).then_inc(e5_ready, 1)

            def weights(i):
                b, c = i // BCH, i % BCH
                if c == 0:
                    codes(b)
                wait_slot(dve, scales_loaded[i % 2], i, i, 2)
                wait_item(dve, wlo_ready, i, back=2)
                wait_item(dve, e5_ready, b)
                dve.scalar_tensor_tensor(out=value[:, i % 2], in0=words[:, b % 2].bitcast(F8E5)[:, c * CH:(c + 1) * CH],
                                         scalar=EXP5_UP, in1=scales[:, i % 2], op0=ALU.mult,
                                         op1=ALU.mult).then_inc(value_ready, 1)

            def statistics(src, n, k):
                wait_item(dve, normed, n, per=3, of=k - 1) if k else wait_item(dve, normed, n, back=1, per=3)
                for t in range(GT):
                    ins = dve.bn_stats(stats[:, t], src[:, t])
                ins.then_inc(stats_ready, 1)
                wait_item(dve, stats_ready, n, per=3, of=k)
                own_wait(dve, shared["passed_dve"])
                for t in range(GT):
                    ins = dve.bn_aggr(mv[:, t], stats[:, t])
                ins.then_inc(mv_ready, 1)

            def normalise(dst, src, n, k):
                wait_item(dve, rstd_ready, n, per=3, of=k)
                for t in range(GT):
                    ins = dve.tensor_scalar(dst[:, t], src[:, t], mv[:, t, 0:1], rstd[:, t:t + 1], ALU.subtract, ALU.mult)
                ins.then_inc(normed, 1)

            def x_stats(n, slot):
                wait_slot(dve, x_loaded[slot], n, slot, U)
                statistics(X[:, slot], n, 0)

            def x_norm(n, slot):
                wait_item(dve, x_turned, n, back=1, per=GT)
                normalise(Z, X[:, slot], n, 0)

            def add_summary(n, slot):
                wait_item(dve, normed, n, per=3, of=0)
                dve.wait_ge(s_loaded, n * (16 * GB) + 16 * GB)
                Zb = Z[:].rearrange("p (b t) d -> p b t d", b=GB)
                for b in range(GB):
                    ins = dve.tensor_tensor(Zb[:, b], Zb[:, b],
                                            summ[:, b].unsqueeze(1).to_broadcast([P, GT // GB, D]), ALU.add)
                ins.then_inc(summed, 1)
                if isinstance(n, int) and n == 0:
                    dve.wait_ge(consts_loaded, 32)
                    dve.tensor_scalar(gamma[:], gamma[:], gates[:, 1:2], None, ALU.mult).then_inc(affine_ready, 1)
                    dve.tensor_scalar(beta[:], beta[:], gates[:, 1:2], None, ALU.mult).then_inc(affine_ready, 1)
                    dve.wait_ge(affine_ready, 2)

            def z_stats(n, slot):
                wait_item(dve, summed, n)
                statistics(Z, n, 1)

            def add_beta(n, slot):
                dve.tensor_tensor(X[:, slot], X[:, slot], beta[:].unsqueeze(1).to_broadcast([P, GT, D]), ALU.add)\
                    .then_inc(shifted, 1)

            def centre_z(n, slot):
                wait_item(dve, mv_ready, n, per=3, of=1)
                for t in range(GT):
                    ins = dve.scalar_tensor_tensor(out=Z[:, t], in0=Z[:, t], scalar=mv[:, t, 0:1], in1=gamma[:],
                                                   op0=ALU.subtract, op1=ALU.mult)
                ins.then_inc(scaled, 1)

            def add_z(n, slot):
                wait_item(dve, scaled, n)
                wait_item(dve, shifted, n)
                wait_item(dve, rstd_ready, n, per=3, of=1)
                for t in range(GT):
                    ins = dve.scalar_tensor_tensor(out=X[:, slot, t], in0=Z[:, t], scalar=rstd[:, t:t + 1],
                                                   in1=X[:, slot, t], op0=ALU.mult, op1=ALU.add)
                ins.then_inc(normed, 1)

            def mixed_stats(n, slot):
                wait_item(dve, normed, n, per=3, of=1)
                statistics(X[:, slot], n, 2)

            def mixed_norm(n, slot):
                normalise(Z, X[:, slot], n, 2)

            def x_part(n, slot):
                for t in range(GT):
                    wait_item(dve, x_hi, n, per=GT, of=t)
                    use = (slot - 1) % U * USES + FB + t // 2
                    bank = (pG, pU)[t % 2][use % 2]
                    dve.tensor_tensor(XT[1][:, slot, :, t * P:(t + 1) * P], bank[:].rearrange("p (k i) -> p k i", i=P),
                                      XT[0][:, slot, :, t * P:(t + 1) * P].bitcast(F32), ALU.subtract).then_inc(x_lo, 1)

            def hidden(n, slot, b):
                use = slot * USES + b
                h = b % 2
                wait_item(dve, silu_ready, n, per=FB, of=b)
                dve.tensor_tensor(H[:, h], H[:, h], pU[use % 2][:], ALU.mult).then_inc(h_ready, 1)
                wait_item(dve, h_hi, n, per=FB, of=b)
                dve.tensor_tensor(HT[1][:, h], H[:, h], HT[0][:, h].bitcast(F32), ALU.subtract).then_inc(h_lo, 1)

            def add_y(n, slot):
                wait_item(dve, rrms_ready, n)
                dve.tensor_scalar(grms[:], rrms[:], gates[:, 3:4], None, ALU.mult).then_inc(grms_ready, 1)
                wait_item(dve, grms_ready, n)
                for t in range(GT):
                    dve.scalar_tensor_tensor(out=X[:, slot, t], in0=pY[t][:], scalar=grms[:, t:t + 1], in1=X[:, slot, t],
                                             op0=ALU.mult, op1=ALU.add).then_inc(y_added, 1)

            between = {1: x_stats, 2: x_norm, 3: add_summary, 4: z_stats, 5: add_beta, 6: centre_z, 7: add_z,
                       8: mixed_stats, 9: mixed_norm}
            early = {1: range(0, 2), 4: range(2, 3), 8: range(3, 4)}
            stages = []
            for b in range(FB):
                stages.append((1, lambda n, slot, b=b: hidden(n, slot, b)))
                stages.append((1, first_group(weights, b + AHEAD)))
                if b in between:
                    stages.append((0, between[b]))
                if b in early:
                    stages.append((0, first_chunks(weights, early[b])))
            run_pipeline(dve.Fori, NG, U, 2, stages + [(0, x_part), (1, add_y), (0, first_chunks(weights, LATER))])

        @block.gpsimd
        def _(pool):
            def rstd_of(n, slot, k):
                wait_item(pool, mv_ready, n, per=3, of=k)
                own_wait(pool, shared["passed_pool"])
                pool.tensor_scalar(veps[:], mv[:, :, 1], LN_EPS, None, ALU.add).then_inc(veps_ready, 1)
                wait_item(pool, veps_ready, n, per=3, of=k)
                pool.tensor_tensor(rstd[:], veps[:], minus_half[:], ALU.pow).then_inc(rstd_ready, 1)

            def rstd_1(n, slot):
                rstd_of(n, slot, 0)

            def rstd_2(n, slot):
                rstd_of(n, slot, 1)

            def rstd_3(n, slot):
                rstd_of(n, slot, 2)

            def rms(n, slot):
                wait_item(pool, squared, n, per=GT)
                own_wait(pool, shared["passed_pool"])
                pool.tensor_scalar(meps[:], sums[:], 1.0 / D, RMS_EPS, ALU.mult, ALU.add).then_inc(meps_ready, 1)
                wait_item(pool, meps_ready, n)
                pool.tensor_tensor(rrms[:], meps[:], minus_half[:], ALU.pow).then_inc(rrms_ready, 1)

            def w_lo(i):
                wait_item(pool, whi_ready, i)
                pool.tensor_tensor(Wp[1][:, i * CH:(i + 1) * CH], value[:, i % 2], Wp[0][:, i * CH:(i + 1) * CH].bitcast(F32),
                                   ALU.subtract).then_inc(wlo_ready, 1)

            between = {1: rstd_1, 4: rstd_2, 8: rstd_3}
            early = {1: range(0, 2), 4: range(2, 3), 8: range(3, 4)}
            stages = []
            for b in range(FB):
                stages.append((1, first_group(w_lo, b + AHEAD)))
                if b in between:
                    stages.append((0, between[b]))
                if b in early:
                    stages.append((0, first_chunks(w_lo, early[b])))
            run_pipeline(pool.Fori, NG, U, 2, stages + [(1, rms), (0, first_chunks(w_lo, LATER))])

        @block.scalar
        def _(act):
            def silu(n, slot, b):
                use = slot * USES + b
                h = b % 2
                wait_item(act, gu_ready, n, per=FB, of=b)
                if b >= 2:
                    wait_item(act, h_lo, n, per=FB, of=b - 2)
                else:
                    wait_item(act, h_lo, n, back=1, per=FB)
                    wait_item(act, squared, n, back=1, per=GT)
                act.activation(H[:, h], pG[use % 2][:], ACT.Silu).then_inc(silu_ready, 1)
                wait_item(act, h_ready, n, per=FB, of=b)
                if b >= 2:
                    wait_item(act, down_done, n, per=FB, of=b - 2)
                else:
                    wait_item(act, down_done, n, back=1, per=FB)
                act.activation(HT[0][:, h], H[:, h], ACT.Copy).then_inc(h_hi, 1)

            def x_part(n, slot):
                for t in range(GT):
                    use = (slot - 1) % U * USES + FB + t // 2
                    bank = (pG, pU)[t % 2][use % 2]
                    wait_item(act, x_turned, n, per=GT, of=t)
                    act.activation(XT[0][:, slot, :, t * P:(t + 1) * P], bank[:].rearrange("p (k i) -> p k i", i=P),
                                   ACT.Copy).then_inc(x_hi, 1)

            def squares_of(n, slot):
                wait_item(act, down_done, n, per=FB)
                wait_item(act, meps_ready, n, back=1)
                for t in range(GT):
                    if t >= 2:
                        wait_item(act, squared, n, per=GT, of=t - 2)
                    act.activation(H[:, t % 2], pY[t][:], ACT.Square, accum_out=sums[:, t:t + 1]).then_inc(squared, 1)

            def w_hi(i):
                wait_item(act, value_ready, i)
                act.activation(Wp[0][:, i * CH:(i + 1) * CH], value[:, i % 2], ACT.Copy).then_inc(whi_ready, 1)

            stages = [(0, first_chunks(w_hi, range(LATER[0])))]
            for b in range(FB):
                stages.append((1, lambda n, slot, b=b: silu(n, slot, b)))
                stages.append((1, first_group(w_hi, b + AHEAD)))
            run_pipeline(act.Fori, NG, U, 2, stages + [(0, x_part), (1, squares_of), (0, first_chunks(w_hi, LATER))])

        @block.tensor
        def _(pe):
            def gate_up(n, slot, b):
                use = slot * USES + b
                if b == 0:
                    wait_item(pe, x_hi, n, per=GT)
                    wait_item(pe, x_lo, n, per=GT)
                if isinstance(n, int) and n == 0:
                    wait_item(pe, whi_ready, b, per=BCH)
                    wait_item(pe, wlo_ready, b, per=BCH)
                if b >= 2:
                    wait_item(pe, h_ready, n, per=FB, of=b - 2)
                for bank, up in ((pG[use % 2], 0), (pU[use % 2], 1)):
                    for g in range(DB):
                        mm = split_matmul(pe, bank[:], [gate_w(s, g, b, up) for s in (0, 1)],
                                          [x[:, slot, g] for x in XT], g == 0, g == DB - 1)
                mm.then_inc(gu_ready, 1)

            def down(n, slot, b):
                wait_item(pe, h_hi, n, per=FB, of=b)
                wait_item(pe, h_lo, n, per=FB, of=b)
                for t in range(GT):
                    if b == 0:
                        wait_item(pe, y_added, n, back=1, per=GT, of=t)
                    mm = split_matmul(pe, pY[t][:], [h[:, b % 2, t * P:(t + 1) * P] for h in HT],
                                      [down_w(s, b) for s in (0, 1)], b == 0, b == FB - 1)
                mm.then_inc(down_done, 1)

            def turn(n, slot):
                wait_item(pe, normed, n, per=3)
                for t in range(GT):
                    use = (slot - 1) % U * USES + FB + t // 2
                    bank = (pG, pU)[t % 2][use % 2]
                    if t % 2 == 0:
                        wait_item(pe, h_ready, n, back=1, per=FB, of=FB - 2 + t // 2)
                    for g in range(DB):
                        mm = pe.transpose(bank[:, g * P:(g + 1) * P], Z[:, t, g * P:(g + 1) * P], shared["ident"][:])
                    mm.then_inc(x_turned, 1)

            stages = []
            for b in range(FB):
                stages.append((1, lambda n, slot, b=b: gate_up(n, slot, b)))
                if b:
                    stages.append((1, lambda n, slot, b=b: down(n, slot, b - 1)))
            stages.append((0, turn))
            stages.append((1, lambda n, slot: down(n, slot, FB - 1)))
            run_pipeline(pe.Fori, NG, U, 2, stages)


def fp4_layer(nc, io, shared, out):
    D, F = shared["x2"].shape[1], io["fp4_inner"]
    with ExitStack() as ctx:
        m = Memory(nc, ctx)
        Wp = [m.sbuf(f"fp4_w_{s}", [P, (D // P) * 2 * F + (F // P) * D], F32R) for s in ("hi", "lo")]
        fp4_ffn(nc, io, shared, Wp, out)


def build(nc, io, out):
    B, S, D = io["x"].shape
    T = B * S
    with ExitStack() as ctx:
        m = Memory(nc, ctx)
        shared = {
            "gates": m.sbuf("tanh_gates", [P, 4]), "ident": m.sbuf("identity", [P, P]),
            "minus_half": m.sbuf("minus_half", [P, 4]),
            **{f"passed_{e}": m.sem(f"passed_{e}") for e in ("sp", "dve", "pool")},
            "x1": nc.dram_tensor("x_after_attention", [T, D], F32, kind="Internal").ap(),
            "x2": nc.dram_tensor("x_after_mx_ffn", [T, D], F32, kind="Internal").ap(),
            "summary": nc.dram_tensor("summary", [B, D], F32, kind="Internal").ap(),
        }
        first_parts(nc, io, shared)
        fp4_layer(nc, io, shared, out)


def kernel(**inputs):
    import concourse.bacc as bacc
    import numpy as np
    from concourse.bass_utils import run_bass_kernel_spmd

    a = {name: np.asarray(value) for name, value in inputs.items()}
    D = a["x"].shape[-1]
    F4 = a["L1_ffn_down_packed"].shape[1] * 8
    def by_feature(packed):
        return np.repeat(np.ascontiguousarray(packed).view(np.uint8).T, 2, axis=0)

    gate_up = by_feature(a["L1_ffn_gate_up_packed"]).reshape(D // P, P, 2, F4 // P, P).transpose(1, 3, 2, 0, 4)
    down = by_feature(a["L1_ffn_down_packed"]).reshape(F4 // P, P, D).transpose(1, 0, 2)
    nibbles = np.concatenate([gate_up.reshape(P, F4 // P, -1), down], axis=2).reshape(P, -1)
    gate_up_scales = a["L1_ffn_gate_up_scales"].reshape(D // P, 2, F4 // P, P).transpose(2, 1, 0, 3)
    scales = np.concatenate([gate_up_scales.reshape(F4 // P, -1), a["L1_ffn_down_scales"]], axis=1).reshape(1, -1)
    arrays = {
        "x": a["x"], "ctx": a["ctx_2048"], "ctxT": a["ctx_2048"].transpose(0, 2, 1),
        "g_xattn": a["g_xattn"], "g_ffn": a["g_ffn"],
        "gate_up_w": np.concatenate([a["L0_ffn_gate_w"], a["L0_ffn_up_w"]]), 
        "down_tiles": a["L0_ffn_down_w"].reshape(D // P, P, -1, 512).transpose(0, 2, 1, 3).reshape(-1, 512),
        "decay": a["L1_xattn_decay"].reshape(1, 1), "W_inT": a["L1_xattn_W_in"].T, "W_outT": a["L1_xattn_W_out"].T,
        "b_in": a["L1_xattn_b_in"].reshape(D // P, P).T, "b_out": a["L1_xattn_b_out"],
        "gamma": a["L1_xattn_gamma"], "beta": a["L1_xattn_beta"],
        "fp4_packed": np.ascontiguousarray(nibbles).view(np.int32), "fp4_scales": scales,
        "nibble_shift": (4 - 4 * (np.arange(P, dtype=np.int32) % 2)).reshape(P, 1),
    }
    arrays = {f"in_{name}": np.ascontiguousarray(value) for name, value in arrays.items()}
    nc = bacc.Bacc("TRN2", target_bir_lowering=False, num_devices=1, dynamic_dma_scratch_size=1024)
    io = {name[3:]: nc.dram_tensor(name, value.shape, mybir.dt.from_np(value.dtype), kind="ExternalInput").ap()
          for name, value in arrays.items()}
    io["fp4_inner"] = F4
    io["down_w_shape"] = a["L0_ffn_down_w"].shape
    out = nc.dram_tensor("out", a["x"].shape, F32, kind="ExternalOutput").ap()
    build(nc, io, out)
    return run_bass_kernel_spmd(nc, [arrays], core_ids=[0]).results[0]["out"]
```
